# Optimizing a Trainium2 kernel written in Bass

```python
import numpy as np
import jax
import jax.numpy as jnp

def _softmax(x, axis=-1):
    return jax.nn.softmax(x, axis=axis)

def _gelu(x):
    return jax.nn.gelu(x, approximate=True)

def _silu(x):
    return jax.nn.silu(x)

def _sigmoid(x):
    return jax.nn.sigmoid(x)

def _layernorm(x, axis=-1, eps=1e-05):
    m = jnp.mean(x, axis=axis, keepdims=True)
    v = jnp.var(x, axis=axis, keepdims=True)
    return (x - m) / jnp.sqrt(v + eps)

def _scatter_add(tgt, idx, src, axis=0):
    return tgt.at[idx].add(src)

def _segment_sum(src, seg, n):
    return jax.ops.segment_sum(src, seg, n)
kernel_name = 'mk_prb_d1_jaxref_r8_a4854f'

def setup_inputs(seed: int=0):
    np.random.seed(seed)
    _w = jnp.asarray

    def _L0_attn_setup():
        import math
        import jax, jax.numpy as jnp
        import numpy as np
        D_MODEL = 128
        N_HEADS = 16
        D_HEAD = D_MODEL // N_HEADS
        BLOCK = 256
        BATCH = 2
        SEQ = 256

        def _rotate(t, cos, sin):
            t1 = t[..., 0::2]
            t2 = t[..., 1::2]
            r1 = t1 * cos - t2 * sin
            r2 = t1 * sin + t2 * cos
            return jnp.stack([r1, r2], axis=-1).reshape(t.shape)
        key = jax.random.key(seed)
        k1, k2, k3 = jax.random.split(key, 3)
        x = jax.random.normal(k1, (BATCH, SEQ, D_MODEL), dtype=jnp.float32)
        Wqkv = jax.random.normal(k2, (3 * D_MODEL, D_MODEL), dtype=jnp.float32) * 0.02
        Wo = jax.random.normal(k3, (D_MODEL, D_MODEL), dtype=jnp.float32) * 0.02
        log_xi = jnp.full((N_HEADS,), math.log(BLOCK / 2.0), dtype=jnp.float32)
        pi_gate_logit = jnp.full((N_HEADS,), 2.0, dtype=jnp.float32)
        e_gate_logit = jnp.full((N_HEADS,), 2.0, dtype=jnp.float32)
        return {'x': x, 'Wqkv': Wqkv, 'Wo': Wo, 'log_xi': log_xi, 'pi_gate_logit': pi_gate_logit, 'e_gate_logit': e_gate_logit}
    _L0_attn_in = _L0_attn_setup()

    def _L0_ffn_setup():
        import jax, jax.numpy as jnp
        import numpy as np
        B, T, C = (4, 256, 128)
        H = 128
        E_ATT = 8
        E_MOE = 8
        I = 128
        MIN_ATT = 2
        MIN_MOE = 2
        EPS_LN = 1e-05

        def _normalize(x, axis):
            n = jnp.linalg.norm(x, axis=axis, keepdims=True)
            return x / jnp.maximum(n, 1e-12)

        def _layernorm(x, w, b):
            m = jnp.mean(x, axis=-1, keepdims=True)
            v = jnp.mean(jnp.square(x - m), axis=-1, keepdims=True)
            return (x - m) / jnp.sqrt(v + EPS_LN) * w + b

        def _gating(flat_hs, sim, gates, min_experts):
            logits = _normalize(flat_hs, -1) @ _normalize(sim, 0) - jax.nn.sigmoid(gates)
            gated = jax.nn.relu(logits)
            mask = (gated > 0).astype(gated.dtype)
            inactive = jnp.sum(mask, axis=1) == 0
            _, idx = jax.lax.top_k(logits, min_experts)
            onehot = jnp.sum(jax.nn.one_hot(idx, logits.shape[-1], dtype=gated.dtype), axis=1)
            put = inactive[:, None] & (onehot > 0)
            mask = jnp.where(put, 1.0, mask)
            masked = jnp.where(mask > 0, gated, -jnp.inf)
            return jax.nn.softmax(masked, axis=-1)
        key = jax.random.key(seed)
        ks = jax.random.split(key, 12)
        d = {}
        d['x'] = jax.random.normal(ks[0], (B, T, C), dtype=jnp.float32)
        d['ln1_w'] = jnp.ones((C,), jnp.float32)
        d['ln1_b'] = jnp.zeros((C,), jnp.float32)
        d['ln2_w'] = jnp.ones((C,), jnp.float32)
        d['ln2_b'] = jnp.zeros((C,), jnp.float32)
        d['smha_sim'] = jax.random.normal(ks[1], (C, E_ATT), dtype=jnp.float32)
        d['smha_gates'] = jnp.zeros((E_ATT,), jnp.float32)
        sq = 1.0 / np.sqrt(C + H)
        d['q_proj'] = jax.random.normal(ks[2], (E_ATT, C, H), dtype=jnp.float32) * sq
        d['k_proj'] = jax.random.normal(ks[3], (E_ATT, C, H), dtype=jnp.float32) * sq
        d['v_proj'] = jax.random.normal(ks[4], (E_ATT, C, H), dtype=jnp.float32) * sq
        d['o_proj'] = jax.random.normal(ks[5], (E_ATT, H, C), dtype=jnp.float32) * sq
        d['moe_sim'] = jax.random.normal(ks[6], (C, E_MOE), dtype=jnp.float32)
        d['moe_gates'] = jnp.zeros((E_MOE,), jnp.float32)
        d['w1'] = jax.random.normal(ks[7], (E_MOE, C, I), dtype=jnp.float32) * (1.0 / np.sqrt(C))
        d['w2'] = jax.random.normal(ks[8], (E_MOE, I, C), dtype=jnp.float32) * (1.0 / np.sqrt(I))
        return d
    _L0_ffn_in = _L0_ffn_setup()
    _d = {'L0_attn_x': _L0_attn_in['x'], 'L0_attn_Wqkv': _L0_attn_in['Wqkv'], 'L0_attn_Wo': _L0_attn_in['Wo'], 'L0_attn_log_xi': _L0_attn_in['log_xi'], 'L0_attn_pi_gate_logit': _L0_attn_in['pi_gate_logit'], 'L0_attn_e_gate_logit': _L0_attn_in['e_gate_logit'], 'L0_ffn_ln1_w': _L0_ffn_in['ln1_w'], 'L0_ffn_ln1_b': _L0_ffn_in['ln1_b'], 'L0_ffn_ln2_w': _L0_ffn_in['ln2_w'], 'L0_ffn_ln2_b': _L0_ffn_in['ln2_b'], 'L0_ffn_smha_sim': _L0_ffn_in['smha_sim'], 'L0_ffn_smha_gates': _L0_ffn_in['smha_gates'], 'L0_ffn_q_proj': _L0_ffn_in['q_proj'], 'L0_ffn_k_proj': _L0_ffn_in['k_proj'], 'L0_ffn_v_proj': _L0_ffn_in['v_proj'], 'L0_ffn_o_proj': _L0_ffn_in['o_proj'], 'L0_ffn_moe_sim': _L0_ffn_in['moe_sim'], 'L0_ffn_moe_gates': _L0_ffn_in['moe_gates'], 'L0_ffn_w1': _L0_ffn_in['w1'], 'L0_ffn_w2': _L0_ffn_in['w2']}
    _x0 = _d['L0_attn_x']
    _d['L0_attn_x'] = jax.random.normal(jax.random.fold_in(jax.random.key(seed), 1), (32, 256, 128), dtype=_x0.dtype)
    del _x0
    return _d

def reference(L0_attn_x, L0_attn_Wqkv, L0_attn_Wo, L0_attn_log_xi, L0_attn_pi_gate_logit, L0_attn_e_gate_logit, L0_ffn_ln1_w, L0_ffn_ln1_b, L0_ffn_ln2_w, L0_ffn_ln2_b, L0_ffn_smha_sim, L0_ffn_smha_gates, L0_ffn_q_proj, L0_ffn_k_proj, L0_ffn_v_proj, L0_ffn_o_proj, L0_ffn_moe_sim, L0_ffn_moe_gates, L0_ffn_w1, L0_ffn_w2):

    def _L0_attn_ref(x, Wqkv, Wo, log_xi, pi_gate_logit, e_gate_logit):
        import math
        import jax, jax.numpy as jnp
        import numpy as np
        D_MODEL = 128
        N_HEADS = 16
        D_HEAD = D_MODEL // N_HEADS
        BLOCK = 256
        BATCH = 2
        SEQ = 256

        def _rotate(t, cos, sin):
            t1 = t[..., 0::2]
            t2 = t[..., 1::2]
            r1 = t1 * cos - t2 * sin
            r2 = t1 * sin + t2 * cos
            return jnp.stack([r1, r2], axis=-1).reshape(t.shape)
        b, n, d = x.shape
        H, dh = (N_HEADS, D_HEAD)
        qkv = (x @ Wqkv.T).reshape(b, n, 3, H, dh)
        q = jnp.transpose(qkv[:, :, 0], (0, 2, 1, 3))
        k = jnp.transpose(qkv[:, :, 1], (0, 2, 1, 3))
        v = jnp.transpose(qkv[:, :, 2], (0, 2, 1, 3))
        pi_g = jax.nn.sigmoid(pi_gate_logit)
        e_g = jax.nn.sigmoid(e_gate_logit)
        kfrac = jnp.arange(0, dh, 2, dtype=jnp.float32) / dh
        pi_inv_freq = jnp.float32(math.pi) ** (1.0 - kfrac)
        pos = jnp.arange(n, dtype=jnp.float32)
        theta = pos[:, None] * pi_inv_freq[None, :]
        theta = theta[None, :, :] * pi_g[:, None, None]
        cos, sin = (jnp.cos(theta), jnp.sin(theta))
        q_rot = _rotate(q, cos, sin)
        k_rot = _rotate(k, cos, sin)
        scores = jnp.einsum('bhqd,bhkd->bhqk', q_rot, k_rot) / jnp.float32(math.sqrt(dh))
        xi = jnp.exp(log_xi)
        i = jnp.arange(n, dtype=jnp.float32)
        d_mat = jnp.abs(i[:, None] - i[None, :])
        decay_bias = -(d_mat[None, :, :] / xi[:, None, None]) * e_g[:, None, None]
        scores = scores + decay_bias[None]
        causal = jnp.tril(jnp.ones((n, n), dtype=bool))
        scores = jnp.where(causal[None, None], scores, jnp.float32(-jnp.inf))
        attn = jax.nn.softmax(scores, axis=-1)
        out = jnp.einsum('bhqk,bhkd->bhqd', attn, v)
        out = jnp.transpose(out, (0, 2, 1, 3)).reshape(b, n, d)
        return out @ Wo.T

    def _L0_ffn_ref(x, ln1_w, ln1_b, ln2_w, ln2_b, smha_sim, smha_gates, q_proj, k_proj, v_proj, o_proj, moe_sim, moe_gates, w1, w2):
        import jax, jax.numpy as jnp
        import numpy as np
        B, T, C = (4, 256, 128)
        H = 128
        E_ATT = 8
        E_MOE = 8
        I = 128
        MIN_ATT = 2
        MIN_MOE = 2
        EPS_LN = 1e-05

        def _normalize(x, axis):
            n = jnp.linalg.norm(x, axis=axis, keepdims=True)
            return x / jnp.maximum(n, 1e-12)

        def _layernorm(x, w, b):
            m = jnp.mean(x, axis=-1, keepdims=True)
            v = jnp.mean(jnp.square(x - m), axis=-1, keepdims=True)
            return (x - m) / jnp.sqrt(v + EPS_LN) * w + b

        def _gating(flat_hs, sim, gates, min_experts):
            logits = _normalize(flat_hs, -1) @ _normalize(sim, 0) - jax.nn.sigmoid(gates)
            gated = jax.nn.relu(logits)
            mask = (gated > 0).astype(gated.dtype)
            inactive = jnp.sum(mask, axis=1) == 0
            _, idx = jax.lax.top_k(logits, min_experts)
            onehot = jnp.sum(jax.nn.one_hot(idx, logits.shape[-1], dtype=gated.dtype), axis=1)
            put = inactive[:, None] & (onehot > 0)
            mask = jnp.where(put, 1.0, mask)
            masked = jnp.where(mask > 0, gated, -jnp.inf)
            return jax.nn.softmax(masked, axis=-1)
        b, t, c = x.shape
        n1 = _layernorm(x, ln1_w, ln1_b)
        rw = _gating(n1.reshape(b * t, c), smha_sim, smha_gates, MIN_ATT).reshape(b, t, -1)
        q = jnp.einsum('btc,ech,bte->bth', n1, q_proj, rw)
        k = jnp.einsum('btc,ech,bte->bth', n1, k_proj, rw)
        v = jnp.einsum('btc,ech,bte->bth', n1, v_proj, rw)
        scale = 1.0 / jnp.sqrt(jnp.asarray(q.shape[-1], q.dtype))
        scores = jnp.einsum('bth,bsh->bts', q, k) * scale
        causal = jnp.tril(jnp.ones((t, t), dtype=bool))
        scores = jnp.where(causal, scores, -jnp.inf)
        attn = jnp.einsum('bts,bsh->bth', jax.nn.softmax(scores, axis=-1), v)
        attn_out = jnp.einsum('bth,ehc,bte->btc', attn, o_proj, rw)
        hs = x + attn_out
        n2 = _layernorm(hs, ln2_w, ln2_b)
        rw2 = _gating(n2.reshape(b * t, c), moe_sim, moe_gates, MIN_MOE).reshape(b, t, -1)
        inter = jax.nn.gelu(jnp.einsum('btc,eci->btei', n2, w1), approximate=False)
        moe_out = jnp.einsum('btei,eic,bte->btc', inter, w2, rw2)
        return hs + moe_out
    x = L0_attn_x
    xn = _layernorm(x, axis=-1)
    x = x + _L0_attn_ref(xn, L0_attn_Wqkv, L0_attn_Wo, L0_attn_log_xi, L0_attn_pi_gate_logit, L0_attn_e_gate_logit) + _L0_ffn_ref(xn, L0_ffn_ln1_w, L0_ffn_ln1_b, L0_ffn_ln2_w, L0_ffn_ln2_b, L0_ffn_smha_sim, L0_ffn_smha_gates, L0_ffn_q_proj, L0_ffn_k_proj, L0_ffn_v_proj, L0_ffn_o_proj, L0_ffn_moe_sim, L0_ffn_moe_gates, L0_ffn_w1, L0_ffn_w2)
    return x

_drawn_inputs = setup_inputs


def setup_inputs(seed=0):
    import zlib

    import numpy as np

    out = dict(_drawn_inputs(seed))
    spreads = {'L0_attn_log_xi': (4.852030277252197, 0.6),
     'L0_attn_pi_gate_logit': (2.0, 0.6),
     'L0_attn_e_gate_logit': (2.0, 0.6),
     'L0_ffn_ln1_w': (1.0, 0.2),
     'L0_ffn_ln1_b': (0.0, 0.297),
     'L0_ffn_ln2_w': (1.0, 0.2),
     'L0_ffn_ln2_b': (0.0, 0.1),
     'L0_ffn_smha_gates': (0.0, 0.274),
     'L0_ffn_moe_gates': (0.0, 0.1)}
    factors = {'L0_attn_Wqkv': 8.0, 'L0_attn_Wo': 8.0, 'L0_ffn_q_proj': 3.535, 'L0_ffn_k_proj': 3.398}
    for name, (base, spread) in spreads.items():
        noise = np.random.default_rng([zlib.crc32(name.encode()), seed]).standard_normal(out[name].shape)
        drawn = base * np.exp(spread * noise) if base else spread * noise
        out[name] = jnp.asarray(drawn.astype(out[name].dtype))
    for name, factor in factors.items():
        out[name] = (out[name] * factor).astype(out[name].dtype)
    return out
```

```python
from contextlib import ExitStack

import numpy as np

import concourse.bass as bass
from concourse import mybir

F32 = mybir.dt.float32
BF16 = mybir.dt.bfloat16
ALU = mybir.AluOpType
ACT = mybir.ActivationFunctionType
AX_X = mybir.AxisListType.X

NB = 32
S = 256
D = 128
H = 16
DH = D // H
P = 128
T = S // P
E = 8
NG = 4
HG = H // NG
UNITS = 3 * NG
EPS = 1e-5
NORM2 = 1e-24
BIG = 1e30
TM = 4
MS = NB * T // TM
W2 = TM * P

R_BIAS_J = 0
R_BIAS_I = 3
R_PARTS = 8
R_MAX = R_PARTS + 6 * DH
Q_SLOTS = ((0, 3, 0), (3, 2, 1), (5, 1, 2))
K_SLOTS = ((0, 3, 0), (3, 2, 0), (5, 1, 0))
KR = P

LN_LINKS = 2 + 10
ROT_LINKS = 7
GATE_LINKS = 21 + 10
MAX_LINKS = 3


class Chain:

    def __init__(self, eng, sem, done_before, per):
        self.eng, self.sem, self.base, self.per, self.k = eng, sem, done_before * per, per, 0

    def add(self, ins):
        ins.then_inc(self.sem, 1)
        self.k += 1

    def link(self, ins):
        self.add(ins)
        self.wait()

    def wait(self):
        self.eng.wait_ge(self.sem, self.base + self.k)

    def close(self):
        assert self.k == self.per, (self.k, self.per)


RSQRT_LINKS = 10


def rsqrt(dve, c, y, v, t):
    c.link(dve.tensor_scalar(y.bitcast(mybir.dt.int32), v.bitcast(mybir.dt.int32), -0.5, float(0x5F3759DF),
                             ALU.mult, ALU.add))
    for _ in range(3):
        c.link(dve.scalar_tensor_tensor(t, y, -0.5, y, ALU.mult, ALU.mult))
        c.link(dve.tensor_tensor(t, t, v, ALU.mult))
        c.link(dve.scalar_tensor_tensor(y, t, 1.5, y, ALU.add, ALU.mult))


def build(nc, x, w_attn, w_o, log_xi, pi_logit, e_logit, ln1_w, ln1_b, ln2_w, ln2_b, sim1, gates1,
          q_proj, k_proj, v_proj, o_proj, sim2, gates2, w1, w2, c_ident, c_mask_qk, c_mask_kq, c_pos_freq,
          c_sin_sign, c_pos, c_rank, out):
    scr_parts = nc.dram_tensor("scr_parts", (2, 2, 3, DH, H, S), BF16, kind="Internal").ap()
    scr_rw = nc.dram_tensor("scr_rw", (2, E, S), F32, kind="Internal").ap()
    scr_rw2 = nc.dram_tensor("scr_rw2", (2, E, W2), F32, kind="Internal").ap()

    scr_base = nc.dram_tensor("scr_base", (NB, P, T, D), F32, kind="Internal").ap()

    with ExitStack() as ctx:
        def sb(name, shape, dt=F32):
            return ctx.enter_context(nc.sbuf_tensor(name, shape, dt))

        def sem(name):
            return ctx.enter_context(nc.semaphore(name))

        ident = sb("ident", [P, P])
        identb = sb("identb", [P, P], BF16)
        mask_in = sb("mask_in", [P, 2, P])
        mask_qk = sb("mask_qk", [P, HG, P], BF16)
        mask_kq = sb("mask_kq", [P, HG, P], BF16)
        wa = sb("wa", [P, 5, D])
        wo = sb("wo", [P, D])
        wq = sb("wq", [P, E, D])
        wk = sb("wk", [P, E, D])
        wv = sb("wv", [P, E, D])
        wop = sb("wop", [P, E, D])
        w1s = sb("w1s", [P, E, D])
        w2s = sb("w2s", [P, E, D])
        lnp = sb("lnp", [P, 4])
        simn = sb("simn", [P, 2, E])
        sg = sb("sg", [P, 2, E])
        rank = sb("rank", [P, E])
        ones_e = sb("ones_e", [P, E])
        ones_p = sb("ones_p", [P, P])
        cs = sb("cs", [P, 2, 2, S])
        theta = sb("theta", [P, S])
        trn = sb("trn", [P, 2, S])
        red = sb("red", [P, 2, S])
        sin_sign = sb("sin_sign", [P, 1])
        pig = sb("pig", [P, 1])
        bias_in = sb("bias_in", [H, 2])
        cpos = sb("cpos", [H, S])
        cb = sb("cb", [H, 2, S])
        cbp = sb("cbp", [H, 2, 3, S], BF16)
        ones_b = sb("ones_b", [3, 1, S], BF16)
        zeros_b = sb("zeros_b", [3, 1, S], BF16)
        sims = sb("sims", [P, 2, E])

        xt = sb("xt", [P, 2, T, D])
        xn = sb("xn", [P, 2, T, D])
        zt = sb("zt", [P, T, D])
        bst = sb("bst", [P, 2, TM, 6])
        bmv = sb("bmv", [P, 2, TM, 2])
        rstd = sb("rstd", [P, 2, TM])
        vstd = sb("vstd", [P, 2, TM])
        xnT = sb("xnT", [P, S])
        n1T = sb("n1T", [P, 2, S])
        sqT = sb("sqT", [P, W2])
        lgT = sb("lgT", [P, W2])
        gt = sb("gt", [P, 10, TM, E])
        gs = sb("gs", [P, 8, TM])
        rwT = sb("rwT", [E, W2])
        rep = sb("rep", [P, 2, E, S])
        n1s = sb("n1s", [P, E, S])
        ats = sb("ats", [P, E, S])
        rott = sb("rott", [P, 2, 2, S])
        rot = sb("rot", [P, 2, S])
        rres = sb("rres", [P, 2, S])
        parts = sb("parts", [P, 3, 2, S], BF16)
        qst = sb("qst", [P, 2, H, S], BF16)
        kst = sb("kst", [P, 2, H, S], BF16)
        vst = sb("vst", [P, 2, T, H, 32])
        mx = sb("mx", [P, T, H])
        mres = sb("mres", [P, T, H])
        mpart = sb("mpart", [P, T, P], BF16)
        mT = sb("mT", [3 * H, S], BF16)
        pr = sb("pr", [P, 2, 3, 512])
        ov = sb("ov", [P, 2, S])
        rden = sb("rden", [P, T, HG])
        att = sb("att", [P, T, D])
        attT = sb("attT", [P, S])
        qT = sb("qT", [P, S])
        kT = sb("kT", [P, S])
        vs = sb("vs", [P, T, D])
        smx = sb("smx", [P, 4, T])
        sp = sb("sp", [P, 3 * P])
        spT = sb("spT", [P, 3 * P])
        hs = sb("hs", [P, NB * T, D])
        bs = sb("bs", [P, 2, T, D])
        xa = sb("xa", [P, T, D])

        prf = pr[:].rearrange("p a i t -> p (a i t)")
        bt = prf[:, 0:2 * TM * D].rearrange("p (a i c) -> p a i c", a=2, i=TM)
        z2 = prf[:, 2 * TM * D:3 * TM * D].rearrange("p (i c) -> p i c", i=TM)
        rep2 = [v[:].rearrange("p a h t -> p (a h t)").bitcast(F32).rearrange("p (e t) -> p e t", e=E)
                for v in (qst, kst)]
        n1f, atf = (v[:].rearrange("p e t -> p (e t)") for v in (n1s, ats))
        n2T = n1f[:, 0:2 * W2].rearrange("p (a t) -> p a t", a=2)
        hg = n1f[:, 2 * W2:4 * W2].rearrange("p (a t) -> p a t", a=2)
        hgs = atf[:, 0:2 * W2].rearrange("p (a t) -> p a t", a=2)
        ot = atf[:, 2 * W2:4 * W2].rearrange("p (a i c) -> p a i c", a=2, i=TM)

        ps = ctx.enter_context(nc.psum_tensor("ps", [P, 8, 512], F32))
        S1, S2, PVB, QKB, G0, G1 = (0, 1), (2, 3), 4, 5, 6, 7

        ld_const, ld_w = sem("ld_const"), sem("ld_w")
        set_dve, set_act, set_pe, set_pool, set_dma = (
            sem("set_dve"), sem("set_act"), sem("set_pe"), sem("set_pool"), sem("set_dma"))
        x_in = sem("x_in")
        ln_chain = sem("ln_chain")
        ln_out = sem("ln_out")
        xzT_out = sem("xzT_out")
        xnT_done = sem("xnT_done")
        n1T_done = sem("n1T_done")
        sq_done = sem("sq_done")
        lgT_out = sem("lgT_out")
        lgT_done = sem("lgT_done")
        lg_out = sem("lg_out")
        lg_read = sem("lg_read")
        gate_chain = sem("gate_chain")
        tanh_in = sem("tanh_in")
        tanh_out = sem("tanh_out")
        rw_out = sem("rw_out")
        rwT_out = sem("rwT_out")
        rwT_done = sem("rwT_done")
        rw_stored = sem("rw_stored")
        rep_in = sem("rep_in")
        n1s_done = sem("n1s_done")
        rot_q_out = sem("rot_q_out")
        rot_k_out = sem("rot_k_out")
        rot_chain = sem("rot_chain")
        parts_out = sem("parts_out")
        parts_stored = sem("parts_stored")
        stack_in = sem("stack_in")
        v_out = sem("v_out")
        v_done = sem("v_done")
        s1_out = sem("s1_out")
        s1_read = sem("s1_read")
        max_chain = sem("max_chain")
        mT_out = sem("mT_out")
        mT_done = sem("mT_done")
        max_in = sem("max_in")
        s2_out = sem("s2_out")
        exp_done = sem("exp_done")
        pv_out = sem("pv_out")
        ov_done = sem("ov_done")
        ot_out = sem("ot_out")
        ot_read = sem("ot_read")
        attT_out = sem("attT_out")
        attT_done = sem("attT_done")
        wo_out = sem("wo_out")
        xa_done = sem("xa_done")
        qk_out = sem("qk_out")
        qkT_done = sem("qkT_done")
        ve_out = sem("ve_out")
        ve_done = sem("ve_done")
        ss_out = sem("ss_out")
        smax_done = sem("smax_done")
        sexp_done = sem("sexp_done")
        snorm_chain = sem("snorm_chain")
        snorm_done = sem("snorm_done")
        spT_out = sem("spT_out")
        spT_done = sem("spT_done")
        av_out = sem("av_out")
        ats_done = sem("ats_done")
        oe_out = sem("oe_out")
        hs_done = sem("hs_done")
        base_done = sem("base_done")
        base_stored = sem("base_stored")
        base_in = sem("base_in")
        ln2_chain = sem("ln2_chain")
        ln2_out = sem("ln2_out")
        zT2_out = sem("zT2_out")
        n2T_done = sem("n2T_done")
        sq2_done = sem("sq2_done")
        lgT2_out = sem("lgT2_out")
        lgT2_done = sem("lgT2_done")
        lg2_out = sem("lg2_out")
        lg2_read = sem("lg2_read")
        gate2_chain = sem("gate2_chain")
        tanh2_in = sem("tanh2_in")
        tanh2_out = sem("tanh2_out")
        rw2_out = sem("rw2_out")
        rwT2_out = sem("rwT2_out")
        rwT2_done = sem("rwT2_done")
        rw2_stored = sem("rw2_stored")
        rep2_in = sem("rep2_in")
        up_out = sem("up_out")
        gelu_done = sem("gelu_done")
        hgs_done = sem("hgs_done")
        moe_out = sem("moe_out")
        out_done = sem("out_done")
        out_stored = sem("out_stored")

        block = ctx.enter_context(nc.Block())
        N_CONST, N_W, N_SMALL = 13, 8, 5
        N_ROWS = 18
        SIN_READY, N_SET_DVE = 18, 55
        UP, MOE = (0, 1, 2), (3, 4)

        @block.sync
        def _(sp_):
            x_v = x.rearrange("b (i p) c -> b p i c", p=P)

            sp_.dma_start(xt[:, 0], x_v[0]).then_inc(x_in, 16)
            for dst, src in ((ident[:], c_ident), (mask_in[:, 0], c_mask_qk), (mask_in[:, 1], c_mask_kq),
                             (theta[:], c_pos_freq), (sin_sign[:], c_sin_sign), (cpos[:], c_pos),
                             (rank[:], c_rank), (lnp[:, 0:1], ln1_w), (lnp[:, 1:2], ln1_b),
                             (lnp[:, 2:3], ln2_w), (lnp[:, 3:4], ln2_b),
                             (sims[:, 0], sim1), (sims[:, 1], sim2)):
                sp_.dma_start(dst, src).then_inc(ld_const, 16)
            for dst, src in ((wa[:], w_attn), (wo[:], w_o), (wq[:], q_proj), (wk[:], k_proj),
                             (wv[:], v_proj), (wop[:], o_proj), (w1s[:], w1), (w2s[:], w2)):
                v = src.rearrange("e c h -> c e h") if len(src.shape) == 3 and src.shape[0] == E else src
                sp_.dma_start(dst, v).then_inc(ld_w, 16)
            sp_.wait_ge(set_pool, 2)
            sp_.wait_ge(set_dve, N_SET_DVE)
            for par in range(2):
                for part in range(3):
                    sp_.dma_start(kst[R_BIAS_J + part:R_BIAS_J + part + 1, par], cbp[:, 0, part]).then_inc(set_dma, 16)
                    sp_.dma_start(qst[R_BIAS_I + part:R_BIAS_I + part + 1, par], cbp[:, 1, part]).then_inc(set_dma, 16)
                sp_.dma_start(qst[R_BIAS_J:R_BIAS_J + 3, par], ones_b[:].broadcast_to((3, H, S))).then_inc(set_dma, 16)
                sp_.dma_start(kst[R_BIAS_I:R_BIAS_I + 3, par], ones_b[:].broadcast_to((3, H, S))).then_inc(set_dma, 16)
                sp_.dma_start(kst[R_MAX:R_MAX + 3, par], ones_b[:].broadcast_to((3, H, S))).then_inc(set_dma, 16)

            def stacks(b, par):
                sp_.wait_ge(parts_out, 1 + b)
                for side in range(2):
                    for part in range(3):
                        sp_.dma_start(scr_parts[par, side, part].rearrange("d h t -> h d t"),
                                      parts[:, part, side]).then_inc(parts_stored, 16)
                sp_.wait_ge(parts_stored, 96 * (b + 1))
                for side, dst, slots in ((0, qst, Q_SLOTS), (1, kst, K_SLOTS)):
                    v = scr_parts[par, side].rearrange("p d h t -> p d (h t)")
                    for first, n, part in slots:
                        rows = dst[R_PARTS + DH * first:R_PARTS + DH * (first + n), par].rearrange("p h t -> p (h t)")
                        src = v[part:part + 1].broadcast_to((n, DH, H * S)) if side == 0 and n > 1 else (
                            v[part:part + n].rearrange("p d x -> (p d) x"))
                        sp_.dma_start(rows, src).then_inc(stack_in, 16)
                sp_.dma_start(qst[R_MAX:R_MAX + 3, par], zeros_b[:].broadcast_to((3, H, S))).then_inc(stack_in, 16)

            def spread_weights(b, par):
                sp_.wait_ge(rwT_done, b + 1)
                sp_.dma_start(scr_rw[par], rwT[:, 0:S]).then_inc(rw_stored, 16)
                sp_.wait_ge(rw_stored, 16 * (b + 1))
                sp_.dma_start(rep[:, par].rearrange("p e t -> p (e t)"),
                              scr_rw[par].rearrange("(o e) t -> o (e t)", o=1).broadcast_to((P, E * S))
                              ).then_inc(rep_in, 16)

            def put_max(b, par):
                sp_.wait_ge(mT_done, b + 1)
                sp_.dma_start(qst[R_MAX:R_MAX + 3, par], mT[:]).then_inc(max_in, 16)

            def load_next(b, par):
                if isinstance(b, int):
                    src = x_v[b]
                else:
                    src = x_v[bass.ds(b, 1)].rearrange("o p i c -> p (o i) c")
                sp_.dma_start(xt[:, par], src).then_inc(x_in, 16)

            def store_base(n, u):
                sp_.wait_ge(base_done, n + 1)
                dst = scr_base[n] if isinstance(n, int) else scr_base[bass.ds(n, 1)].rearrange("o p i c -> p (o i) c")
                sp_.dma_start(dst, bs[:, u]).then_inc(base_stored, 16)

            def step(n, u, last):
                if last:
                    store_base(n, u)
                    return
                sp_.wait_ge(base_done, n)
                load_next(n + 1, 1 - u)
                stacks(n + 1, 1 - u)
                spread_weights(n + 1, 1 - u)
                put_max(n + 1, 1 - u)
                store_base(n, u)

            stacks(0, 0)
            spread_weights(0, 0)
            put_max(0, 0)
            step(0, 0, False)
            step(1, 1, False)
            with sp_.Fori(1, NB // 2 - 1) as j:
                for u in range(2):
                    step(2 * j + u, u, False)
            step(NB - 2, 0, False)
            step(NB - 1, 1, True)

            def spread2(g, par):
                sp_.wait_ge(rwT2_done, g + 1)
                sp_.dma_start(scr_rw2[par], rwT[:]).then_inc(rw2_stored, 16)
                sp_.wait_ge(rw2_stored, 16 * (g + 1))
                sp_.dma_start(rep2[par].rearrange("p e t -> p (e t)"),
                              scr_rw2[par].rearrange("(o e) t -> o (e t)", o=1).broadcast_to((P, E * W2))
                              ).then_inc(rep2_in, 16)

            o_v = out.rearrange("b (i p) c -> p (b i) c", p=P)

            base_v = scr_base.rearrange("b p i c -> p b (i c)")

            def load_base(g, par):
                v = base_v[:, 2 * g:2 * g + 2] if isinstance(g, int) else base_v[:, bass.ds(g * 2, 2)]
                sp_.dma_start(bt[:, par].rearrange("p (b i) c -> p b (i c)", b=2), v).then_inc(base_in, 16)

            def step2(g, u, last):
                if not last:
                    sp_.wait_ge(out_done, g)
                    load_base(g + 1, 1 - u)
                    spread2(g + 1, 1 - u)
                sp_.wait_ge(out_done, g + 1)
                dst = o_v[:, TM * g:TM * g + TM] if isinstance(g, int) else o_v[:, bass.ds(g * TM, TM)]
                sp_.dma_start(dst, ot[:, u]).then_inc(out_stored, 16)

            sp_.wait_ge(base_stored, 16 * NB)
            load_base(0, 0)
            spread2(0, 0)
            step2(0, 0, False)
            step2(1, 1, False)
            with sp_.Fori(1, MS // 2 - 1) as j:
                for u in range(2):
                    step2(2 * j + u, u, False)
            step2(MS - 2, 0, False)
            step2(MS - 1, 1, True)
            sp_.wait_ge(out_stored, 16 * MS)

        @block.gpsimd
        def _(pool):
            pool.memset(qst[:], 0.0).then_inc(set_pool, 1)
            pool.memset(kst[:], 0.0).then_inc(set_pool, 1)

            def scale(b, par):
                pool.wait_ge(rep_in, 16 * (b + 1))
                pool.wait_ge(n1T_done, b + 1)
                pool.wait_ge(ve_out, b)
                pool.tensor_tensor(n1s[:], rep[:, par], n1T[:, par:par + 1, :].broadcast_to((P, E, S)),
                                   ALU.mult).then_inc(n1s_done, 1)

            scale(0, 0)
            scale(1, 1)
            scale(2, 0)
            with pool.Fori(1, NB // 2 - 1) as j:
                for u in range(2):
                    scale(2 * j + u + 1, 1 - u)
            scale(NB - 1, 1)

        @block.scalar
        def _(act):
            def col(v, n):
                return v.rearrange("(p o) -> p o", o=1)
            act.dma_start(pig[:], pi_logit.rearrange("(h o) -> h o", o=1).broadcast_to((H, DH))
                          ).then_inc(set_dma, 16)
            act.dma_start(bias_in[:, 0:1], col(log_xi, H)).then_inc(set_dma, 16)
            act.dma_start(bias_in[:, 1:2], col(e_logit, H)).then_inc(set_dma, 16)
            act.dma_start(sg[:, 0], gates1.rearrange("(o e) -> o e", o=1).broadcast_to((P, E))).then_inc(set_dma, 16)
            act.dma_start(sg[:, 1], gates2.rearrange("(o e) -> o e", o=1).broadcast_to((P, E))).then_inc(set_dma, 16)
            act.wait_ge(set_dma, 16 * N_SMALL)
            act.activation(pig[:], pig[:], ACT.Tanh, scale=0.5).then_inc(set_act, 1)
            act.activation(sg[:], sg[:], ACT.Tanh, scale=0.5).then_inc(set_act, 1)
            act.activation(bias_in[:, 1:2], bias_in[:, 1:2], ACT.Tanh, scale=0.5).then_inc(set_act, 1)
            act.activation(bias_in[:, 0:1], bias_in[:, 0:1], ACT.Exp, scale=-1.0).then_inc(set_act, 1)
            act.wait_ge(set_dve, SIN_READY)
            act.activation(red[:], red[:], ACT.Sin).then_inc(set_act, 1)

            def evac_norm(b, par):
                act.wait_ge(xzT_out, b + 1)
                act.activation(xnT[:], ps[:, G0, 0:S], ACT.Copy).then_inc(xnT_done, 1)
                act.activation(n1T[:, par], ps[:, G0, S:2 * S], ACT.Identity, bias=lnp[:, 1:2],
                               scale=lnp[:, 0:1]).then_inc(n1T_done, 1)
                act.wait_ge(n1T_done, b + 1)
                act.activation(sqT[:, 0:S], n1T[:, par], ACT.Square).then_inc(sq_done, 1)

            def evac_logits(b):
                act.wait_ge(lgT_out, b + 1)
                act.activation(lgT[0:E, 0:S], ps[0:E, G0, 0:S], ACT.Copy).then_inc(lgT_done, 1)
                act.activation(lgT[32:32 + E, 0:S], ps[32:32 + E, G0, 0:S], ACT.Copy).then_inc(lgT_done, 1)

            def evac_v(b, par):
                act.wait_ge(v_out, b + 1)
                act.activation(vst[:, par, :, :, 0:DH],
                               ps[:, G1, 0:T * D].rearrange("p (i h d) -> p i h d", i=T, d=DH),
                               ACT.Copy).then_inc(v_done, 1)

            def gate_tanh(b):
                act.wait_ge(tanh_in, b + 1)
                act.activation(gt[:, 9, 0:T], gt[:, 1, 0:T], ACT.Tanh, scale=0.5).then_inc(tanh_out, 1)

            def evac_weights(b):
                act.wait_ge(rwT_out, b + 1)
                act.wait_ge(rw_stored, 16 * b)
                act.activation(rwT[:, 0:S], ps[0:E, G1, 0:S], ACT.Copy).then_inc(rwT_done, 1)

            def evac_max(b):
                act.wait_ge(mT_out, b + 1)
                act.wait_ge(max_in, 16 * b)
                act.activation(mT[:], ps[0:3 * H, G1, 0:S // 2].bitcast(BF16), ACT.Copy).then_inc(mT_done, 1)

            def exps(n, k):
                G, i = divmod(k, 3)
                act.wait_ge(s2_out, UNITS * n + k + 1)
                if i == 0:
                    act.wait_ge(pv_out, NG * n + max(G - 1, 0))
                act.activation(pr[:, G % 2, i], ps[:, S2[k % 2]], ACT.Exp).then_inc(exp_done, 1)

            def evac_pv(n, G):
                act.wait_ge(pv_out, NG * n + G + 1)
                act.wait_ge(ot_out, NG * n + max(G - 1, 0))
                act.activation(ov[:, G % 2], ps[:, PVB, 0:S], ACT.Copy).then_inc(ov_done, 1)

            def evac_qk(n):
                act.wait_ge(qk_out, n + 1)
                act.activation(qT[:], ps[:, QKB, 0:S], ACT.Copy, scale=D ** -0.5).then_inc(qkT_done, 1)
                act.activation(kT[:], ps[:, QKB, S:2 * S], ACT.Copy).then_inc(qkT_done, 1)

            def soft_exp(n):
                act.wait_ge(smax_done, 2 * n + 2)
                act.activation(sp[:, 0:P], ps[:, G1, 0:P], ACT.Exp, bias=smx[:, 1, 0:1],
                               accum_out=smx[:, 2, 0:1]).then_inc(sexp_done, 1)
                act.activation(sp[:, P:3 * P], ps[:, G1, P:3 * P], ACT.Exp, bias=smx[:, 1, 1:2],
                               accum_out=smx[:, 2, 1:2]).then_inc(sexp_done, 1)

            def evac_soft(n):
                act.wait_ge(spT_out, n + 1)
                act.activation(spT[:], ps[:, G1, 0:3 * P], ACT.Copy).then_inc(spT_done, 1)

            def evac_ve(n):
                act.wait_ge(ve_out, n + 1)
                act.activation(vs[:], ps[:, QKB, 0:T * D].rearrange("p (i c) -> p i c", i=T),
                               ACT.Copy).then_inc(ve_done, 1)

            def evac_att(n):
                act.wait_ge(attT_out, n + 1)
                act.activation(attT[:], ps[:, G0, 0:S], ACT.Copy).then_inc(attT_done, 1)

            def step(n, u, last):
                f, pf = n + 1, 1 - u
                if not last:
                    evac_norm(f, pf)
                exps(n, 0)
                exps(n, 1)
                if not last:
                    evac_logits(f)
                exps(n, 2)
                if not last:
                    evac_v(f, pf)
                exps(n, 3)
                evac_pv(n, 0)
                exps(n, 4)
                if not last:
                    gate_tanh(f)
                exps(n, 5)
                exps(n, 6)
                evac_pv(n, 1)
                evac_qk(n)
                if not last:
                    evac_weights(f)
                exps(n, 7)
                exps(n, 8)
                soft_exp(n)
                evac_pv(n, 2)
                exps(n, 9)
                exps(n, 10)
                evac_soft(n)
                exps(n, 11)
                evac_ve(n)
                evac_pv(n, 3)
                evac_att(n)
                if not last:
                    evac_max(f)

            evac_norm(0, 0)
            evac_logits(0)
            evac_v(0, 0)
            gate_tanh(0)
            evac_weights(0)
            evac_max(0)
            step(0, 0, False)
            step(1, 1, False)
            with act.Fori(1, NB // 2 - 1) as j:
                for u in range(2):
                    step(2 * j + u, u, False)
            step(NB - 2, 0, False)
            step(NB - 1, 1, True)

            act.wait_ge(snorm_done, NB)
            act.activation(smx[:, 0], smx[:, 3], ACT.Gelu).then_inc(set_act, 1)

            def evac_norm2(g, par):
                act.wait_ge(zT2_out, g + 1)
                act.activation(n2T[:, par], ps[:, G0], ACT.Identity, bias=lnp[:, 3:4],
                               scale=lnp[:, 2:3]).then_inc(n2T_done, 1)
                act.wait_ge(n2T_done, g + 1)
                act.activation(sqT[:], n2T[:, par], ACT.Square).then_inc(sq2_done, 1)

            def evac_logits2(g):
                act.wait_ge(lgT2_out, g + 1)
                act.activation(lgT[0:E], ps[0:E, G1], ACT.Copy).then_inc(lgT2_done, 1)
                act.activation(lgT[32:32 + E], ps[32:32 + E, G1], ACT.Copy).then_inc(lgT2_done, 1)

            def gate_tanh2(g):
                act.wait_ge(tanh2_in, g + 1)
                act.activation(gt[:, 9], gt[:, 1], ACT.Tanh, scale=0.5).then_inc(tanh2_out, 1)

            def evac_weights2(g):
                act.wait_ge(rwT2_out, g + 1)
                act.wait_ge(rw2_stored, 16 * g)
                act.activation(rwT[:], ps[0:E, G1], ACT.Copy).then_inc(rwT2_done, 1)

            def gelu(g, e):
                act.wait_ge(up_out, E * g + e + 1)
                act.wait_ge(hgs_done, E * g + max(e - 1, 0))
                act.activation(hg[:, e % 2], ps[:, UP[e % 3]], ACT.Gelu).then_inc(gelu_done, 1)

            def step2(g, u, last):
                for e in range(E):
                    if not last and e == 1:
                        evac_norm2(g + 1, 1 - u)
                    if not last and e == 2:
                        evac_logits2(g + 1)
                    if not last and e == 4:
                        gate_tanh2(g + 1)
                    if not last and e == 7:
                        evac_weights2(g + 1)
                    gelu(g, e)

            evac_norm2(0, 0)
            evac_logits2(0)
            gate_tanh2(0)
            evac_weights2(0)
            step2(0, 0, False)
            step2(1, 1, False)
            with act.Fori(1, MS // 2 - 1) as j:
                for u in range(2):
                    step2(2 * j + u, u, False)
            step2(MS - 2, 0, False)
            step2(MS - 1, 1, True)

        @block.vector
        def _(dve):
            ch = Chain(dve, set_dve, 0, N_SET_DVE)
            ch.add(dve.memset(ones_e[:], 1.0))
            ch.add(dve.memset(ones_p[:], 1.0))
            ch.add(dve.memset(ones_b[:], 1.0))
            ch.add(dve.memset(zeros_b[:], 0.0))
            ch.add(dve.memset(lgT[:], 0.0))
            ch.add(dve.memset(mpart[:], 0.0))
            ch.add(dve.memset(vst[:], 0.0))
            dve.wait_ge(ld_const, 16 * N_CONST)
            dve.wait_ge(set_act, 4)
            ch.link(dve.tensor_scalar(pig[:], pig[:], 0.5, 0.5, ALU.mult, ALU.add))
            ch.link(dve.tensor_scalar(theta[:], theta[:], pig[:, 0:1], None, ALU.mult))
            ROUND = 1.5 * 2.0 ** 23
            C1 = 6.28125
            C2 = float(np.float32(np.round((2 * np.pi - C1) * 2 ** 22) / 2 ** 22))
            C3 = float(2 * np.pi - C1 - C2)
            LIM = 3.1415925
            ch.add(dve.tensor_scalar(trn[:, 0], theta[:], 0.5 / np.pi, 0.25, ALU.mult, ALU.add))
            ch.link(dve.tensor_scalar(trn[:, 1], theta[:], 0.5 / np.pi, None, ALU.mult))
            ch.link(dve.tensor_scalar(trn[:], trn[:], ROUND, None, ALU.add))
            ch.link(dve.tensor_scalar(trn[:], trn[:], -ROUND, None, ALU.add))
            for i in range(2):
                ins = dve.scalar_tensor_tensor(red[:, i], trn[:, i], -C1, theta[:], ALU.mult, ALU.add)
            ch.link(ins)
            ch.link(dve.scalar_tensor_tensor(red[:], trn[:], -C2, red[:], ALU.mult, ALU.add))
            ch.link(dve.scalar_tensor_tensor(red[:], trn[:], -C3, red[:], ALU.mult, ALU.add))
            ch.link(dve.tensor_scalar(red[:, 0], red[:, 0], float(np.pi / 2), None, ALU.add))
            ch.link(dve.tensor_scalar(red[:], red[:], LIM, -LIM, ALU.min, ALU.max))
            assert ch.k == SIN_READY, ch.k
            dve.wait_ge(set_act, 5)
            qs = DH ** -0.5
            ch.add(dve.tensor_scalar(cs[:, 0, 0], red[:, 0], qs, None, ALU.mult))
            ch.add(dve.tensor_scalar(cs[:, 0, 1], red[:, 1], sin_sign[:, 0:1], qs, ALU.mult, ALU.mult))
            ch.add(dve.tensor_copy(cs[:, 1, 0], red[:, 0]))
            ch.add(dve.tensor_scalar(cs[:, 1, 1], red[:, 1], sin_sign[:, 0:1], None, ALU.mult))
            ch.link(dve.tensor_scalar(bias_in[:, 1:2], bias_in[:, 1:2], 0.5, 0.5, ALU.mult, ALU.add))
            ch.link(dve.tensor_tensor(bias_in[:, 0:1], bias_in[:, 0:1], bias_in[:, 1:2], ALU.mult))
            ch.link(dve.tensor_scalar(cb[:, 0], cpos[:], bias_in[:, 0:1], None, ALU.mult))
            ch.link(dve.tensor_scalar(cb[:, 1], cb[:, 0], -1.0, None, ALU.mult))
            for part in range(3):
                ch.link(dve.tensor_copy(cbp[:, :, part], cb[:]))
                if part < 2:
                    ch.link(dve.tensor_tensor(cb[:], cb[:], cbp[:, :, part], ALU.subtract))
            for h in range(HG):
                ch.add(dve.tensor_copy(mask_qk[:, h], mask_in[:, 0]))
                ch.add(dve.tensor_copy(mask_kq[:, h], mask_in[:, 1]))
            ch.add(dve.tensor_copy(identb[:], ident[:]))
            ch.add(dve.memset(vst[:, :, :, :, DH:DH + 1], 1.0))
            ch.add(dve.tensor_scalar(sg[:], sg[:], 0.5, 0.5, ALU.mult, ALU.add))
            ch.link(dve.tensor_tensor(gt[:, 0:2, 0], sims[:], sims[:], ALU.mult))
            dve.wait_ge(set_pe, 1)
            ch.link(dve.tensor_scalar(gt[:, 2:4, 0], ps[:, G0, 0:2 * E].rearrange("p (a e) -> p a e", a=2),
                                      NORM2, None, ALU.max))
            rsqrt(dve, ch, gt[:, 4:6, 0], gt[:, 2:4, 0], gt[:, 6:8, 0])
            ch.link(dve.tensor_tensor(simn[:], sims[:], gt[:, 4:6, 0], ALU.mult))
            ch.close()

            def layer_norm(b, par):
                c = Chain(dve, ln_chain, b, 2 * LN_LINKS)
                dve.wait_ge(x_in, 16 * (b + 1))
                dve.wait_ge(xzT_out, b)
                for rnd, (src, dst) in enumerate(((xt[:, par], xn[:, par]), (xn[:, par], zt[:]))):
                    for i in range(T):
                        dve.bn_stats(bst[:, rnd, i], src[:, i])
                    dve.drain()
                    for i in range(T):
                        ins = dve.bn_aggr(bmv[:, rnd, i], bst[:, rnd, i])
                    c.link(ins)
                    c.link(dve.tensor_scalar(vstd[:, 0, 0:T], bmv[:, rnd, 0:T, 1], EPS, None, ALU.add))
                    rsqrt(dve, c, rstd[:, rnd, 0:T], vstd[:, 0, 0:T], vstd[:, 1, 0:T])
                    for i in range(T):
                        ins = dve.tensor_scalar(dst[:, i], src[:, i], bmv[:, rnd, i, 0:1], rstd[:, rnd, i:i + 1],
                                                ALU.subtract, ALU.mult)
                        if rnd == 1 or i == T - 1:
                            ins.then_inc(ln_out, 1)
                    if rnd == 0:
                        dve.wait_ge(ln_out, (b * 3) + 1)
                c.close()

            def rotate(b):
                c = Chain(dve, rot_chain, b, ROT_LINKS)
                dve.wait_ge(rot_q_out, b + 1)
                c.link(dve.tensor_tensor(rott[:, 0], ps[:, G1].rearrange("p (a t) -> p a t", a=2), cs[:, 0], ALU.mult))
                c.add(dve.tensor_tensor(rot[:, 0], rott[:, 0, 0], rott[:, 0, 1], ALU.add))
                dve.wait_ge(rot_k_out, b + 1)
                c.link(dve.tensor_tensor(rott[:, 1], ps[:, G1].rearrange("p (a t) -> p a t", a=2), cs[:, 1], ALU.mult))
                c.link(dve.tensor_tensor(rot[:, 1], rott[:, 1, 0], rott[:, 1, 1], ALU.add))
                dve.wait_ge(parts_stored, 96 * b)
                c.link(dve.tensor_copy(parts[:, 0], rot[:]))
                c.link(dve.tensor_tensor(rres[:], rot[:], parts[:, 0], ALU.subtract))
                c.link(dve.tensor_copy(parts[:, 1], rres[:]))
                dve.tensor_tensor(parts[:, 2], rres[:], parts[:, 1], ALU.subtract).then_inc(parts_out, 1)
                c.close()

            def gating(b, nt, which, q):
                chain, lg_out, lg_read, tanh_in, tanh_out, rwT_out, rw_out = q
                c = Chain(dve, chain, b, GATE_LINKS)
                L, Dm, A, B2, C2_, F = (gt[:, k, 0:nt] for k in range(6))
                th = gt[:, 9, 0:nt]
                m1, m2, mc, rn, ina, tot = (gs[:, k, 0:nt] for k in range(6))

                def bc(v):
                    return v.rearrange("p (t o) -> p t o", o=1).broadcast_to((P, nt, E))
                rk = rank[:].rearrange("p (o e) -> p o e", o=1).broadcast_to((P, nt, E))
                sgb = sg[:, which:which + 1].broadcast_to((P, nt, E))
                lg = ps[:, LGB[which], 0:P * nt].rearrange("p (i k) -> p i k", k=P)
                dve.wait_ge(lg_out, b + 1)
                c.link(dve.tensor_scalar(rn, lg[:, :, 32], NORM2, None, ALU.max))
                rsqrt(dve, c, gs[:, 6, 0:nt], rn, gs[:, 7, 0:nt])
                dve.tensor_tensor(L, lg[:, :, 0:E], bc(gs[:, 6, 0:nt]), ALU.mult).then_inc(lg_read, 1)
                dve.wait_ge(lg_read, b + 1)
                c.link(dve.tensor_tensor(L, L, sgb, ALU.subtract))
                c.link(dve.tensor_reduce(m1, L, AX_X, ALU.max))
                dve.tensor_tensor(Dm, L, bc(m1), ALU.subtract).then_inc(tanh_in, 1)
                dve.wait_ge(tanh_in, b + 1)
                c.link(dve.scalar_tensor_tensor(A, Dm, 0.0, rk, ALU.is_ge, ALU.mult))
                c.link(dve.tensor_reduce(mc, A, AX_X, ALU.max))
                c.link(dve.tensor_tensor(A, A, bc(mc), ALU.is_equal))
                c.link(dve.scalar_tensor_tensor(B2, A, -BIG, L, ALU.mult, ALU.add))
                c.link(dve.tensor_reduce(m2, B2, AX_X, ALU.max))
                c.link(dve.tensor_tensor(C2_, B2, bc(m2), ALU.is_equal))
                c.link(dve.tensor_tensor(C2_, C2_, rk, ALU.mult))
                c.link(dve.tensor_reduce(mc, C2_, AX_X, ALU.max))
                c.link(dve.tensor_tensor(C2_, C2_, bc(mc), ALU.is_equal))
                c.add(dve.tensor_scalar(ina, m1, 0.0, None, ALU.is_le))
                c.link(dve.tensor_tensor(F, A, C2_, ALU.add))
                c.add(dve.tensor_tensor(F, F, bc(ina), ALU.mult))
                dve.wait_ge(tanh_out, b + 1)
                c.add(dve.tensor_scalar(A, th, 1.0, None, ALU.add))
                c.link(dve.tensor_scalar(B2, th, -1.0, 1.0, ALU.mult, ALU.add))
                c.link(dve.reciprocal(B2, B2))
                c.link(dve.tensor_tensor(A, A, B2, ALU.mult))
                c.link(dve.scalar_tensor_tensor(A, L, 0.0, A, ALU.is_gt, ALU.mult))
                dve.wait_ge(rwT_out, b)
                fin = gt[:, 6, 0:nt]
                dve.tensor_tensor(F, A, F, ALU.add).then_inc(rw_out, 1)
                dve.wait_ge(rw_out, 3 * b + 1)
                dve.tensor_reduce(tot, F, AX_X, ALU.add).then_inc(rw_out, 1)
                dve.wait_ge(rw_out, 3 * b + 2)
                c.link(dve.reciprocal(tot, tot))
                dve.tensor_tensor(fin, F, bc(tot), ALU.mult).then_inc(rw_out, 1)
                c.close()

            LGB = (G0, G0)
            gate1 = (gate_chain, lg_out, lg_read, tanh_in, tanh_out, rwT_out, rw_out)
            gate2 = (gate2_chain, lg2_out, lg2_read, tanh2_in, tanh2_out, rwT2_out, rw2_out)

            def row_max(b, k):
                G, i = divmod(k, 3)
                dve.wait_ge(s1_out, UNITS * b + k + 1)
                if k == 0:
                    dve.wait_ge(max_chain, (MAX_LINKS + 1) * b)
                n = HG if i == 0 else 2
                h = HG * G + (0 if i < 2 else 2)
                dve.tensor_reduce(mx[:, min(i, 1), h:h + n], ps[:, S1[k % 2]].rearrange("p (h t) -> p h t", h=n),
                                  AX_X, ALU.max).then_inc(s1_read, 1)

            def max_parts(b):
                c = Chain(dve, max_chain, b, MAX_LINKS + 1)
                mp = [mpart[:, :, k * H:(k + 1) * H] for k in range(3)]
                dve.wait_ge(s1_read, UNITS * (b + 1))
                dve.wait_ge(mT_out, b)
                c.link(dve.tensor_scalar(mp[0], mx[:], -1.0, None, ALU.mult))
                c.link(dve.scalar_tensor_tensor(mres[:], mx[:], -1.0, mp[0], ALU.mult, ALU.subtract))
                c.link(dve.tensor_copy(mp[1], mres[:]))
                c.add(dve.tensor_tensor(mp[2], mres[:], mp[1], ALU.subtract))
                c.close()

            def normalise(n, G):
                dve.wait_ge(ot_out, NG * n + G + 1)
                o = ps[:, G0, 0:S].rearrange("p (i h r) -> p i h r", i=T, r=32)
                c = Chain(dve, ot_read, NG * n + G, 2)
                c.link(dve.reciprocal(rden[:], o[:, :, :, DH]))
                if G == 0:
                    dve.wait_ge(attT_out, n)
                for i in range(T):
                    ins = dve.tensor_tensor(
                        att[:, i, DH * HG * G:DH * HG * (G + 1)].rearrange("p (h d) -> p h d", d=DH),
                        o[:, i, :, 0:DH],
                        rden[:, i].rearrange("p (h o) -> p h o", o=1).broadcast_to((P, HG, DH)), ALU.mult)
                c.add(ins)
                c.close()

            def soft_max(n):
                dve.wait_ge(ss_out, n + 1)
                dve.tensor_reduce(smx[:, 0, 0:1], ps[:, G1, 0:P], AX_X, ALU.max)
                dve.tensor_reduce(smx[:, 0, 1:2], ps[:, G1, P:3 * P], AX_X, ALU.max).then_inc(smax_done, 1)
                dve.wait_ge(smax_done, 2 * n + 1)
                dve.tensor_scalar(smx[:, 1], smx[:, 0], -1.0, None, ALU.mult).then_inc(smax_done, 1)

            def soft_norm(n):
                dve.wait_ge(sexp_done, 2 * n + 2)
                dve.reciprocal(smx[:, 3], smx[:, 2]).then_inc(snorm_chain, 1)
                dve.wait_ge(snorm_chain, n + 1)
                dve.tensor_scalar(sp[:, 0:P], sp[:, 0:P], smx[:, 3, 0:1], None, ALU.mult)
                dve.tensor_scalar(sp[:, P:3 * P], sp[:, P:3 * P], smx[:, 3, 1:2], None, ALU.mult
                                  ).then_inc(snorm_done, 1)

            def scale_att(n, u):
                dve.wait_ge(av_out, n + 1)
                dve.wait_ge(oe_out, n)
                dve.wait_ge(rep_in, 16 * (n + 1))
                dve.tensor_tensor(ats[:], rep[:, u],
                                  ps[:, G1:G1 + 1, 0:S].broadcast_to((P, E, S)), ALU.mult).then_inc(ats_done, 1)

            def add_x(n, u):
                dve.wait_ge(wo_out, n + 1)
                dve.tensor_tensor(xa[:], xt[:, u], ps[:, G0, 0:T * D].rearrange("p (i c) -> p i c", i=T),
                                  ALU.add).then_inc(xa_done, 1)

            def add_hs(n, u):
                dve.wait_ge(oe_out, n + 1)
                hv = hs[:, T * n:T * n + T] if isinstance(n, int) else hs[:, bass.ds(n * T, T)]
                dve.tensor_tensor(hv, xn[:, u], ps[:, G1, 0:T * D].rearrange("p (i c) -> p i c", i=T),
                                  ALU.add).then_inc(hs_done, 1)
                dve.wait_ge(hs_done, n + 1)
                dve.wait_ge(xa_done, n + 1)
                dve.wait_ge(base_stored, 16 * n)
                dve.tensor_tensor(bs[:, u], hv, xa[:], ALU.add).then_inc(base_done, 1)

            def step(n, u, last):
                f, pf = n + 1, 1 - u
                if not last:
                    layer_norm(f, pf)
                    rotate(f)
                    gating(f, T, 0, gate1)
                normalise(n, 0)
                normalise(n, 1)
                soft_max(n)
                if not last:
                    row_max(f, 0)
                normalise(n, 2)
                soft_norm(n)
                if not last:
                    row_max(f, 1)
                    row_max(f, 2)
                    row_max(f, 3)
                    row_max(f, 4)
                normalise(n, 3)
                if not last:
                    row_max(f, 5)
                scale_att(n, u)
                if not last:
                    row_max(f, 6)
                    row_max(f, 7)
                    row_max(f, 8)
                add_x(n, u)
                if not last:
                    row_max(f, 9)
                    row_max(f, 10)
                add_hs(n, u)
                if not last:
                    row_max(f, 11)
                    max_parts(f)

            layer_norm(0, 0)
            rotate(0)
            gating(0, T, 0, gate1)
            for k in range(UNITS):
                row_max(0, k)
            max_parts(0)
            step(0, 0, False)
            step(1, 1, False)
            with dve.Fori(1, NB // 2 - 1) as j:
                for u in range(2):
                    step(2 * j + u, u, False)
            step(NB - 2, 0, False)
            step(NB - 1, 1, True)

            def layer_norm2(g):
                c = Chain(dve, ln2_chain, g, LN_LINKS)
                dve.wait_ge(zT2_out, g)
                dve.wait_ge(hs_done, NB)

                def h(i):
                    return hs[:, TM * g + i] if isinstance(g, int) else hs[:, bass.ds(g * TM + i, 1)].rearrange(
                        "p o c -> p (o c)")
                for i in range(TM):
                    dve.bn_stats(bst[:, 0, i], h(i))
                dve.drain()
                for i in range(TM):
                    ins = dve.bn_aggr(bmv[:, 0, i], bst[:, 0, i])
                c.link(ins)
                c.link(dve.tensor_scalar(vstd[:, 0], bmv[:, 0, :, 1], EPS, None, ALU.add))
                rsqrt(dve, c, rstd[:, 0], vstd[:, 0], vstd[:, 1])
                for i in range(TM):
                    dve.tensor_scalar(z2[:, i], h(i), bmv[:, 0, i, 0:1], rstd[:, 0, i:i + 1],
                                      ALU.subtract, ALU.mult).then_inc(ln2_out, 1)
                c.close()

            def scale_gelu(g, e, par):
                dve.wait_ge(gelu_done, E * g + e + 1)
                dve.wait_ge(rep2_in, 16 * (g + 1))
                dve.wait_ge(moe_out, E * g + max(e - 1, 0))
                dve.tensor_tensor(hgs[:, e % 2], hg[:, e % 2], rep2[par][:, e], ALU.mult).then_inc(hgs_done, 1)

            def finish(g, u):
                dve.wait_ge(moe_out, E * (g + 1))
                if not isinstance(g, int) or g >= 1:
                    dve.wait_ge(out_stored, 16 * (g - 1) if isinstance(g, int) else 16 * g)
                dve.wait_ge(base_in, 16 * (g + 1))
                dve.tensor_tensor(ot[:, u], bt[:, u], ps[:, MOE[u]].rearrange("p (i c) -> p i c", i=TM),
                                  ALU.add).then_inc(out_done, 1)

            def step2(g, u, last):
                for e in range(E):
                    if not last and e == 0:
                        layer_norm2(g + 1)
                    if not last and e == 4:
                        gating(g + 1, TM, 1, gate2)
                    scale_gelu(g, e, u)
                finish(g, u)

            dve.wait_ge(base_done, NB)
            layer_norm2(0)
            gating(0, TM, 1, gate2)
            step2(0, 0, False)
            step2(1, 1, False)
            with dve.Fori(1, MS // 2 - 1) as j:
                for u in range(2):
                    step2(2 * j + u, u, False)
            step2(MS - 2, 0, False)
            step2(MS - 1, 1, True)

        @block.tensor
        def _(pe):
            mm = pe.matmul
            pe.wait_ge(set_dve, N_SET_DVE - 12)
            mm(ps[:, G0, 0:2 * E], ones_p[:], gt[:, 0:2, 0], start=True, stop=True).then_inc(set_pe, 1)
            pe.wait_ge(set_dve, N_SET_DVE)
            pe.wait_ge(ld_w, 16 * N_W)
            pe.wait_ge(set_dma, 16 * (N_SMALL + N_ROWS))

            def norm_T(b, par):
                pe.wait_ge(ln_out, 3 * (b + 1))
                for k, src in enumerate((xn[:, par], zt[:])):
                    for i in range(T):
                        ins = pe.transpose(ps[:, G0, (T * k + i) * P:(T * k + i + 1) * P], src[:, i], ident[:])
                ins.then_inc(xzT_out, 1)

            def proj(b, side, prev):
                pe.wait_ge(xnT_done, b + 1)
                prev()
                for k in range(2):
                    ins = mm(ps[:, G1, k * S:(k + 1) * S], wa[:, 2 * side + k], xnT[:], start=True, stop=True)
                ins.then_inc((rot_q_out, rot_k_out)[side], 1)

            def logits_T(b, par):
                pe.wait_ge(sq_done, b + 1)
                mm(ps[0:E, G0, 0:S], simn[:, 0], n1T[:, par], start=True, stop=True)
                mm(ps[32:32 + E, G0, 0:S], ones_e[:], sqT[:, 0:S], start=True, stop=True).then_inc(lgT_out, 1)

            def logits(b):
                pe.wait_ge(lgT_done, 2 * (b + 1))
                for i in range(T):
                    ins = pe.transpose(ps[:, G0, i * P:(i + 1) * P], lgT[:, i * P:(i + 1) * P], ident[:])
                ins.then_inc(lg_out, 1)

            def proj_v(b):
                pe.wait_ge(rot_chain, ROT_LINKS * b + 3)
                for i in range(T):
                    ins = mm(ps[:, G1, i * D:(i + 1) * D], xnT[:, i * P:(i + 1) * P], wa[:, 4], start=True, stop=True)
                ins.then_inc(v_out, 1)

            def weights_T(b):
                pe.wait_ge(v_done, b + 1)
                pe.wait_ge(rw_out, 3 * (b + 1))
                for i in range(T):
                    ins = pe.transpose(ps[0:E, G1, i * P:(i + 1) * P], gt[:, 6, i], ident[:])
                ins.then_inc(rwT_out, 1)

            def unit1(b, par, k):
                G, i = divmod(k, 3)
                if k == 0:
                    pe.wait_ge(stack_in, 16 * 7 * (b + 1))
                if k >= 2:
                    pe.wait_ge(s1_read, UNITS * b + k - 1)
                else:
                    pe.wait_ge(s1_read, UNITS * b)
                bank = ps[:, S1[k % 2]]
                if i == 0:
                    mm(bank, identb[:], mask_qk[:].rearrange("p h t -> p (h t)"), start=True, stop=False,
                       skip_group_check=True)
                    for h in range(HG):
                        hh = HG * G + h
                        ins = mm(bank[:, h * P:(h + 1) * P], qst[0:KR, par, hh, 0:P], kst[0:KR, par, hh, 0:P],
                                 start=False, stop=True, skip_group_check=True)
                else:
                    mm(bank.rearrange("p (h t) -> p h t", h=2)[:, :, P:S], identb[:], mask_qk[:, 0:2],
                       start=True, stop=False, skip_group_check=True)
                    for h in range(2):
                        hh = HG * G + 2 * (i - 1) + h
                        ins = mm(bank[:, h * S:(h + 1) * S], qst[0:KR, par, hh, P:S], kst[0:KR, par, hh, :],
                                 start=False, stop=True, skip_group_check=True)
                ins.then_inc(s1_out, 1)

            def max_T(b, prev):
                pe.wait_ge(max_chain, (MAX_LINKS + 1) * (b + 1))
                prev()
                pv = ps[:, G1, 0:S // 2].bitcast(BF16)
                for i in range(T):
                    ins = pe.transpose(pv[:, i * P:(i + 1) * P], mpart[:, i], identb[:])
                ins.then_inc(mT_out, 1)

            def unit2(n, u, k):
                G, i = divmod(k, 3)
                if k == 0:
                    pe.wait_ge(max_in, 16 * (n + 1))
                pe.wait_ge(exp_done, UNITS * n + max(k - 1, 0))
                bank = ps[:, S2[k % 2]]
                if i < 2:
                    mm(bank.rearrange("p (h t) -> p h t", h=2)[:, :, 0:P], identb[:], mask_kq[:, 0:2],
                       start=True, stop=False, skip_group_check=True)
                    for h in range(2):
                        hh = HG * G + 2 * i + h
                        ins = mm(bank[:, h * S:(h + 1) * S], kst[0:KR, u, hh, 0:P], qst[0:KR, u, hh, :],
                                 start=False, stop=True, skip_group_check=True)
                else:
                    mm(bank, identb[:], mask_kq[:].rearrange("p h t -> p (h t)"), start=True, stop=False,
                       skip_group_check=True)
                    for h in range(HG):
                        hh = HG * G + h
                        ins = mm(bank[:, h * P:(h + 1) * P], kst[0:KR, u, hh, P:S], qst[0:KR, u, hh, P:S],
                                 start=False, stop=True, skip_group_check=True)
                ins.then_inc(s2_out, 1)

            def pv(n, u, G):
                pe.wait_ge(exp_done, UNITS * n + 3 * (G + 1))
                pe.wait_ge(ov_done, NG * n + G)
                if G == 0:
                    pe.wait_ge(v_done, n + 1)
                for h in range(HG):
                    mm(ps[32 * h:32 * h + 32, PVB, 0:S], vst[:, u, 0, HG * G + h],
                       pr[:, G % 2, h // 2, (h % 2) * S:(h % 2 + 1) * S], start=True, stop=False,
                       skip_group_check=True)
                for h in range(HG):
                    ins = mm(ps[32 * h:32 * h + 32, PVB, P:S], vst[:, u, 1, HG * G + h],
                             pr[:, G % 2, 2, h * P:(h + 1) * P], start=False, stop=True, skip_group_check=True)
                ins.then_inc(pv_out, 1)

            def out_T(n, G, prev):
                pe.wait_ge(ov_done, NG * n + G + 1)
                prev()
                for i in range(T):
                    ins = pe.transpose(ps[:, G0, i * P:(i + 1) * P], ov[:, G % 2, i * P:(i + 1) * P], ident[:])
                ins.then_inc(ot_out, 1)

            def qk(n, e):
                if e == 0:
                    pe.wait_ge(n1s_done, n + 1)
                    pe.wait_ge(ve_done, n)
                mm(ps[:, QKB, 0:S], wq[:, e], n1s[:, e], start=(e == 0), stop=(e == E - 1), skip_group_check=True)
                ins = mm(ps[:, QKB, S:2 * S], wk[:, e], n1s[:, e], start=False, stop=(e == E - 1),
                         skip_group_check=True)
                if e == E - 1:
                    ins.then_inc(qk_out, 1)

            def ve(n, e):
                if e == 0:
                    pe.wait_ge(qkT_done, 2 * (n + 1))
                for i in range(T):
                    ins = mm(ps[:, QKB, i * D:(i + 1) * D], n1s[:, e, i * P:(i + 1) * P], wv[:, e],
                             start=(e == 0 and i == 0), stop=(e == E - 1), skip_group_check=True)
                if e == E - 1:
                    ins.then_inc(ve_out, 1)

            def soft_scores(n, last):
                pe.wait_ge(qkT_done, 2 * (n + 1))
                pe.wait_ge(rwT_done, min(n + 2, NB) if isinstance(n, int) else n + 2)
                b = ps[:, G1]
                mm(b.rearrange("p (a t) -> p a t", a=2)[:, :, 0:P], identb[:], mask_qk[:, 0:2], start=True,
                   stop=False, skip_group_check=True)
                mm(b[:, 0:P], qT[:, 0:P], kT[:, 0:P], start=False, stop=True, skip_group_check=True)
                mm(b[:, P:3 * P], qT[:, P:S], kT[:], start=False, stop=True, skip_group_check=True
                   ).then_inc(ss_out, 1)

            def soft_T(n):
                pe.wait_ge(snorm_done, n + 1)
                for k in range(3):
                    ins = pe.transpose(ps[:, G1, k * P:(k + 1) * P], sp[:, k * P:(k + 1) * P], ident[:])
                ins.then_inc(spT_out, 1)

            def soft_av(n):
                pe.wait_ge(spT_done, n + 1)
                pe.wait_ge(ve_done, n + 1)
                mm(ps[:, G1, 0:S], vs[:, 0], spT[:, 0:S], start=True, stop=False, skip_group_check=True)
                mm(ps[:, G1, P:S], vs[:, 1], spT[:, S:3 * P], start=False, stop=True, skip_group_check=True
                   ).then_inc(av_out, 1)

            def oe(n, e):
                if e == 0:
                    pe.wait_ge(ats_done, n + 1)
                for i in range(T):
                    ins = mm(ps[:, G1, i * D:(i + 1) * D], ats[:, e, i * P:(i + 1) * P], wop[:, e],
                             start=(e == 0 and i == 0), stop=(e == E - 1), skip_group_check=True)
                if e == E - 1:
                    ins.then_inc(oe_out, 1)

            def att_T(n):
                pe.wait_ge(ot_read, 2 * NG * (n + 1))
                for i in range(T):
                    ins = pe.transpose(ps[:, G0, i * P:(i + 1) * P], att[:, i], ident[:])
                ins.then_inc(attT_out, 1)

            def att_out(n):
                pe.wait_ge(attT_done, n + 1)
                for i in range(T):
                    ins = mm(ps[:, G0, i * D:(i + 1) * D], attT[:, i * P:(i + 1) * P], wo[:], start=True, stop=True)
                ins.then_inc(wo_out, 1)

            def step(n, u, last):
                f, pf = n + 1, 1 - u
                qk(n, 0)
                qk(n, 1)
                if not last:
                    pe.wait_ge(xa_done, n)
                    norm_T(f, pf)
                qk(n, 2)
                unit2(n, u, 0)
                if not last:
                    proj(f, 0, lambda: pe.wait_ge(mT_done, f))
                unit2(n, u, 1)
                qk(n, 3)
                if not last:
                    logits_T(f, pf)
                unit2(n, u, 2)
                if not last:
                    proj(f, 1, lambda: pe.wait_ge(rot_chain, ROT_LINKS * f + 1))
                qk(n, 4)
                if not last:
                    logits(f)
                    proj_v(f)
                unit2(n, u, 3)
                pv(n, u, 0)
                qk(n, 5)
                unit2(n, u, 4)
                out_T(n, 0, lambda: pe.wait_ge(lg_read, n + (1 if last else 2)))
                qk(n, 6)
                unit2(n, u, 5)
                unit2(n, u, 6)
                pv(n, u, 1)
                qk(n, 7)
                if not last:
                    weights_T(f)
                unit2(n, u, 7)
                out_T(n, 1, lambda: pe.wait_ge(ot_read, 2 * (NG * n + 1)))
                unit2(n, u, 8)
                ve(n, 0)
                ve(n, 1)
                soft_scores(n, last)
                if not last:
                    unit1(f, pf, 0)
                pv(n, u, 2)
                ve(n, 2)
                unit2(n, u, 9)
                out_T(n, 2, lambda: pe.wait_ge(ot_read, 2 * (NG * n + 2)))
                if not last:
                    unit1(f, pf, 1)
                ve(n, 3)
                ve(n, 4)
                unit2(n, u, 10)
                if not last:
                    unit1(f, pf, 2)
                soft_T(n)
                ve(n, 5)
                ve(n, 6)
                unit2(n, u, 11)
                if not last:
                    unit1(f, pf, 3)
                ve(n, 7)
                pv(n, u, 3)
                if not last:
                    unit1(f, pf, 4)
                out_T(n, 3, lambda: pe.wait_ge(ot_read, 2 * (NG * n + 3)))
                if not last:
                    unit1(f, pf, 5)
                soft_av(n)
                if not last:
                    unit1(f, pf, 6)
                att_T(n)
                if not last:
                    unit1(f, pf, 7)
                oe(n, 0)
                oe(n, 1)
                if not last:
                    unit1(f, pf, 8)
                oe(n, 2)
                oe(n, 3)
                att_out(n)
                if not last:
                    unit1(f, pf, 9)
                oe(n, 4)
                oe(n, 5)
                if not last:
                    unit1(f, pf, 10)
                oe(n, 6)
                oe(n, 7)
                if not last:
                    unit1(f, pf, 11)
                    max_T(f, lambda: pe.wait_ge(hs_done, f))

            norm_T(0, 0)
            proj(0, 0, lambda: None)
            logits_T(0, 0)
            proj(0, 1, lambda: pe.wait_ge(rot_chain, 1))
            logits(0)
            proj_v(0)
            weights_T(0)
            for k in range(UNITS):
                unit1(0, 0, k)
            max_T(0, lambda: pe.wait_ge(rwT_done, 1))
            step(0, 0, False)
            step(1, 1, False)
            with pe.Fori(1, NB // 2 - 1) as j:
                for u in range(2):
                    step(2 * j + u, u, False)
            step(NB - 2, 0, False)
            step(NB - 1, 1, True)

            def norm_T2(g):
                pe.wait_ge(ln2_out, TM * (g + 1))
                pe.wait_ge(lg2_read, g)
                for i in range(TM):
                    ins = pe.transpose(ps[:, G0, i * P:(i + 1) * P], z2[:, i], ident[:])
                ins.then_inc(zT2_out, 1)

            def logits_T2(g, par):
                pe.wait_ge(sq2_done, g + 1)
                pe.wait_ge(rwT2_done, g)
                mm(ps[0:E, G1], simn[:, 1], n2T[:, par], start=True, stop=True)
                mm(ps[32:32 + E, G1], ones_e[:], sqT[:], start=True, stop=True).then_inc(lgT2_out, 1)

            def logits2(g):
                pe.wait_ge(lgT2_done, 2 * (g + 1))
                for i in range(TM):
                    ins = pe.transpose(ps[:, G0, i * P:(i + 1) * P], lgT[:, i * P:(i + 1) * P], ident[:])
                ins.then_inc(lg2_out, 1)

            def weights_T2(g):
                pe.wait_ge(rw2_out, 3 * (g + 1))
                for i in range(TM):
                    ins = pe.transpose(ps[0:E, G1, i * P:(i + 1) * P], gt[:, 6, i], ident[:])
                ins.then_inc(rwT2_out, 1)

            def up(g, u, e):
                pe.wait_ge(n2T_done, g + 1)
                pe.wait_ge(gelu_done, E * g + max(e - 2, 0))
                mm(ps[:, UP[e % 3]], w1s[:, e], n2T[:, u], start=True, stop=True).then_inc(up_out, 1)

            def down(g, u, e):
                pe.wait_ge(hgs_done, E * g + e + 1)
                if e == 0:
                    pe.wait_ge(out_done, g if not isinstance(g, int) else max(g - 1, 0))
                for i in range(TM):
                    ins = mm(ps[:, MOE[u], i * D:(i + 1) * D], hgs[:, e % 2, i * P:(i + 1) * P], w2s[:, e],
                             start=(e == 0 and i == 0), stop=(e == E - 1), skip_group_check=True)
                ins.then_inc(moe_out, 1)

            def step2(g, u, last):
                up(g, u, 0)
                up(g, u, 1)
                for e in range(E):
                    down(g, u, e)
                    if e + 2 < E:
                        up(g, u, e + 2)
                    if not last and e == 0:
                        norm_T2(g + 1)
                    if not last and e == 1:
                        logits_T2(g + 1, 1 - u)
                    if not last and e == 2:
                        logits2(g + 1)
                    if not last and e == 6:
                        weights_T2(g + 1)

            norm_T2(0)
            logits_T2(0, 0)
            logits2(0)
            weights_T2(0)
            step2(0, 0, False)
            step2(1, 1, False)
            with pe.Fori(1, MS // 2 - 1) as j:
                for u in range(2):
                    step2(2 * j + u, u, False)
            step2(MS - 2, 0, False)
            step2(MS - 1, 1, True)


def kernel(L0_attn_x, L0_attn_Wqkv, L0_attn_Wo, L0_attn_log_xi, L0_attn_pi_gate_logit, L0_attn_e_gate_logit,
           L0_ffn_ln1_w, L0_ffn_ln1_b, L0_ffn_ln2_w, L0_ffn_ln2_b, L0_ffn_smha_sim, L0_ffn_smha_gates,
           L0_ffn_q_proj, L0_ffn_k_proj, L0_ffn_v_proj, L0_ffn_o_proj, L0_ffn_moe_sim, L0_ffn_moe_gates,
           L0_ffn_w1, L0_ffn_w2):
    import concourse.bacc as bacc
    from concourse.bass_utils import run_bass_kernel_spmd

    wqkv_t = np.ascontiguousarray(L0_attn_Wqkv).T.reshape(D, 3, D)
    swap = np.arange(D) ^ 1
    w_attn = np.stack([wqkv_t[:, 0], wqkv_t[:, 0][:, swap], wqkv_t[:, 1], wqkv_t[:, 1][:, swap], wqkv_t[:, 2]], 1)

    inv_freq = np.float32(np.pi) ** (np.float32(1.0) - np.arange(0, DH, 2, dtype=np.float32) / np.float32(DH))
    pos = np.arange(S, dtype=np.float32)
    pos_freq = pos[None, :] * inv_freq.astype(np.float32)[(np.arange(D) % DH) // 2][:, None]
    r = np.arange(P)
    arrays = {
        "x": L0_attn_x, "w_attn": w_attn, "w_o": np.ascontiguousarray(L0_attn_Wo).T,
        "log_xi": L0_attn_log_xi, "pi_logit": L0_attn_pi_gate_logit, "e_logit": L0_attn_e_gate_logit,
        "ln1_w": np.reshape(L0_ffn_ln1_w, (D, 1)), "ln1_b": np.reshape(L0_ffn_ln1_b, (D, 1)),
        "ln2_w": np.reshape(L0_ffn_ln2_w, (D, 1)), "ln2_b": np.reshape(L0_ffn_ln2_b, (D, 1)),
        "sim1": L0_ffn_smha_sim, "gates1": L0_ffn_smha_gates,
        "q_proj": L0_ffn_q_proj, "k_proj": L0_ffn_k_proj, "v_proj": L0_ffn_v_proj, "o_proj": L0_ffn_o_proj,
        "sim2": L0_ffn_moe_sim, "gates2": L0_ffn_moe_gates, "w1": L0_ffn_w1, "w2": L0_ffn_w2,
        "c_ident": np.eye(P, dtype=np.float32),
        "c_mask_qk": np.where(r[None, :] > r[:, None], -BIG, 0.0).astype(np.float32),
        "c_mask_kq": np.where(r[:, None] > r[None, :], -BIG, 0.0).astype(np.float32),
        "c_pos_freq": pos_freq.astype(np.float32),
        "c_sin_sign": np.where(r % 2 == 0, -1.0, 1.0).astype(np.float32)[:, None],
        "c_pos": np.broadcast_to(pos, (H, S)).astype(np.float32),
        "c_rank": np.broadcast_to(np.arange(E, 0, -1), (P, E)).astype(np.float32),
    }
    arrays = {f"in_{k}": np.ascontiguousarray(v) for k, v in arrays.items()}
    nc = bacc.Bacc("TRN2", target_bir_lowering=False, num_devices=1)
    args = [nc.dram_tensor(k, v.shape, mybir.dt.from_np(v.dtype), kind="ExternalInput").ap() for k, v in arrays.items()]
    out = nc.dram_tensor("out", (NB, S, D), F32, kind="ExternalOutput").ap()
    build(nc, *args, out)
    r = run_bass_kernel_spmd(nc, [arrays], core_ids=[0])
    return r.results[0]["out"]
```

```python
from contextlib import ExitStack

import numpy as np

import concourse.bass as bass
from concourse import mybir

F32 = mybir.dt.float32
BF16 = mybir.dt.bfloat16
ALU = mybir.AluOpType
ACT = mybir.ActivationFunctionType
AX_X = mybir.AxisListType.X

NB = 32
S = 256
D = 128
H = 16
DH = D // H
P = 128
T = S // P
E = 8
NG = 4
HG = H // NG
UNITS = 3 * NG
EPS = 1e-5
NORM2 = 1e-24
BIG = 1e30
TM = 4
MS = NB * T // TM
W2 = TM * P

R_BIAS_J = 0
R_BIAS_I = 3
R_PARTS = 8
R_MAX = R_PARTS + 6 * DH
Q_SLOTS = ((0, 3, 0), (3, 2, 1), (5, 1, 2))
K_SLOTS = ((0, 3, 0), (3, 2, 0), (5, 1, 0))
KR = P

LN_LINKS = 2 + 10
ROT_LINKS = 7
GATE_LINKS = 21 + 10
MAX_LINKS = 3
ROW_MAX_AT = (3, 5, 8, 10, 15, 17, 19, 21)


class Chain:

    def __init__(self, eng, sem, done_before, per, beside=None):
        self.eng, self.sem, self.base, self.per, self.k = eng, sem, done_before * per, per, 0
        self.beside = beside or (lambda k: None)

    def add(self, ins):
        ins.then_inc(self.sem, 1)
        self.k += 1

    def link(self, ins):
        self.add(ins)
        self.beside(self.k)
        self.wait()

    def wait(self):
        self.eng.wait_ge(self.sem, self.base + self.k)

    def close(self):
        assert self.k == self.per, (self.k, self.per)


RSQRT_LINKS = 10


def rsqrt(dve, c, y, v, t):
    c.link(dve.tensor_scalar(y.bitcast(mybir.dt.int32), v.bitcast(mybir.dt.int32), -0.5, float(0x5F3759DF),
                             ALU.mult, ALU.add))
    for _ in range(3):
        c.link(dve.scalar_tensor_tensor(t, y, -0.5, y, ALU.mult, ALU.mult))
        c.link(dve.tensor_tensor(t, t, v, ALU.mult))
        c.link(dve.scalar_tensor_tensor(y, t, 1.5, y, ALU.add, ALU.mult))


def build(nc, x, w_attn, w_o, log_xi, pi_logit, e_logit, ln1_w, ln1_b, ln2_w, ln2_b, sim1, gates1,
          q_proj, k_proj, v_proj, o_proj, sim2, gates2, w1, w2, c_ident, c_mask_qk, c_mask_kq, c_pos_freq,
          c_sin_sign, c_pos, c_rank, out):
    scr_parts = nc.dram_tensor("scr_parts", (2, 3, 2, DH, H, S), BF16, kind="Internal").ap()
    scr_rw = nc.dram_tensor("scr_rw", (2, E, S), F32, kind="Internal").ap()
    scr_rw2 = nc.dram_tensor("scr_rw2", (2, E, W2), F32, kind="Internal").ap()

    scr_base = nc.dram_tensor("scr_base", (NB, P, T, D), F32, kind="Internal").ap()

    with ExitStack() as ctx:
        def sb(name, shape, dt=F32):
            return ctx.enter_context(nc.sbuf_tensor(name, shape, dt))

        def sem(name):
            return ctx.enter_context(nc.semaphore(name))

        ident = sb("ident", [P, P])
        identb = sb("identb", [P, P], BF16)
        mask_in = sb("mask_in", [P, 2, P])
        mask_qk = sb("mask_qk", [P, HG, P], BF16)
        mask_kq = sb("mask_kq", [P, HG, P], BF16)
        wa = sb("wa", [P, 5, D])
        wo = sb("wo", [P, D])
        wq = sb("wq", [P, E, D])
        wk = sb("wk", [P, E, D])
        wv = sb("wv", [P, E, D])
        wop = sb("wop", [P, E, D])
        w1s = sb("w1s", [P, E, D])
        w2s = sb("w2s", [P, E, D])
        lnp = sb("lnp", [P, 4])
        simn = sb("simn", [P, 2, E])
        sg = sb("sg", [P, 2, E])
        rank = sb("rank", [P, E])
        ones_e = sb("ones_e", [P, E])
        ones_p = sb("ones_p", [P, P])
        cs = sb("cs", [P, 2, 2, S])
        theta = sb("theta", [P, S])
        trn = sb("trn", [P, 2, S])
        red = sb("red", [P, 2, S])
        sin_sign = sb("sin_sign", [P, 1])
        pig = sb("pig", [P, 1])
        bias_in = sb("bias_in", [H, 2])
        cpos = sb("cpos", [H, S])
        cb = sb("cb", [H, 2, S])
        cbp = sb("cbp", [H, 2, 3, S], BF16)
        ones_b = sb("ones_b", [3, 1, S], BF16)
        zeros_b = sb("zeros_b", [3, 1, S], BF16)
        sims = sb("sims", [P, 2, E])

        xt = sb("xt", [P, 2, T, D])
        xr = sb("xr", [P, 2, T, D])
        xn = sb("xn", [P, T, D])
        zt = sb("zt", [P, T, D])
        bst = sb("bst", [P, 2, TM, 6])
        bmv = sb("bmv", [P, 2, TM, 2])
        rstd = sb("rstd", [P, 2, TM])
        vstd = sb("vstd", [P, 2, TM])
        xnT = sb("xnT", [P, S])
        n1T = sb("n1T", [P, 2, S])
        sqT = sb("sqT", [P, W2])
        lgT = sb("lgT", [P, W2])
        gt = sb("gt", [P, 10, TM, E])
        gs = sb("gs", [P, 8, TM])
        rwT = sb("rwT", [E, W2])
        rep = sb("rep", [P, 2, E, S])
        n1s = sb("n1s", [P, E, S])
        ats = sb("ats", [P, E, S])
        rott = sb("rott", [P, 2, 2, S])
        rot = sb("rot", [P, 2, S])
        rres = sb("rres", [P, 2, S])
        parts = sb("parts", [P, 3, 2, S], BF16)
        qst = sb("qst", [P, 2, H, S], BF16)
        kst = sb("kst", [P, 2, H, S], BF16)
        vst = sb("vst", [P, 2, T, H, 32])
        mx = sb("mx", [P, T, H])
        mres = sb("mres", [P, T, H])
        mpart = sb("mpart", [P, T, P], BF16)
        mT = sb("mT", [3 * H, S], BF16)
        pr = sb("pr", [P, 2, 3, 512])
        ov = sb("ov", [P, 2, S])
        rden = sb("rden", [P, T, HG])
        att = sb("att", [P, T, D])
        attT = sb("attT", [P, S])
        avT = sb("avT", [P, S])
        qT = sb("qT", [P, S])
        kT = sb("kT", [P, S])
        vs = sb("vs", [P, T, D])
        smx = sb("smx", [P, 4, T])
        sp = sb("sp", [P, 3 * P])
        spT = sb("spT", [P, 3 * P])
        hs = sb("hs", [P, NB * T, D])
        bs = sb("bs", [P, 2, T, D])
        xa = sb("xa", [P, 2, T, D])

        prf = pr[:].rearrange("p a i t -> p (a i t)")
        bt = prf[:, 0:2 * TM * D].rearrange("p (a i c) -> p a i c", a=2, i=TM)
        z2 = prf[:, 2 * TM * D:3 * TM * D].rearrange("p (i c) -> p i c", i=TM)
        rep2 = [v[:].rearrange("p a h t -> p (a h t)").bitcast(F32).rearrange("p (e t) -> p e t", e=E)
                for v in (qst, kst)]
        n1f, atf = (v[:].rearrange("p e t -> p (e t)") for v in (n1s, ats))
        n2T = n1f[:, 0:2 * W2].rearrange("p (a t) -> p a t", a=2)
        hg = n1f[:, 2 * W2:4 * W2].rearrange("p (a t) -> p a t", a=2)
        hgs = atf[:, 0:2 * W2].rearrange("p (a t) -> p a t", a=2)
        ot = atf[:, 2 * W2:4 * W2].rearrange("p (a i c) -> p a i c", a=2, i=TM)

        ps = ctx.enter_context(nc.psum_tensor("ps", [P, 8, 512], F32))
        S1, S2, PVB, QKB, G0, G1 = (0, 1), (2, 3), 4, 5, 6, 7

        ld_const, ld_w = sem("ld_const"), sem("ld_w")
        set_dve, set_act, set_pe, set_pool, set_dma = (
            sem("set_dve"), sem("set_act"), sem("set_pe"), sem("set_pool"), sem("set_dma"))
        x_in = sem("x_in")
        ln_chain = sem("ln_chain")
        ln_out = sem("ln_out")
        xzT_out = sem("xzT_out")
        xr_in = sem("xr_in")
        keep_done = sem("keep_done")
        zp_done = sem("zp_done")
        av_done = sem("av_done")
        xnT_done = sem("xnT_done")
        n1T_done = sem("n1T_done")
        sq_done = sem("sq_done")
        lgT_out = sem("lgT_out")
        lgT_done = sem("lgT_done")
        lg_out = sem("lg_out")
        lg_read = sem("lg_read")
        gate_chain = sem("gate_chain")
        tanh_in = sem("tanh_in")
        tanh_out = sem("tanh_out")
        rw_out = sem("rw_out")
        rwT_out = sem("rwT_out")
        rwT_done = sem("rwT_done")
        rw_stored = sem("rw_stored")
        rep_in = sem("rep_in")
        n1s_done = sem("n1s_done")
        rot_q_out = sem("rot_q_out")
        rot_k_out = sem("rot_k_out")
        rot_chain = sem("rot_chain")
        parts_out = sem("parts_out")
        parts_stored = sem("parts_stored")
        stack_in = sem("stack_in")
        v_out = sem("v_out")
        v_done = sem("v_done")
        s1_out = sem("s1_out")
        s1_read = sem("s1_read")
        max_chain = sem("max_chain")
        mT_out = sem("mT_out")
        mT_done = sem("mT_done")
        max_in = sem("max_in")
        s2_out = sem("s2_out")
        exp_done = sem("exp_done")
        pv_out = sem("pv_out")
        ov_done = sem("ov_done")
        ot_out = sem("ot_out")
        ot_read = sem("ot_read")
        attT_out = sem("attT_out")
        attT_done = sem("attT_done")
        wo_out = sem("wo_out")
        xa_done = sem("xa_done")
        qk_out = sem("qk_out")
        qkT_done = sem("qkT_done")
        ve_out = sem("ve_out")
        ve_done = sem("ve_done")
        ss_out = sem("ss_out")
        smax_done = sem("smax_done")
        sexp_done = sem("sexp_done")
        snorm_chain = sem("snorm_chain")
        snorm_done = sem("snorm_done")
        spT_out = sem("spT_out")
        spT_done = sem("spT_done")
        av_out = sem("av_out")
        ats_done = sem("ats_done")
        oe_out = sem("oe_out")
        hs_done = sem("hs_done")
        base_done = sem("base_done")
        base_stored = sem("base_stored")
        base_in = sem("base_in")
        ln2_chain = sem("ln2_chain")
        ln2_out = sem("ln2_out")
        zT2_out = sem("zT2_out")
        n2T_done = sem("n2T_done")
        sq2_done = sem("sq2_done")
        lgT2_out = sem("lgT2_out")
        lgT2_done = sem("lgT2_done")
        lg2_out = sem("lg2_out")
        lg2_read = sem("lg2_read")
        gate2_chain = sem("gate2_chain")
        tanh2_in = sem("tanh2_in")
        tanh2_out = sem("tanh2_out")
        rw2_out = sem("rw2_out")
        rwT2_out = sem("rwT2_out")
        rwT2_done = sem("rwT2_done")
        rw2_stored = sem("rw2_stored")
        rep2_in = sem("rep2_in")
        up_out = sem("up_out")
        hgs2_done = sem("hgs2_done")
        gelu_done = sem("gelu_done")
        hgs_done = sem("hgs_done")
        moe_out = sem("moe_out")
        out_done = sem("out_done")
        out_stored = sem("out_stored")

        block = ctx.enter_context(nc.Block())
        N_CONST, N_W, N_SMALL = 13, 8, 5
        N_ROWS = 18
        SIN_READY, N_SET_DVE = 18, 55
        UP, MOE = (0, 1, 2), (3, 4)

        @block.sync
        def _(sp_):
            x_v = x.rearrange("b (i p) c -> b p i c", p=P)

            sp_.dma_start(xt[:, 0], x_v[0]).then_inc(x_in, 16)
            sp_.dma_start(xt[:, 1], x_v[1]).then_inc(x_in, 16)
            for dst, src in ((ident[:], c_ident), (mask_in[:, 0], c_mask_qk), (mask_in[:, 1], c_mask_kq),
                             (theta[:], c_pos_freq), (sin_sign[:], c_sin_sign), (cpos[:], c_pos),
                             (rank[:], c_rank), (lnp[:, 0:1], ln1_w), (lnp[:, 1:2], ln1_b),
                             (lnp[:, 2:3], ln2_w), (lnp[:, 3:4], ln2_b),
                             (sims[:, 0], sim1), (sims[:, 1], sim2)):
                sp_.dma_start(dst, src).then_inc(ld_const, 16)
            for dst, src in ((wa[:], w_attn), (wo[:], w_o), (wq[:], q_proj), (wk[:], k_proj),
                             (wv[:], v_proj), (wop[:], o_proj), (w1s[:], w1), (w2s[:], w2)):
                v = src.rearrange("e c h -> c e h") if len(src.shape) == 3 and src.shape[0] == E else src
                sp_.dma_start(dst, v).then_inc(ld_w, 16)
            sp_.wait_ge(set_pool, 2)
            sp_.wait_ge(set_dve, N_SET_DVE)
            for par in range(2):
                for part in range(3):
                    sp_.dma_start(kst[R_BIAS_J + part:R_BIAS_J + part + 1, par], cbp[:, 0, part]).then_inc(set_dma, 16)
                    sp_.dma_start(qst[R_BIAS_I + part:R_BIAS_I + part + 1, par], cbp[:, 1, part]).then_inc(set_dma, 16)
                sp_.dma_start(qst[R_BIAS_J:R_BIAS_J + 3, par], ones_b[:].broadcast_to((3, H, S))).then_inc(set_dma, 16)
                sp_.dma_start(kst[R_BIAS_I:R_BIAS_I + 3, par], ones_b[:].broadcast_to((3, H, S))).then_inc(set_dma, 16)
                sp_.dma_start(kst[R_MAX:R_MAX + 3, par], ones_b[:].broadcast_to((3, H, S))).then_inc(set_dma, 16)

            def stacks(b, par):
                sp_.wait_ge(parts_out, 1 + b)
                sp_.dma_start(scr_parts[par].rearrange("p s d h t -> (d h) (p s) t"),
                              parts[:].rearrange("q p s t -> q (p s) t")).then_inc(parts_stored, 16)
                sp_.wait_ge(parts_stored, 16 * (b + 1))
                for side, dst, slots in ((0, qst, Q_SLOTS), (1, kst, K_SLOTS)):
                    v = scr_parts[par, :, side].rearrange("p d h t -> p d (h t)")
                    for first, n, part in slots:
                        rows = dst[R_PARTS + DH * first:R_PARTS + DH * (first + n), par].rearrange("p h t -> p (h t)")
                        src = v[part:part + 1].broadcast_to((n, DH, H * S)) if side == 0 and n > 1 else (
                            v[part:part + n])
                        sp_.dma_start(rows, src).then_inc(stack_in, 16)
                sp_.dma_start(qst[R_MAX:R_MAX + 3, par], zeros_b[:].broadcast_to((3, H, S))).then_inc(stack_in, 16)

            def spread_weights(b, par):
                sp_.wait_ge(rwT_done, b + 1)
                sp_.dma_start(scr_rw[par], rwT[:, 0:S]).then_inc(rw_stored, 16)
                sp_.wait_ge(rw_stored, 16 * (b + 1))
                sp_.dma_start(rep[:, par].rearrange("p e t -> p (e t)"),
                              scr_rw[par].rearrange("(o e) t -> o (e t)", o=1).broadcast_to((P, E * S))
                              ).then_inc(rep_in, 16)

            def put_max(b, par):
                sp_.wait_ge(mT_done, b + 1)
                sp_.dma_start(qst[R_MAX:R_MAX + 3, par], mT[:]).then_inc(max_in, 16)

            def load_x(b, par, dst, arrived):
                src = x_v[b] if isinstance(b, int) else x_v[bass.ds(b, 1)].rearrange("o p i c -> p (o i) c")
                sp_.dma_start(dst[:, par], src).then_inc(arrived, 16)

            def store_base(n, u):
                sp_.wait_ge(base_done, n + 1)
                dst = scr_base[n] if isinstance(n, int) else scr_base[bass.ds(n, 1)].rearrange("o p i c -> p (o i) c")
                sp_.dma_start(dst, bs[:, u]).then_inc(base_stored, 16)

            def step(n, u, n_x):
                sp_.wait_ge(base_done, n)
                if n_x == 2:
                    load_x(n + 2, u, xt, x_in)
                load_x(n, u, xr, xr_in)
                if n_x:
                    stacks(n + 1, 1 - u)
                    spread_weights(n + 1, 1 - u)
                    put_max(n + 1, 1 - u)
                store_base(n, u)

            stacks(0, 0)
            spread_weights(0, 0)
            put_max(0, 0)
            step(0, 0, 2)
            step(1, 1, 2)
            with sp_.Fori(1, NB // 2 - 1) as j:
                for u in range(2):
                    step(2 * j + u, u, 2)
            step(NB - 2, 0, 1)
            step(NB - 1, 1, 0)

            def spread2(g, par):
                sp_.wait_ge(rwT2_done, g + 1)
                sp_.dma_start(scr_rw2[par], rwT[:]).then_inc(rw2_stored, 16)
                sp_.wait_ge(rw2_stored, 16 * (g + 1))
                sp_.dma_start(rep2[par].rearrange("p e t -> p (e t)"),
                              scr_rw2[par].rearrange("(o e) t -> o (e t)", o=1).broadcast_to((P, E * W2))
                              ).then_inc(rep2_in, 16)

            o_v = out.rearrange("b (i p) c -> p (b i) c", p=P)

            base_v = scr_base.rearrange("b p i c -> p b (i c)")

            def load_base(g, par):
                v = base_v[:, 2 * g:2 * g + 2] if isinstance(g, int) else base_v[:, bass.ds(g * 2, 2)]
                sp_.dma_start(bt[:, par].rearrange("p (b i) c -> p b (i c)", b=2), v).then_inc(base_in, 16)

            def store_out(g, u):
                dst = o_v[:, TM * g:TM * g + TM] if isinstance(g, int) else o_v[:, bass.ds(g * TM, TM)]
                sp_.dma_start(dst, ot[:, u]).then_inc(out_stored, 16)

            def step2(g, u, n_x):
                sp_.wait_ge(out_done, g)
                if not isinstance(g, int) or g > 0:
                    store_out(g - 1, 1 - u)
                if n_x:
                    load_base(g + 1, 1 - u)
                    spread2(g + 1, 1 - u)

            sp_.wait_ge(base_stored, 16 * NB)
            load_base(0, 0)
            spread2(0, 0)
            step2(0, 0, 2)
            step2(1, 1, 2)
            with sp_.Fori(1, MS // 2 - 1) as j:
                for u in range(2):
                    step2(2 * j + u, u, 2)
            step2(MS - 2, 0, 1)
            step2(MS - 1, 1, 0)
            sp_.wait_ge(out_done, MS)
            store_out(MS - 1, 1)
            sp_.wait_ge(out_stored, 16 * MS)

        @block.gpsimd
        def _(pool):
            pool.memset(qst[:], 0.0).then_inc(set_pool, 1)
            pool.memset(kst[:], 0.0).then_inc(set_pool, 1)

            def scale(b, par):
                pool.wait_ge(rep_in, 16 * (b + 1))
                pool.wait_ge(n1T_done, b + 1)
                pool.wait_ge(ve_out, b)
                pool.tensor_tensor(n1s[:], rep[:, par], n1T[:, par:par + 1, :].broadcast_to((P, E, S)),
                                   ALU.mult).then_inc(n1s_done, 1)

            def second_norm(b):
                pool.wait_ge(ln_chain, 2 * LN_LINKS * (b + 1))
                pool.wait_ge(xzT_out, b)
                pool.tensor_tensor(zt[:], xn[:], bmv[:, 1, 0:T, 0:1].broadcast_to((P, T, D)),
                                   ALU.subtract).then_inc(zp_done, 1)
                pool.wait_ge(zp_done, 2 * b + 1)
                pool.tensor_tensor(zt[:], zt[:],
                                   rstd[:, 1, 0:T].rearrange("p (i o) -> p i o", o=1).broadcast_to((P, T, D)),
                                   ALU.mult).then_inc(zp_done, 1)
                hv = hs[:, T * b:T * b + T] if isinstance(b, int) else hs[:, bass.ds(b * T, T)]
                pool.tensor_copy(hv, xn[:]).then_inc(keep_done, 1)

            def step(n, u, n_x):
                if n_x:
                    scale(n + 1, 1 - u)
                if n_x == 2:
                    second_norm(n + 2)

            second_norm(0)
            scale(0, 0)
            second_norm(1)
            step(0, 0, 2)
            step(1, 1, 2)
            with pool.Fori(1, NB // 2 - 1) as j:
                for u in range(2):
                    step(2 * j + u, u, 2)
            step(NB - 2, 0, 1)
            step(NB - 1, 1, 0)

            def scale_gelu(g, e, par):
                pool.wait_ge(gelu_done, E * g + e + 1)
                pool.wait_ge(rep2_in, 16 * (g + 1))
                pool.wait_ge(moe_out, E * g + max(e - 1, 0))
                pool.tensor_tensor(hgs[:, 1], hg[:, 1], rep2[par][:, e], ALU.mult).then_inc(hgs2_done, 1)

            def norm2(g):
                pool.wait_ge(ln2_chain, LN_LINKS * (g + 1))
                pool.wait_ge(zT2_out, g)
                h = hs[:, TM * g:TM * g + TM] if isinstance(g, int) else hs[:, bass.ds(g * TM, TM)]
                pool.tensor_tensor(z2, h, bmv[:, 0, :, 0:1].broadcast_to((P, TM, D)), ALU.subtract
                                   ).then_inc(ln2_out, 1)
                pool.wait_ge(ln2_out, 2 * g + 1)
                pool.tensor_tensor(z2, z2, rstd[:, 0].rearrange("p (i o) -> p i o", o=1).broadcast_to((P, TM, D)),
                                   ALU.mult).then_inc(ln2_out, 1)

            def step2(g, u, n_x):
                for e in range(1, E, 2):
                    scale_gelu(g, e, u)
                    if e == 5 and n_x == 2:
                        norm2(g + 2)

            norm2(0)
            norm2(1)
            step2(0, 0, 2)
            step2(1, 1, 2)
            with pool.Fori(1, MS // 2 - 1) as j:
                for u in range(2):
                    step2(2 * j + u, u, 2)
            step2(MS - 2, 0, 1)
            step2(MS - 1, 1, 0)

        @block.scalar
        def _(act):
            def col(v, n):
                return v.rearrange("(p o) -> p o", o=1)
            act.dma_start(pig[:], pi_logit.rearrange("(o h) -> o h", o=1).broadcast_to((DH, H))
                          ).then_inc(set_dma, 16)
            act.dma_start(bias_in[:, 0:1], col(log_xi, H)).then_inc(set_dma, 16)
            act.dma_start(bias_in[:, 1:2], col(e_logit, H)).then_inc(set_dma, 16)
            act.dma_start(sg[:, 0], gates1.rearrange("(o e) -> o e", o=1).broadcast_to((P, E))).then_inc(set_dma, 16)
            act.dma_start(sg[:, 1], gates2.rearrange("(o e) -> o e", o=1).broadcast_to((P, E))).then_inc(set_dma, 16)
            act.wait_ge(set_dma, 16 * N_SMALL)
            act.activation(pig[:], pig[:], ACT.Tanh, scale=0.5).then_inc(set_act, 1)
            act.activation(sg[:], sg[:], ACT.Tanh, scale=0.5).then_inc(set_act, 1)
            act.activation(bias_in[:, 1:2], bias_in[:, 1:2], ACT.Tanh, scale=0.5).then_inc(set_act, 1)
            act.activation(bias_in[:, 0:1], bias_in[:, 0:1], ACT.Exp, scale=-1.0).then_inc(set_act, 1)
            act.wait_ge(set_dve, SIN_READY)
            act.activation(red[:], red[:], ACT.Sin).then_inc(set_act, 1)

            def evac_norm(b, par):
                act.wait_ge(xzT_out, b + 1)
                act.activation(xnT[:], ps[:, G0, 0:S], ACT.Copy).then_inc(xnT_done, 1)
                act.activation(n1T[:, par], ps[:, G0, S:2 * S], ACT.Identity, bias=lnp[:, 1:2],
                               scale=lnp[:, 0:1]).then_inc(n1T_done, 1)
                act.wait_ge(n1T_done, b + 1)
                act.activation(sqT[:, 0:S], n1T[:, par], ACT.Square).then_inc(sq_done, 1)

            def evac_logits(b):
                act.wait_ge(lgT_out, b + 1)
                act.activation(lgT[0:E, 0:S], ps[0:E, G0, 0:S], ACT.Copy).then_inc(lgT_done, 1)
                act.activation(lgT[32:32 + E, 0:S], ps[32:32 + E, G0, 0:S], ACT.Copy).then_inc(lgT_done, 1)

            def evac_v(b, par):
                act.wait_ge(v_out, b + 1)
                act.activation(vst[:, par, :, :, 0:DH],
                               ps[:, G1, 0:T * D].rearrange("p (i h d) -> p i h d", i=T, d=DH),
                               ACT.Copy).then_inc(v_done, 1)

            def gate_tanh(b):
                act.wait_ge(tanh_in, b + 1)
                act.activation(gt[:, 9, 0:T], gt[:, 1, 0:T], ACT.Tanh, scale=0.5).then_inc(tanh_out, 1)

            def evac_weights(b):
                act.wait_ge(rwT_out, b + 1)
                act.wait_ge(rw_stored, 16 * b)
                act.activation(rwT[:, 0:S], ps[0:E, G1, 0:S], ACT.Copy).then_inc(rwT_done, 1)

            def evac_max(b):
                act.wait_ge(mT_out, b + 1)
                act.wait_ge(max_in, 16 * b)
                act.activation(mT[:], ps[0:3 * H, S1[0], 0:S // 2].bitcast(BF16), ACT.Copy).then_inc(mT_done, 1)

            def exps(n, k):
                G, i = divmod(k, 3)
                act.wait_ge(s2_out, UNITS * n + k + 1)
                if i == 0:
                    act.wait_ge(pv_out, NG * n + max(G - 1, 0))
                act.activation(pr[:, G % 2, i], ps[:, S2[k % 2]], ACT.Exp).then_inc(exp_done, 1)

            def evac_pv(n, G):
                act.wait_ge(pv_out, NG * n + G + 1)
                act.wait_ge(ot_out, NG * n + max(G - 1, 0))
                act.activation(ov[:, G % 2], ps[:, PVB, 0:S], ACT.Copy).then_inc(ov_done, 1)

            def evac_qk(n):
                act.wait_ge(qk_out, n + 1)
                act.activation(qT[:], ps[:, QKB, 0:S], ACT.Copy, scale=D ** -0.5).then_inc(qkT_done, 1)
                act.activation(kT[:], ps[:, QKB, S:2 * S], ACT.Copy).then_inc(qkT_done, 1)

            def soft_exp(n):
                act.wait_ge(smax_done, 2 * n + 2)
                act.activation(sp[:, 0:P], ps[:, G1, 0:P], ACT.Exp, bias=smx[:, 1, 0:1],
                               accum_out=smx[:, 2, 0:1]).then_inc(sexp_done, 1)
                act.activation(sp[:, P:3 * P], ps[:, G1, P:3 * P], ACT.Exp, bias=smx[:, 1, 1:2],
                               accum_out=smx[:, 2, 1:2]).then_inc(sexp_done, 1)

            def evac_soft(n):
                act.wait_ge(spT_out, n + 1)
                act.activation(spT[:], ps[:, G1, 0:3 * P], ACT.Copy).then_inc(spT_done, 1)

            def evac_ve(n):
                act.wait_ge(ve_out, n + 1)
                act.activation(vs[:], ps[:, QKB, 0:T * D].rearrange("p (i c) -> p i c", i=T),
                               ACT.Copy).then_inc(ve_done, 1)

            def evac_att(n):
                act.wait_ge(attT_out, n + 1)
                act.activation(attT[:], ps[:, G0, 0:S], ACT.Copy).then_inc(attT_done, 1)

            def evac_av(n):
                act.wait_ge(av_out, n + 1)
                act.activation(avT[:], ps[:, G1, 0:S], ACT.Copy).then_inc(av_done, 1)

            def step(n, u, n_x):
                f, pf = n + 1, 1 - u
                if n_x:
                    evac_norm(f, pf)
                exps(n, 0)
                exps(n, 1)
                if n_x:
                    evac_logits(f)
                exps(n, 2)
                if n_x:
                    evac_v(f, pf)
                exps(n, 3)
                evac_pv(n, 0)
                exps(n, 4)
                exps(n, 5)
                exps(n, 6)
                evac_pv(n, 1)
                if n_x:
                    gate_tanh(f)
                evac_qk(n)
                exps(n, 7)
                if n_x:
                    evac_weights(f)
                exps(n, 8)
                soft_exp(n)
                evac_pv(n, 2)
                exps(n, 9)
                exps(n, 10)
                evac_soft(n)
                exps(n, 11)
                evac_ve(n)
                evac_pv(n, 3)
                evac_av(n)
                evac_att(n)
                if n_x:
                    evac_max(f)

            evac_norm(0, 0)
            evac_logits(0)
            evac_v(0, 0)
            gate_tanh(0)
            evac_weights(0)
            evac_max(0)
            step(0, 0, 2)
            step(1, 1, 2)
            with act.Fori(1, NB // 2 - 1) as j:
                for u in range(2):
                    step(2 * j + u, u, 2)
            step(NB - 2, 0, 1)
            step(NB - 1, 1, 0)

            act.wait_ge(snorm_done, NB)
            act.activation(smx[:, 0], smx[:, 3], ACT.Gelu).then_inc(set_act, 1)

            def evac_norm2(g, par):
                act.wait_ge(zT2_out, g + 1)
                act.activation(n2T[:, par], ps[:, G0], ACT.Identity, bias=lnp[:, 3:4],
                               scale=lnp[:, 2:3]).then_inc(n2T_done, 1)
                act.wait_ge(n2T_done, g + 1)
                act.activation(sqT[:], n2T[:, par], ACT.Square).then_inc(sq2_done, 1)

            def evac_logits2(g):
                act.wait_ge(lgT2_out, g + 1)
                act.activation(lgT[0:E], ps[0:E, G1], ACT.Copy).then_inc(lgT2_done, 1)
                act.activation(lgT[32:32 + E], ps[32:32 + E, G1], ACT.Copy).then_inc(lgT2_done, 1)

            def gate_tanh2(g):
                act.wait_ge(tanh2_in, g + 1)
                act.activation(gt[:, 9], gt[:, 1], ACT.Tanh, scale=0.5).then_inc(tanh2_out, 1)

            def evac_weights2(g):
                act.wait_ge(rwT2_out, g + 1)
                act.wait_ge(rw2_stored, 16 * g)
                act.activation(rwT[:], ps[0:E, G1], ACT.Copy).then_inc(rwT2_done, 1)

            def gelu(g, e):
                act.wait_ge(up_out, E * g + e + 1)
                if e % 2:
                    act.wait_ge(hgs2_done, E // 2 * g + e // 2)
                else:
                    act.wait_ge(hgs_done, E // 2 * g + e // 2)
                act.activation(hg[:, e % 2], ps[:, UP[e % 3]], ACT.Gelu).then_inc(gelu_done, 1)

            def step2(g, u, n_x):
                for e in range(E):
                    if n_x and e == 3:
                        gate_tanh2(g + 1)
                    if n_x and e == 6:
                        evac_weights2(g + 1)
                    if n_x == 2 and e == 7:
                        evac_norm2(g + 2, u)
                    gelu(g, e)
                if n_x == 2:
                    evac_logits2(g + 2)

            evac_norm2(0, 0)
            evac_logits2(0)
            gate_tanh2(0)
            evac_weights2(0)
            evac_norm2(1, 1)
            evac_logits2(1)
            step2(0, 0, 2)
            step2(1, 1, 2)
            with act.Fori(1, MS // 2 - 1) as j:
                for u in range(2):
                    step2(2 * j + u, u, 2)
            step2(MS - 2, 0, 1)
            step2(MS - 1, 1, 0)

        @block.vector
        def _(dve):
            ch = Chain(dve, set_dve, 0, N_SET_DVE)
            ch.add(dve.memset(ones_e[:], 1.0))
            ch.add(dve.memset(ones_p[:], 1.0))
            ch.add(dve.memset(ones_b[:], 1.0))
            ch.add(dve.memset(zeros_b[:], 0.0))
            ch.add(dve.memset(lgT[:], 0.0))
            ch.add(dve.memset(mpart[:], 0.0))
            ch.add(dve.memset(vst[:], 0.0))
            dve.wait_ge(ld_const, 16 * N_CONST)
            dve.wait_ge(set_act, 4)
            ch.link(dve.tensor_scalar(pig[:], pig[:], 0.5, 0.5, ALU.mult, ALU.add))
            ch.link(dve.tensor_scalar(theta[:], theta[:], pig[:, 0:1], None, ALU.mult))
            ROUND = 1.5 * 2.0 ** 23
            C1 = 6.28125
            C2 = float(np.float32(np.round((2 * np.pi - C1) * 2 ** 22) / 2 ** 22))
            C3 = float(2 * np.pi - C1 - C2)
            LIM = 3.1415925
            ch.add(dve.tensor_scalar(trn[:, 0], theta[:], 0.5 / np.pi, 0.25, ALU.mult, ALU.add))
            ch.link(dve.tensor_scalar(trn[:, 1], theta[:], 0.5 / np.pi, None, ALU.mult))
            ch.link(dve.tensor_scalar(trn[:], trn[:], ROUND, None, ALU.add))
            ch.link(dve.tensor_scalar(trn[:], trn[:], -ROUND, None, ALU.add))
            for i in range(2):
                ins = dve.scalar_tensor_tensor(red[:, i], trn[:, i], -C1, theta[:], ALU.mult, ALU.add)
            ch.link(ins)
            ch.link(dve.scalar_tensor_tensor(red[:], trn[:], -C2, red[:], ALU.mult, ALU.add))
            ch.link(dve.scalar_tensor_tensor(red[:], trn[:], -C3, red[:], ALU.mult, ALU.add))
            ch.link(dve.tensor_scalar(red[:, 0], red[:, 0], float(np.pi / 2), None, ALU.add))
            ch.link(dve.tensor_scalar(red[:], red[:], LIM, -LIM, ALU.min, ALU.max))
            assert ch.k == SIN_READY, ch.k
            dve.wait_ge(set_act, 5)
            qs = DH ** -0.5
            ch.add(dve.tensor_scalar(cs[:, 0, 0], red[:, 0], qs, None, ALU.mult))
            ch.add(dve.tensor_scalar(cs[:, 0, 1], red[:, 1], sin_sign[:, 0:1], qs, ALU.mult, ALU.mult))
            ch.add(dve.tensor_copy(cs[:, 1, 0], red[:, 0]))
            ch.add(dve.tensor_scalar(cs[:, 1, 1], red[:, 1], sin_sign[:, 0:1], None, ALU.mult))
            ch.link(dve.tensor_scalar(bias_in[:, 1:2], bias_in[:, 1:2], 0.5, 0.5, ALU.mult, ALU.add))
            ch.link(dve.tensor_tensor(bias_in[:, 0:1], bias_in[:, 0:1], bias_in[:, 1:2], ALU.mult))
            ch.link(dve.tensor_scalar(cb[:, 0], cpos[:], bias_in[:, 0:1], None, ALU.mult))
            ch.link(dve.tensor_scalar(cb[:, 1], cb[:, 0], -1.0, None, ALU.mult))
            for part in range(3):
                ch.link(dve.tensor_copy(cbp[:, :, part], cb[:]))
                if part < 2:
                    ch.link(dve.tensor_tensor(cb[:], cb[:], cbp[:, :, part], ALU.subtract))
            for h in range(HG):
                ch.add(dve.tensor_copy(mask_qk[:, h], mask_in[:, 0]))
                ch.add(dve.tensor_copy(mask_kq[:, h], mask_in[:, 1]))
            ch.add(dve.tensor_copy(identb[:], ident[:]))
            ch.add(dve.memset(vst[:, :, :, :, DH:DH + 1], 1.0))
            ch.add(dve.tensor_scalar(sg[:], sg[:], 0.5, 0.5, ALU.mult, ALU.add))
            ch.link(dve.tensor_tensor(gt[:, 0:2, 0], sims[:], sims[:], ALU.mult))
            dve.wait_ge(set_pe, 1)
            ch.link(dve.tensor_scalar(gt[:, 2:4, 0], ps[:, G0, 0:2 * E].rearrange("p (a e) -> p a e", a=2),
                                      NORM2, None, ALU.max))
            rsqrt(dve, ch, gt[:, 4:6, 0], gt[:, 2:4, 0], gt[:, 6:8, 0])
            ch.link(dve.tensor_tensor(simn[:], sims[:], gt[:, 4:6, 0], ALU.mult))
            ch.close()

            def layer_norm(b, par, beside=None):
                c = Chain(dve, ln_chain, b, 2 * LN_LINKS, beside)
                dve.wait_ge(x_in, 16 * (b + 1))
                dve.wait_ge(xzT_out, b)
                dve.wait_ge(keep_done, b)
                for rnd, src in enumerate((xt[:, par], xn[:])):
                    for i in range(T):
                        dve.bn_stats(bst[:, rnd, i], src[:, i])
                    dve.drain()
                    for i in range(T):
                        ins = dve.bn_aggr(bmv[:, rnd, i], bst[:, rnd, i])
                    c.link(ins)
                    c.link(dve.tensor_scalar(vstd[:, 0, 0:T], bmv[:, rnd, 0:T, 1], EPS, None, ALU.add))
                    rsqrt(dve, c, rstd[:, rnd, 0:T], vstd[:, 0, 0:T], vstd[:, 1, 0:T])
                    if rnd == 0:
                        for i in range(T):
                            ins = dve.tensor_scalar(xn[:, i], src[:, i], bmv[:, 0, i, 0:1], rstd[:, 0, i:i + 1],
                                                    ALU.subtract, ALU.mult)
                        ins.then_inc(ln_out, 1)
                        dve.wait_ge(ln_out, b + 1)
                c.close()

            def rotate(b):
                c = Chain(dve, rot_chain, b, ROT_LINKS)
                dve.wait_ge(rot_q_out, b + 1)
                c.link(dve.tensor_tensor(rott[:, 0], ps[:, G1].rearrange("p (a t) -> p a t", a=2), cs[:, 0], ALU.mult))
                c.add(dve.tensor_tensor(rot[:, 0], rott[:, 0, 0], rott[:, 0, 1], ALU.add))
                dve.wait_ge(rot_k_out, b + 1)
                c.link(dve.tensor_tensor(rott[:, 1], ps[:, G1].rearrange("p (a t) -> p a t", a=2), cs[:, 1], ALU.mult))
                c.link(dve.tensor_tensor(rot[:, 1], rott[:, 1, 0], rott[:, 1, 1], ALU.add))
                dve.wait_ge(parts_stored, 16 * b)
                c.link(dve.tensor_copy(parts[:, 0], rot[:]))
                c.link(dve.tensor_tensor(rres[:], rot[:], parts[:, 0], ALU.subtract))
                c.link(dve.tensor_copy(parts[:, 1], rres[:]))
                dve.tensor_tensor(parts[:, 2], rres[:], parts[:, 1], ALU.subtract).then_inc(parts_out, 1)
                c.close()

            def gating(b, nt, which, q, beside=None):
                chain, lg_out, lg_read, tanh_in, tanh_out, rwT_out, rw_out = q
                c = Chain(dve, chain, b, GATE_LINKS, beside)
                L, Dm, A, B2, C2_, F = (gt[:, k, 0:nt] for k in range(6))
                th = gt[:, 9, 0:nt]
                m1, m2, mc, rn, ina, tot = (gs[:, k, 0:nt] for k in range(6))

                def bc(v):
                    return v.rearrange("p (t o) -> p t o", o=1).broadcast_to((P, nt, E))
                rk = rank[:].rearrange("p (o e) -> p o e", o=1).broadcast_to((P, nt, E))
                sgb = sg[:, which:which + 1].broadcast_to((P, nt, E))
                lg = ps[:, LGB[which], 0:P * nt].rearrange("p (i k) -> p i k", k=P)
                dve.wait_ge(lg_out, b + 1)
                c.link(dve.tensor_scalar(rn, lg[:, :, 32], NORM2, None, ALU.max))
                rsqrt(dve, c, gs[:, 6, 0:nt], rn, gs[:, 7, 0:nt])
                dve.tensor_tensor(L, lg[:, :, 0:E], bc(gs[:, 6, 0:nt]), ALU.mult).then_inc(lg_read, 1)
                dve.wait_ge(lg_read, b + 1)
                c.link(dve.tensor_tensor(L, L, sgb, ALU.subtract))
                c.link(dve.tensor_reduce(m1, L, AX_X, ALU.max))
                dve.tensor_tensor(Dm, L, bc(m1), ALU.subtract).then_inc(tanh_in, 1)
                dve.wait_ge(tanh_in, b + 1)
                c.link(dve.scalar_tensor_tensor(A, Dm, 0.0, rk, ALU.is_ge, ALU.mult))
                c.link(dve.tensor_reduce(mc, A, AX_X, ALU.max))
                c.link(dve.tensor_tensor(A, A, bc(mc), ALU.is_equal))
                c.link(dve.scalar_tensor_tensor(B2, A, -BIG, L, ALU.mult, ALU.add))
                c.link(dve.tensor_reduce(m2, B2, AX_X, ALU.max))
                c.link(dve.tensor_tensor(C2_, B2, bc(m2), ALU.is_equal))
                c.link(dve.tensor_tensor(C2_, C2_, rk, ALU.mult))
                c.link(dve.tensor_reduce(mc, C2_, AX_X, ALU.max))
                c.link(dve.tensor_tensor(C2_, C2_, bc(mc), ALU.is_equal))
                c.add(dve.tensor_scalar(ina, m1, 0.0, None, ALU.is_le))
                c.link(dve.tensor_tensor(F, A, C2_, ALU.add))
                c.add(dve.tensor_tensor(F, F, bc(ina), ALU.mult))
                dve.wait_ge(tanh_out, b + 1)
                c.add(dve.tensor_scalar(A, th, 1.0, None, ALU.add))
                c.link(dve.tensor_scalar(B2, th, -1.0, 1.0, ALU.mult, ALU.add))
                c.link(dve.reciprocal(B2, B2))
                c.link(dve.tensor_tensor(A, A, B2, ALU.mult))
                c.link(dve.scalar_tensor_tensor(A, L, 0.0, A, ALU.is_gt, ALU.mult))
                dve.wait_ge(rwT_out, b)
                fin = gt[:, 6, 0:nt]
                dve.tensor_tensor(F, A, F, ALU.add).then_inc(rw_out, 1)
                dve.wait_ge(rw_out, 3 * b + 1)
                dve.tensor_reduce(tot, F, AX_X, ALU.add).then_inc(rw_out, 1)
                dve.wait_ge(rw_out, 3 * b + 2)
                c.link(dve.reciprocal(tot, tot))
                dve.tensor_tensor(fin, F, bc(tot), ALU.mult).then_inc(rw_out, 1)
                c.close()

            LGB = (G0, G0)
            gate1 = (gate_chain, lg_out, lg_read, tanh_in, tanh_out, rwT_out, rw_out)
            gate2 = (gate2_chain, lg2_out, lg2_read, tanh2_in, tanh2_out, rwT2_out, rw2_out)

            def row_max(b, k):
                G, i = divmod(k, 3)
                dve.wait_ge(s1_out, UNITS * b + k + 1)
                if k == 0:
                    dve.wait_ge(max_chain, (MAX_LINKS + 1) * b)
                n = HG if i == 0 else 2
                h = HG * G + (0 if i < 2 else 2)
                dve.tensor_reduce(mx[:, min(i, 1), h:h + n], ps[:, S1[k % 2]].rearrange("p (h t) -> p h t", h=n),
                                  AX_X, ALU.max).then_inc(s1_read, 1)

            def max_parts(b):
                c = Chain(dve, max_chain, b, MAX_LINKS + 1)
                mp = [mpart[:, :, k * H:(k + 1) * H] for k in range(3)]
                dve.wait_ge(s1_read, UNITS * (b + 1))
                dve.wait_ge(mT_out, b)
                c.link(dve.tensor_scalar(mp[0], mx[:], -1.0, None, ALU.mult))
                c.link(dve.scalar_tensor_tensor(mres[:], mx[:], -1.0, mp[0], ALU.mult, ALU.subtract))
                c.link(dve.tensor_copy(mp[1], mres[:]))
                c.add(dve.tensor_tensor(mp[2], mres[:], mp[1], ALU.subtract))
                c.close()

            def normalise(n, G):
                dve.wait_ge(ot_out, NG * n + G + 1)
                o = ps[:, G0, 0:S].rearrange("p (i h r) -> p i h r", i=T, r=32)
                c = Chain(dve, ot_read, NG * n + G, 2)
                c.link(dve.reciprocal(rden[:], o[:, :, :, DH]))
                if G == 0:
                    dve.wait_ge(attT_out, n)
                for i in range(T):
                    ins = dve.tensor_tensor(
                        att[:, i, DH * HG * G:DH * HG * (G + 1)].rearrange("p (h d) -> p h d", d=DH),
                        o[:, i, :, 0:DH],
                        rden[:, i].rearrange("p (h o) -> p h o", o=1).broadcast_to((P, HG, DH)), ALU.mult)
                c.add(ins)
                c.close()

            def soft_max(n):
                dve.wait_ge(ss_out, n + 1)
                dve.tensor_reduce(smx[:, 0, 0:1], ps[:, G1, 0:P], AX_X, ALU.max)
                dve.tensor_reduce(smx[:, 0, 1:2], ps[:, G1, P:3 * P], AX_X, ALU.max).then_inc(smax_done, 1)
                dve.wait_ge(smax_done, 2 * n + 1)
                dve.tensor_scalar(smx[:, 1], smx[:, 0], -1.0, None, ALU.mult).then_inc(smax_done, 1)

            def soft_norm(n):
                dve.wait_ge(sexp_done, 2 * n + 2)
                dve.reciprocal(smx[:, 3], smx[:, 2]).then_inc(snorm_chain, 1)
                dve.wait_ge(snorm_chain, n + 1)
                dve.tensor_scalar(sp[:, 0:P], sp[:, 0:P], smx[:, 3, 0:1], None, ALU.mult)
                dve.tensor_scalar(sp[:, P:3 * P], sp[:, P:3 * P], smx[:, 3, 1:2], None, ALU.mult
                                  ).then_inc(snorm_done, 1)

            def scale_att(n, u, e):
                if e == 0:
                    dve.wait_ge(oe_out, n)
                    dve.wait_ge(rep_in, 16 * (n + 1))
                    dve.wait_ge(av_done, n + 1)
                dve.tensor_tensor(ats[:, e:e + 2], rep[:, u, e:e + 2],
                                  avT[:].rearrange("p (o t) -> p o t", o=1).broadcast_to((P, 2, S)), ALU.mult
                                  ).then_inc(ats_done, 1)

            def add_x(n, u):
                dve.wait_ge(wo_out, n + 1)
                dve.wait_ge(xr_in, 16 * (n + 1))
                dve.tensor_tensor(xa[:, u], xr[:, u], ps[:, G0, 0:T * D].rearrange("p (i c) -> p i c", i=T),
                                  ALU.add).then_inc(xa_done, 1)

            def add_hs(n, u):
                dve.wait_ge(oe_out, n + 1)
                dve.wait_ge(keep_done, n + 1)
                hv = hs[:, T * n:T * n + T] if isinstance(n, int) else hs[:, bass.ds(n * T, T)]
                dve.tensor_tensor(hv, hv, ps[:, G1, 0:T * D].rearrange("p (i c) -> p i c", i=T),
                                  ALU.add).then_inc(hs_done, 1)
                dve.wait_ge(hs_done, n + 1)
                dve.wait_ge(xa_done, n + 1)
                dve.wait_ge(base_stored, 16 * n)
                dve.tensor_tensor(bs[:, u], hv, xa[:, u], ALU.add).then_inc(base_done, 1)

            def step(n, u, n_x):
                f, pf = n + 1, 1 - u
                def beside_gating(k):
                    if k in (14, 24):
                        normalise(n, 0 if k == 14 else 1)

                def beside_norm(k):
                    if k in ROW_MAX_AT and n_x:
                        row_max(f, ROW_MAX_AT.index(k))
                    if k == 7:
                        soft_max(n)
                    if k == 12:
                        normalise(n, 2)
                    if k == 13:
                        soft_norm(n)
                if n_x:
                    rotate(f)
                    gating(f, T, 0, gate1, beside_gating)
                else:
                    normalise(n, 0)
                    normalise(n, 1)
                if n_x == 2:
                    layer_norm(n + 2, u, beside_norm)
                else:
                    for k in range(1, 24):
                        beside_norm(k)
                if n_x:
                    row_max(f, 8)
                normalise(n, 3)
                scale_att(n, u, 0)
                scale_att(n, u, 2)
                if n_x:
                    row_max(f, 9)
                scale_att(n, u, 4)
                if n_x:
                    row_max(f, 10)
                scale_att(n, u, 6)
                if n_x:
                    row_max(f, 11)
                    max_parts(f)
                add_x(n, u)
                add_hs(n, u)

            layer_norm(0, 0)
            layer_norm(1, 1)
            rotate(0)
            gating(0, T, 0, gate1)
            for k in range(UNITS):
                row_max(0, k)
            max_parts(0)
            step(0, 0, 2)
            step(1, 1, 2)
            with dve.Fori(1, NB // 2 - 1) as j:
                for u in range(2):
                    step(2 * j + u, u, 2)
            step(NB - 2, 0, 1)
            step(NB - 1, 1, 0)

            def layer_norm2(g, beside=None):
                c = Chain(dve, ln2_chain, g, LN_LINKS, beside)
                dve.wait_ge(ln2_out, 2 * g)
                for i in range(TM):
                    h = hs[:, TM * g + i] if isinstance(g, int) else hs[:, bass.ds(g * TM + i, 1)].rearrange(
                        "p o c -> p (o c)")
                    dve.bn_stats(bst[:, 0, i], h)
                dve.drain()
                for i in range(TM):
                    ins = dve.bn_aggr(bmv[:, 0, i], bst[:, 0, i])
                c.link(ins)
                c.link(dve.tensor_scalar(vstd[:, 0], bmv[:, 0, :, 1], EPS, None, ALU.add))
                rsqrt(dve, c, rstd[:, 0], vstd[:, 0], vstd[:, 1])
                c.close()

            def scale_gelu(g, e, par):
                dve.wait_ge(gelu_done, E * g + e + 1)
                dve.wait_ge(rep2_in, 16 * (g + 1))
                dve.wait_ge(moe_out, E * g + max(e - 1, 0))
                dve.tensor_tensor(hgs[:, 0], hg[:, 0], rep2[par][:, e], ALU.mult).then_inc(hgs_done, 1)

            def finish(g, u):
                dve.wait_ge(moe_out, E * (g + 1))
                dve.wait_ge(out_stored, 16 * g)
                dve.wait_ge(base_in, 16 * (g + 1))
                dve.tensor_tensor(ot[:, u], bt[:, u], ps[:, MOE[u]].rearrange("p (i c) -> p i c", i=TM),
                                  ALU.add).then_inc(out_done, 1)

            def step2(g, u, n_x):
                scale_gelu(g, 0, u)
                if not isinstance(g, int) or g > 0:
                    finish(g - 1, 1 - u)

                def beside_gating(k):
                    if k in (5, 19):
                        scale_gelu(g, 2 if k == 5 else 4, u)

                def beside_norm(k):
                    if k == 4:
                        scale_gelu(g, 6, u)
                if n_x:
                    gating(g + 1, TM, 1, gate2, beside_gating)
                else:
                    scale_gelu(g, 2, u)
                    scale_gelu(g, 4, u)
                if n_x == 2:
                    layer_norm2(g + 2, beside_norm)
                else:
                    scale_gelu(g, 6, u)

            dve.wait_ge(base_done, NB)
            layer_norm2(0)
            gating(0, TM, 1, gate2)
            layer_norm2(1)
            step2(0, 0, 2)
            step2(1, 1, 2)
            with dve.Fori(1, MS // 2 - 1) as j:
                for u in range(2):
                    step2(2 * j + u, u, 2)
            step2(MS - 2, 0, 1)
            step2(MS - 1, 1, 0)
            finish(MS - 1, 1)

        @block.tensor
        def _(pe):
            mm = pe.matmul
            pe.wait_ge(set_dve, N_SET_DVE - 12)
            mm(ps[:, G0, 0:2 * E], ones_p[:], gt[:, 0:2, 0], start=True, stop=True).then_inc(set_pe, 1)
            pe.wait_ge(set_dve, N_SET_DVE)
            pe.wait_ge(ld_w, 16 * N_W)
            pe.wait_ge(set_dma, 16 * (N_SMALL + N_ROWS))

            def norm_T(b):
                pe.wait_ge(ln_out, b + 1)
                pe.wait_ge(zp_done, 2 * (b + 1))
                for k, src in enumerate((xn[:], zt[:])):
                    for i in range(T):
                        ins = pe.transpose(ps[:, G0, (T * k + i) * P:(T * k + i + 1) * P], src[:, i], ident[:])
                ins.then_inc(xzT_out, 1)

            def proj(b, side, prev):
                pe.wait_ge(xnT_done, b + 1)
                prev()
                for k in range(2):
                    ins = mm(ps[:, G1, k * S:(k + 1) * S], wa[:, 2 * side + k], xnT[:], start=True, stop=True)
                ins.then_inc((rot_q_out, rot_k_out)[side], 1)

            def logits_T(b, par):
                pe.wait_ge(sq_done, b + 1)
                mm(ps[0:E, G0, 0:S], simn[:, 0], n1T[:, par], start=True, stop=True)
                mm(ps[32:32 + E, G0, 0:S], ones_e[:], sqT[:, 0:S], start=True, stop=True).then_inc(lgT_out, 1)

            def logits(b):
                pe.wait_ge(lgT_done, 2 * (b + 1))
                for i in range(T):
                    ins = pe.transpose(ps[:, G0, i * P:(i + 1) * P], lgT[:, i * P:(i + 1) * P], ident[:])
                ins.then_inc(lg_out, 1)

            def proj_v(b):
                pe.wait_ge(rot_chain, ROT_LINKS * b + 3)
                for i in range(T):
                    ins = mm(ps[:, G1, i * D:(i + 1) * D], xnT[:, i * P:(i + 1) * P], wa[:, 4], start=True, stop=True)
                ins.then_inc(v_out, 1)

            def weights_T(b):
                pe.wait_ge(v_done, b + 1)
                pe.wait_ge(rw_out, 3 * (b + 1))
                for i in range(T):
                    ins = pe.transpose(ps[0:E, G1, i * P:(i + 1) * P], gt[:, 6, i], ident[:])
                ins.then_inc(rwT_out, 1)

            def unit1(b, par, k):
                G, i = divmod(k, 3)
                if k == 0:
                    pe.wait_ge(stack_in, 16 * 7 * (b + 1))
                if k == 0:
                    pe.wait_ge(mT_done, b)
                pe.wait_ge(s1_read, UNITS * b + max(k - 1, 0))
                bank = ps[:, S1[k % 2]]
                if i == 0:
                    mm(bank, identb[:], mask_qk[:].rearrange("p h t -> p (h t)"), start=True, stop=False,
                       skip_group_check=True)
                    for h in range(HG):
                        hh = HG * G + h
                        ins = mm(bank[:, h * P:(h + 1) * P], qst[0:KR, par, hh, 0:P], kst[0:KR, par, hh, 0:P],
                                 start=False, stop=True, skip_group_check=True)
                else:
                    mm(bank.rearrange("p (h t) -> p h t", h=2)[:, :, P:S], identb[:], mask_qk[:, 0:2],
                       start=True, stop=False, skip_group_check=True)
                    for h in range(2):
                        hh = HG * G + 2 * (i - 1) + h
                        ins = mm(bank[:, h * S:(h + 1) * S], qst[0:KR, par, hh, P:S], kst[0:KR, par, hh, :],
                                 start=False, stop=True, skip_group_check=True)
                ins.then_inc(s1_out, 1)

            def max_T(b):
                pe.wait_ge(max_chain, (MAX_LINKS + 1) * (b + 1))
                pv = ps[:, S1[0], 0:S // 2].bitcast(BF16)
                for i in range(T):
                    ins = pe.transpose(pv[:, i * P:(i + 1) * P], mpart[:, i], identb[:])
                ins.then_inc(mT_out, 1)

            def unit2(n, u, k):
                G, i = divmod(k, 3)
                if k == 0:
                    pe.wait_ge(max_in, 16 * (n + 1))
                pe.wait_ge(exp_done, UNITS * n + max(k - 1, 0))
                bank = ps[:, S2[k % 2]]
                if i < 2:
                    mm(bank.rearrange("p (h t) -> p h t", h=2)[:, :, 0:P], identb[:], mask_kq[:, 0:2],
                       start=True, stop=False, skip_group_check=True)
                    for h in range(2):
                        hh = HG * G + 2 * i + h
                        ins = mm(bank[:, h * S:(h + 1) * S], kst[0:KR, u, hh, 0:P], qst[0:KR, u, hh, :],
                                 start=False, stop=True, skip_group_check=True)
                else:
                    mm(bank, identb[:], mask_kq[:].rearrange("p h t -> p (h t)"), start=True, stop=False,
                       skip_group_check=True)
                    for h in range(HG):
                        hh = HG * G + h
                        ins = mm(bank[:, h * P:(h + 1) * P], kst[0:KR, u, hh, P:S], qst[0:KR, u, hh, P:S],
                                 start=False, stop=True, skip_group_check=True)
                ins.then_inc(s2_out, 1)

            def pv(n, u, G):
                pe.wait_ge(exp_done, UNITS * n + 3 * (G + 1))
                pe.wait_ge(ov_done, NG * n + G)
                if G == 0:
                    pe.wait_ge(v_done, n + 1)
                for h in range(HG):
                    mm(ps[32 * h:32 * h + 32, PVB, 0:S], vst[:, u, 0, HG * G + h],
                       pr[:, G % 2, h // 2, (h % 2) * S:(h % 2 + 1) * S], start=True, stop=False,
                       skip_group_check=True)
                for h in range(HG):
                    ins = mm(ps[32 * h:32 * h + 32, PVB, P:S], vst[:, u, 1, HG * G + h],
                             pr[:, G % 2, 2, h * P:(h + 1) * P], start=False, stop=True, skip_group_check=True)
                ins.then_inc(pv_out, 1)

            def out_T(n, G, prev):
                pe.wait_ge(ov_done, NG * n + G + 1)
                prev()
                for i in range(T):
                    ins = pe.transpose(ps[:, G0, i * P:(i + 1) * P], ov[:, G % 2, i * P:(i + 1) * P], ident[:])
                ins.then_inc(ot_out, 1)

            def qk(n, e):
                if e == 0:
                    pe.wait_ge(n1s_done, n + 1)
                    pe.wait_ge(ve_done, n)
                mm(ps[:, QKB, 0:S], wq[:, e], n1s[:, e], start=(e == 0), stop=(e == E - 1), skip_group_check=True)
                ins = mm(ps[:, QKB, S:2 * S], wk[:, e], n1s[:, e], start=False, stop=(e == E - 1),
                         skip_group_check=True)
                if e == E - 1:
                    ins.then_inc(qk_out, 1)

            def ve(n, e):
                if e == 0:
                    pe.wait_ge(qkT_done, 2 * (n + 1))
                for i in range(T):
                    ins = mm(ps[:, QKB, i * D:(i + 1) * D], n1s[:, e, i * P:(i + 1) * P], wv[:, e],
                             start=(e == 0 and i == 0), stop=(e == E - 1), skip_group_check=True)
                if e == E - 1:
                    ins.then_inc(ve_out, 1)

            def soft_scores(n):
                pe.wait_ge(qkT_done, 2 * (n + 1))
                pe.wait_ge(rwT_done, min(n + 2, NB) if isinstance(n, int) else n + 2)
                b = ps[:, G1]
                mm(b.rearrange("p (a t) -> p a t", a=2)[:, :, 0:P], identb[:], mask_qk[:, 0:2], start=True,
                   stop=False, skip_group_check=True)
                mm(b[:, 0:P], qT[:, 0:P], kT[:, 0:P], start=False, stop=True, skip_group_check=True)
                mm(b[:, P:3 * P], qT[:, P:S], kT[:], start=False, stop=True, skip_group_check=True
                   ).then_inc(ss_out, 1)

            def soft_T(n):
                pe.wait_ge(snorm_done, n + 1)
                for k in range(3):
                    ins = pe.transpose(ps[:, G1, k * P:(k + 1) * P], sp[:, k * P:(k + 1) * P], ident[:])
                ins.then_inc(spT_out, 1)

            def soft_av(n):
                pe.wait_ge(spT_done, n + 1)
                pe.wait_ge(ve_done, n + 1)
                mm(ps[:, G1, 0:S], vs[:, 0], spT[:, 0:S], start=True, stop=False, skip_group_check=True)
                mm(ps[:, G1, P:S], vs[:, 1], spT[:, S:3 * P], start=False, stop=True, skip_group_check=True
                   ).then_inc(av_out, 1)

            def oe(n, e):
                if e % 2 == 0:
                    pe.wait_ge(ats_done, E // 2 * n + e // 2 + 1)
                for i in range(T):
                    ins = mm(ps[:, G1, i * D:(i + 1) * D], ats[:, e, i * P:(i + 1) * P], wop[:, e],
                             start=(e == 0 and i == 0), stop=(e == E - 1), skip_group_check=True)
                if e == E - 1:
                    ins.then_inc(oe_out, 1)

            def att_T(n):
                pe.wait_ge(ot_read, 2 * NG * (n + 1))
                for i in range(T):
                    ins = pe.transpose(ps[:, G0, i * P:(i + 1) * P], att[:, i], ident[:])
                ins.then_inc(attT_out, 1)

            def att_out(n):
                pe.wait_ge(attT_done, n + 1)
                for i in range(T):
                    ins = mm(ps[:, G0, i * D:(i + 1) * D], attT[:, i * P:(i + 1) * P], wo[:], start=True, stop=True)
                ins.then_inc(wo_out, 1)

            def step(n, u, n_x):
                f, pf = n + 1, 1 - u
                if n_x:
                    pe.wait_ge(xa_done, n)
                    norm_T(f)
                qk(n, 0)
                unit2(n, u, 0)
                if n_x:
                    proj(f, 0, lambda: pe.wait_ge(hs_done, n))
                qk(n, 1)
                unit2(n, u, 1)
                if n_x:
                    logits_T(f, pf)
                    proj(f, 1, lambda: pe.wait_ge(rot_chain, ROT_LINKS * f + 1))
                qk(n, 2)
                unit2(n, u, 2)
                if n_x:
                    logits(f)
                    proj_v(f)
                qk(n, 3)
                unit2(n, u, 3)
                pv(n, u, 0)
                qk(n, 4)
                unit2(n, u, 4)
                out_T(n, 0, (lambda: pe.wait_ge(lg_read, n + 2)) if n_x else (lambda: pe.wait_ge(xa_done, n)))
                qk(n, 5)
                unit2(n, u, 5)
                qk(n, 6)
                unit2(n, u, 6)
                pv(n, u, 1)
                qk(n, 7)
                out_T(n, 1, lambda: pe.wait_ge(ot_read, 2 * (NG * n + 1)))
                unit2(n, u, 7)
                ve(n, 0)
                if n_x:
                    unit1(f, pf, 0)
                ve(n, 1)
                if n_x:
                    unit1(f, pf, 1)
                    weights_T(f)
                unit2(n, u, 8)
                ve(n, 2)
                soft_scores(n)
                if n_x:
                    unit1(f, pf, 2)
                ve(n, 3)
                pv(n, u, 2)
                if n_x:
                    unit1(f, pf, 3)
                unit2(n, u, 9)
                ve(n, 4)
                out_T(n, 2, lambda: pe.wait_ge(ot_read, 2 * (NG * n + 2)))
                if n_x:
                    unit1(f, pf, 4)
                ve(n, 5)
                unit2(n, u, 10)
                ve(n, 6)
                if n_x:
                    unit1(f, pf, 5)
                soft_T(n)
                ve(n, 7)
                unit2(n, u, 11)
                if n_x:
                    unit1(f, pf, 6)
                pv(n, u, 3)
                if n_x:
                    unit1(f, pf, 7)
                soft_av(n)
                out_T(n, 3, lambda: pe.wait_ge(ot_read, 2 * (NG * n + 3)))
                if n_x:
                    unit1(f, pf, 8)
                    unit1(f, pf, 9)
                oe(n, 0)
                att_T(n)
                if n_x:
                    unit1(f, pf, 10)
                oe(n, 1)
                oe(n, 2)
                att_out(n)
                if n_x:
                    unit1(f, pf, 11)
                for e in range(3, E):
                    oe(n, e)
                if n_x:
                    max_T(f)

            norm_T(0)
            proj(0, 0, lambda: None)
            logits_T(0, 0)
            proj(0, 1, lambda: pe.wait_ge(rot_chain, 1))
            logits(0)
            proj_v(0)
            weights_T(0)
            for k in range(UNITS):
                unit1(0, 0, k)
            max_T(0)
            step(0, 0, 2)
            step(1, 1, 2)
            with pe.Fori(1, NB // 2 - 1) as j:
                for u in range(2):
                    step(2 * j + u, u, 2)
            step(NB - 2, 0, 1)
            step(NB - 1, 1, 0)

            def norm_T2(g):
                pe.wait_ge(ln2_out, 2 * (g + 1))
                pe.wait_ge(lg2_read, g)
                for i in range(TM):
                    ins = pe.transpose(ps[:, G0, i * P:(i + 1) * P], z2[:, i], ident[:])
                ins.then_inc(zT2_out, 1)

            def logits_T2(g, par):
                pe.wait_ge(sq2_done, g + 1)
                pe.wait_ge(rwT2_done, g)
                mm(ps[0:E, G1], simn[:, 1], n2T[:, par], start=True, stop=True)
                mm(ps[32:32 + E, G1], ones_e[:], sqT[:], start=True, stop=True).then_inc(lgT2_out, 1)

            def logits2(g):
                pe.wait_ge(lgT2_done, 2 * (g + 1))
                for i in range(TM):
                    ins = pe.transpose(ps[:, G0, i * P:(i + 1) * P], lgT[:, i * P:(i + 1) * P], ident[:])
                ins.then_inc(lg2_out, 1)

            def weights_T2(g):
                pe.wait_ge(rw2_out, 3 * (g + 1))
                for i in range(TM):
                    ins = pe.transpose(ps[0:E, G1, i * P:(i + 1) * P], gt[:, 6, i], ident[:])
                ins.then_inc(rwT2_out, 1)

            def up(g, u, e):
                pe.wait_ge(n2T_done, g + 1)
                pe.wait_ge(gelu_done, E * g + max(e - 2, 0))
                mm(ps[:, UP[e % 3]], w1s[:, e], n2T[:, u], start=True, stop=True).then_inc(up_out, 1)

            def down(g, u, e):
                pe.wait_ge(hgs2_done if e % 2 else hgs_done, E // 2 * g + e // 2 + 1)
                if e == 0:
                    pe.wait_ge(out_done, max(g - 1, 0) if isinstance(g, int) else g - 1)
                for i in range(TM):
                    ins = mm(ps[:, MOE[u], i * D:(i + 1) * D], hgs[:, e % 2, i * P:(i + 1) * P], w2s[:, e],
                             start=(e == 0 and i == 0), stop=(e == E - 1), skip_group_check=True)
                ins.then_inc(moe_out, 1)

            def step2(g, u, n_x):
                up(g, u, 0)
                up(g, u, 1)
                for e in range(E):
                    down(g, u, e)
                    if e + 2 < E:
                        up(g, u, e + 2)
                    if n_x and e == 4:
                        weights_T2(g + 1)
                    if n_x == 2 and e == 5:
                        norm_T2(g + 2)
                    if n_x == 2 and e == 6:
                        logits_T2(g + 2, u)
                    if n_x == 2 and e == 7:
                        logits2(g + 2)

            norm_T2(0)
            logits_T2(0, 0)
            logits2(0)
            weights_T2(0)
            norm_T2(1)
            logits_T2(1, 1)
            logits2(1)
            step2(0, 0, 2)
            step2(1, 1, 2)
            with pe.Fori(1, MS // 2 - 1) as j:
                for u in range(2):
                    step2(2 * j + u, u, 2)
            step2(MS - 2, 0, 1)
            step2(MS - 1, 1, 0)


def kernel(L0_attn_x, L0_attn_Wqkv, L0_attn_Wo, L0_attn_log_xi, L0_attn_pi_gate_logit, L0_attn_e_gate_logit,
           L0_ffn_ln1_w, L0_ffn_ln1_b, L0_ffn_ln2_w, L0_ffn_ln2_b, L0_ffn_smha_sim, L0_ffn_smha_gates,
           L0_ffn_q_proj, L0_ffn_k_proj, L0_ffn_v_proj, L0_ffn_o_proj, L0_ffn_moe_sim, L0_ffn_moe_gates,
           L0_ffn_w1, L0_ffn_w2):
    import concourse.bacc as bacc
    from concourse.bass_utils import run_bass_kernel_spmd

    wqkv_t = np.ascontiguousarray(L0_attn_Wqkv).T.reshape(D, 3, D)
    swap = np.arange(D) ^ 1
    by_pos = np.arange(D).reshape(H, DH).T.reshape(D)
    w_attn = np.stack([wqkv_t[:, k][:, cols] for k in range(2) for cols in (by_pos, swap[by_pos])]
                      + [wqkv_t[:, 2]], 1)

    inv_freq = np.float32(np.pi) ** (np.float32(1.0) - np.arange(0, DH, 2, dtype=np.float32) / np.float32(DH))
    pos = np.arange(S, dtype=np.float32)
    pos_freq = pos[None, :] * inv_freq.astype(np.float32)[np.arange(D) // H // 2][:, None]
    r = np.arange(P)
    arrays = {
        "x": L0_attn_x, "w_attn": w_attn, "w_o": np.ascontiguousarray(L0_attn_Wo).T,
        "log_xi": L0_attn_log_xi, "pi_logit": L0_attn_pi_gate_logit, "e_logit": L0_attn_e_gate_logit,
        "ln1_w": np.reshape(L0_ffn_ln1_w, (D, 1)), "ln1_b": np.reshape(L0_ffn_ln1_b, (D, 1)),
        "ln2_w": np.reshape(L0_ffn_ln2_w, (D, 1)), "ln2_b": np.reshape(L0_ffn_ln2_b, (D, 1)),
        "sim1": L0_ffn_smha_sim, "gates1": L0_ffn_smha_gates,
        "q_proj": L0_ffn_q_proj, "k_proj": L0_ffn_k_proj, "v_proj": L0_ffn_v_proj, "o_proj": L0_ffn_o_proj,
        "sim2": L0_ffn_moe_sim, "gates2": L0_ffn_moe_gates, "w1": L0_ffn_w1, "w2": L0_ffn_w2,
        "c_ident": np.eye(P, dtype=np.float32),
        "c_mask_qk": np.where(r[None, :] > r[:, None], -BIG, 0.0).astype(np.float32),
        "c_mask_kq": np.where(r[:, None] > r[None, :], -BIG, 0.0).astype(np.float32),
        "c_pos_freq": pos_freq.astype(np.float32),
        "c_sin_sign": np.where(r // H % 2 == 0, -1.0, 1.0).astype(np.float32)[:, None],
        "c_pos": np.broadcast_to(pos, (H, S)).astype(np.float32),
        "c_rank": np.broadcast_to(np.arange(E, 0, -1), (P, E)).astype(np.float32),
    }
    arrays = {f"in_{k}": np.ascontiguousarray(v) for k, v in arrays.items()}
    nc = bacc.Bacc("TRN2", target_bir_lowering=False, num_devices=1)
    args = [nc.dram_tensor(k, v.shape, mybir.dt.from_np(v.dtype), kind="ExternalInput").ap() for k, v in arrays.items()]
    out = nc.dram_tensor("out", (NB, S, D), F32, kind="ExternalOutput").ap()
    build(nc, *args, out)
    r = run_bass_kernel_spmd(nc, [arrays], core_ids=[0])
    return r.results[0]["out"]
```

```python
from contextlib import ExitStack

import numpy as np

import concourse.bass as bass
from concourse import mybir

F32 = mybir.dt.float32
BF16 = mybir.dt.bfloat16
ALU = mybir.AluOpType
ACT = mybir.ActivationFunctionType
AX_X = mybir.AxisListType.X

NB = 32
S = 256
D = 128
H = 16
DH = D // H
P = 128
T = S // P
E = 8
NG = 4
HG = H // NG
UNITS = 3 * NG
EPS = 1e-5
NORM2 = 1e-24
BIG = 1e30
TM = 4
MS = NB * T // TM
W2 = TM * P

R_BIAS_J = 0
R_BIAS_I = 3
R_PARTS = 8
R_MAX = R_PARTS + 6 * DH
Q_SLOTS = ((0, 3, 0), (3, 2, 1), (5, 1, 2))
K_SLOTS = ((0, 3, 0), (3, 2, 0), (5, 1, 0))
KR = P

LN_LINKS = 2 + 10
ROT_LINKS = 7
GATE_LINKS = 21 + 10
MAX_LINKS = 3
ATS_CHUNKS = ((0, 1), (1, 1), (2, 2), (4, 2), (6, 2))
GATE_MAX_AT = (3, 7, 10, 14, 18, 21, 24)


class Chain:

    def __init__(self, eng, sem, done_before, per, beside=None):
        self.eng, self.sem, self.base, self.per, self.k = eng, sem, done_before * per, per, 0
        self.beside = beside or (lambda k: None)

    def add(self, ins):
        ins.then_inc(self.sem, 1)
        self.k += 1

    def link(self, ins):
        self.add(ins)
        self.beside(self.k)
        self.wait()

    def wait(self):
        self.eng.wait_ge(self.sem, self.base + self.k)

    def close(self):
        assert self.k == self.per, (self.k, self.per)


RSQRT_LINKS = 10


def rsqrt(dve, c, y, v, t):
    c.add(dve.tensor_scalar(y.bitcast(mybir.dt.int32), v.bitcast(mybir.dt.int32), -0.5, float(0x5F3759DF),
                            ALU.mult, ALU.add))
    yield
    c.wait()
    for _ in range(3):
        c.add(dve.scalar_tensor_tensor(t, y, -0.5, y, ALU.mult, ALU.mult))
        yield
        c.wait()
        c.add(dve.tensor_tensor(t, t, v, ALU.mult))
        yield
        c.wait()
        c.add(dve.scalar_tensor_tensor(y, t, 1.5, y, ALU.add, ALU.mult))
        yield
        c.wait()


def run(steps):
    for _ in steps:
        pass


def build(nc, x, w_attn, w_o, log_xi, pi_logit, e_logit, ln1_w, ln1_b, ln2_w, ln2_b, sim1, gates1,
          q_proj, k_proj, v_proj, o_proj, sim2, gates2, w1, w2, c_ident, c_mask_qk, c_mask_kq, c_pos_freq,
          c_sin_sign, c_pos, c_rank, out):
    scr_parts = nc.dram_tensor("scr_parts", (2, 3, 2, DH, H, S), BF16, kind="Internal").ap()
    scr_rw = nc.dram_tensor("scr_rw", (2, E, S), F32, kind="Internal").ap()
    scr_rw2 = nc.dram_tensor("scr_rw2", (2, E, W2), F32, kind="Internal").ap()

    scr_base = nc.dram_tensor("scr_base", (NB, P, T, D), F32, kind="Internal").ap()

    with ExitStack() as ctx:
        def sb(name, shape, dt=F32):
            return ctx.enter_context(nc.sbuf_tensor(name, shape, dt))

        def sem(name):
            return ctx.enter_context(nc.semaphore(name))

        ident = sb("ident", [P, P])
        identb = sb("identb", [P, P], BF16)
        mask_in = sb("mask_in", [P, 2, P])
        mask_qk = sb("mask_qk", [P, HG, P], BF16)
        mask_kq = sb("mask_kq", [P, HG, P], BF16)
        wa = sb("wa", [P, 5, D])
        wo = sb("wo", [P, D])
        wq = sb("wq", [P, E, D])
        wk = sb("wk", [P, E, D])
        wv = sb("wv", [P, E, D])
        wop = sb("wop", [P, E, D])
        w1s = sb("w1s", [P, E, D])
        w2s = sb("w2s", [P, E, D])
        lnp = sb("lnp", [P, 4])
        simn = sb("simn", [P, 2, E])
        sg = sb("sg", [P, 2, E])
        rank = sb("rank", [P, E])
        ones_e = sb("ones_e", [P, E])
        ones_p = sb("ones_p", [P, P])
        cs = sb("cs", [P, 2, 2, S])
        theta = sb("theta", [P, S])
        trn = sb("trn", [P, 2, S])
        red = sb("red", [P, 2, S])
        sin_sign = sb("sin_sign", [P, 1])
        pig = sb("pig", [P, 1])
        bias_in = sb("bias_in", [H, 2])
        cpos = sb("cpos", [H, S])
        cb = sb("cb", [H, 2, S])
        cbp = sb("cbp", [H, 2, 3, S], BF16)
        ones_b = sb("ones_b", [3, 1, S], BF16)
        zeros_b = sb("zeros_b", [3, 1, S], BF16)
        sims = sb("sims", [P, 2, E])

        xt = sb("xt", [P, 2, T, D])
        xr = sb("xr", [P, 2, T, D])
        xn = sb("xn", [P, T, D])
        zt = sb("zt", [P, T, D])
        bst = sb("bst", [P, 2, TM, 6])
        bmv = sb("bmv", [P, 2, TM, 2])
        rstd = sb("rstd", [P, 2, TM])
        vstd = sb("vstd", [P, 2, TM])
        xnT = sb("xnT", [P, S])
        n1T = sb("n1T", [P, 2, S])
        sqT = sb("sqT", [P, W2])
        lgT = sb("lgT", [P, W2])
        gt = sb("gt", [P, 10, TM, E])
        gs = sb("gs", [P, 8, TM])
        rwT = sb("rwT", [E, W2])
        rep = sb("rep", [P, 2, E, S])
        n1s = sb("n1s", [P, E, S])
        ats = sb("ats", [P, E, S])
        rott = sb("rott", [P, 2, 2, S])
        rot = sb("rot", [P, 2, S])
        rres = sb("rres", [P, 2, S])
        parts = sb("parts", [P, 3, 2, S], BF16)
        qst = sb("qst", [P, 2, H, S], BF16)
        kst = sb("kst", [P, 2, H, S], BF16)
        vst = sb("vst", [P, 2, T, H, 32])
        mx = sb("mx", [P, T, H])
        mres = sb("mres", [P, T, H])
        mpart = sb("mpart", [P, T, P], BF16)
        mT = sb("mT", [3 * H, S], BF16)
        pr = sb("pr", [P, 2, 3, 512])
        ov = sb("ov", [P, 2, S])
        rden = sb("rden", [P, T, HG])
        att = sb("att", [P, T, D])
        attT = sb("attT", [P, S])
        avT = sb("avT", [P, S])
        qT = sb("qT", [P, S])
        kT = sb("kT", [P, S])
        vs = sb("vs", [P, T, D])
        smx = sb("smx", [P, 4, T])
        sp = sb("sp", [P, 3 * P])
        spT = sb("spT", [P, 3 * P])
        hs = sb("hs", [P, NB * T, D])
        bs = sb("bs", [P, 2, T, D])
        xa = sb("xa", [P, 2, T, D])

        prf = pr[:].rearrange("p a i t -> p (a i t)")
        bt = prf[:, 0:2 * TM * D].rearrange("p (a i c) -> p a i c", a=2, i=TM)
        z2 = prf[:, 2 * TM * D:3 * TM * D].rearrange("p (i c) -> p i c", i=TM)
        rep2 = [v[:].rearrange("p a h t -> p (a h t)").bitcast(F32).rearrange("p (e t) -> p e t", e=E)
                for v in (qst, kst)]
        n1f, atf = (v[:].rearrange("p e t -> p (e t)") for v in (n1s, ats))
        n2T = n1f[:, 0:2 * W2].rearrange("p (a t) -> p a t", a=2)
        n2Tn = rep[:].rearrange("p a e t -> p (a e t)")[:, 0:W2]
        hg = n1f[:, 2 * W2:4 * W2].rearrange("p (a t) -> p a t", a=2)
        hgs = atf[:, 0:2 * W2].rearrange("p (a t) -> p a t", a=2)
        ot = atf[:, 2 * W2:4 * W2].rearrange("p (a i c) -> p a i c", a=2, i=TM)

        ps = ctx.enter_context(nc.psum_tensor("ps", [P, 8, 512], F32))
        S1, S2, PVB, QKB, G0, G1 = (0, 1), (2, 3), 4, 5, 6, 7

        ld_const, ld_w = sem("ld_const"), sem("ld_w")
        set_dve, set_act, set_pe, set_pool, set_dma = (
            sem("set_dve"), sem("set_act"), sem("set_pe"), sem("set_pool"), sem("set_dma"))
        x_in = sem("x_in")
        ln_chain = sem("ln_chain")
        ln_out = sem("ln_out")
        xzT_out = sem("xzT_out")
        xr_in = sem("xr_in")
        keep_done = sem("keep_done")
        zp_done = sem("zp_done")
        av_done = sem("av_done")
        xnT_done = sem("xnT_done")
        n1T_done = sem("n1T_done")
        sq_done = sem("sq_done")
        lgT_out = sem("lgT_out")
        lgT_done = sem("lgT_done")
        lg_out = sem("lg_out")
        lg_read = sem("lg_read")
        gate_chain = sem("gate_chain")
        tanh_in = sem("tanh_in")
        tanh_out = sem("tanh_out")
        rw_out = sem("rw_out")
        rwT_out = sem("rwT_out")
        rwT_done = sem("rwT_done")
        rw_stored = sem("rw_stored")
        rep_in = sem("rep_in")
        n1s_done = sem("n1s_done")
        rot_q_out = sem("rot_q_out")
        rot_k_out = sem("rot_k_out")
        rot_chain = sem("rot_chain")
        parts_out = sem("parts_out")
        parts_stored = sem("parts_stored")
        stack_in = sem("stack_in")
        v_out = sem("v_out")
        v_done = sem("v_done")
        s1_out = sem("s1_out")
        s1_read = sem("s1_read")
        max_chain = sem("max_chain")
        mT_out = sem("mT_out")
        mT_done = sem("mT_done")
        max_in = sem("max_in")
        s2_out = sem("s2_out")
        exp_done = sem("exp_done")
        pv_out = sem("pv_out")
        ov_done = sem("ov_done")
        ot_out = sem("ot_out")
        ot_read = sem("ot_read")
        attT_out = sem("attT_out")
        attT_done = sem("attT_done")
        wo_out = sem("wo_out")
        xa_done = sem("xa_done")
        qk_out = sem("qk_out")
        qkT_done = sem("qkT_done")
        ve_out = sem("ve_out")
        ve_done = sem("ve_done")
        ss_out = sem("ss_out")
        smax_done = sem("smax_done")
        sexp_done = sem("sexp_done")
        snorm_chain = sem("snorm_chain")
        snorm_done = sem("snorm_done")
        spT_out = sem("spT_out")
        spT_done = sem("spT_done")
        av_out = sem("av_out")
        ats_done = sem("ats_done")
        oe_out = sem("oe_out")
        hs_done = sem("hs_done")
        base_done = sem("base_done")
        base_stored = sem("base_stored")
        base_in = sem("base_in")
        ln2_chain = sem("ln2_chain")
        ln2_out = sem("ln2_out")
        zT2_out = sem("zT2_out")
        n2Tn_done = sem("n2Tn_done")
        n2T_done = sem("n2T_done")
        sq2_done = sem("sq2_done")
        lgT2_out = sem("lgT2_out")
        lgT2_done = sem("lgT2_done")
        lg2_out = sem("lg2_out")
        lg2_read = sem("lg2_read")
        gate2_chain = sem("gate2_chain")
        tanh2_in = sem("tanh2_in")
        tanh2_out = sem("tanh2_out")
        rw2_out = sem("rw2_out")
        rwT2_out = sem("rwT2_out")
        rwT2_done = sem("rwT2_done")
        rw2_stored = sem("rw2_stored")
        rep2_in = sem("rep2_in")
        up_out = sem("up_out")
        hgs2_done = sem("hgs2_done")
        gelu_done = sem("gelu_done")
        hgs_done = sem("hgs_done")
        moe_out = sem("moe_out")
        out_done = sem("out_done")
        out_stored = sem("out_stored")

        block = ctx.enter_context(nc.Block())
        N_CONST, N_W, N_SMALL = 13, 8, 5
        N_ROWS = 18
        SIN_READY, N_SET_DVE = 18, 55
        UP, MOE = (0, 1, 2), (3, 4)

        @block.sync
        def _(sp_):
            x_v = x.rearrange("b (i p) c -> b p i c", p=P)

            sp_.dma_start(xt[:, 0], x_v[0]).then_inc(x_in, 16)
            for dst, src in ((ident[:], c_ident), (mask_in[:, 0], c_mask_qk), (mask_in[:, 1], c_mask_kq),
                             (theta[:], c_pos_freq), (sin_sign[:], c_sin_sign), (cpos[:], c_pos),
                             (rank[:], c_rank), (lnp[:, 0:1], ln1_w), (lnp[:, 1:2], ln1_b),
                             (lnp[:, 2:3], ln2_w), (lnp[:, 3:4], ln2_b),
                             (sims[:, 0], sim1), (sims[:, 1], sim2)):
                sp_.dma_start(dst, src).then_inc(ld_const, 16)
            for dst, src in ((wa[:], w_attn), (wo[:], w_o), (wq[:], q_proj), (wk[:], k_proj),
                             (wv[:], v_proj), (wop[:], o_proj), (w1s[:], w1), (w2s[:], w2)):
                v = src.rearrange("e c h -> c e h") if len(src.shape) == 3 and src.shape[0] == E else src
                sp_.dma_start(dst, v).then_inc(ld_w, 16)
            sp_.wait_ge(x_in, 16)
            sp_.dma_start(xt[:, 1], x_v[1]).then_inc(x_in, 16)
            sp_.wait_ge(set_pool, 2)
            sp_.wait_ge(set_dve, N_SET_DVE)
            for par in range(2):
                for part in range(3):
                    sp_.dma_start(kst[R_BIAS_J + part:R_BIAS_J + part + 1, par], cbp[:, 0, part]).then_inc(set_dma, 16)
                    sp_.dma_start(qst[R_BIAS_I + part:R_BIAS_I + part + 1, par], cbp[:, 1, part]).then_inc(set_dma, 16)
                sp_.dma_start(qst[R_BIAS_J:R_BIAS_J + 3, par], ones_b[:].broadcast_to((3, H, S))).then_inc(set_dma, 16)
                sp_.dma_start(kst[R_BIAS_I:R_BIAS_I + 3, par], ones_b[:].broadcast_to((3, H, S))).then_inc(set_dma, 16)
                sp_.dma_start(kst[R_MAX:R_MAX + 3, par], ones_b[:].broadcast_to((3, H, S))).then_inc(set_dma, 16)

            def store_parts(b, par):
                sp_.wait_ge(parts_out, 1 + b)
                sp_.dma_start(scr_parts[par].rearrange("p s d h t -> (d h) (p s) t"),
                              parts[:].rearrange("q p s t -> q (p s) t")).then_inc(parts_stored, 16)

            def stacks(b, par, old):
                if old:
                    sp_.wait_ge(s2_out, UNITS * (b - 1))
                sp_.dma_start(qst[R_MAX:R_MAX + 3, par], zeros_b[:].broadcast_to((3, H, S))).then_inc(stack_in, 16)
                sp_.wait_ge(parts_stored, 16 * (b + 1))
                for side, dst, slots in ((0, qst, Q_SLOTS), (1, kst, K_SLOTS)):
                    v = scr_parts[par, :, side].rearrange("p d h t -> p d (h t)")
                    for first, n, part in slots:
                        rows = dst[R_PARTS + DH * first:R_PARTS + DH * (first + n), par].rearrange("p h t -> p (h t)")
                        src = v[part:part + 1].broadcast_to((n, DH, H * S)) if side == 0 and n > 1 else (
                            v[part:part + n])
                        sp_.dma_start(rows, src).then_inc(stack_in, 16)

            def store_weights(b, par):
                sp_.wait_ge(rwT_done, b + 1)
                sp_.dma_start(scr_rw[par], rwT[:, 0:S]).then_inc(rw_stored, 16)

            def spread_weights(b, par):
                sp_.wait_ge(rw_stored, 16 * (b + 1))
                sp_.dma_start(rep[:, par].rearrange("p e t -> p (e t)"),
                              scr_rw[par].rearrange("(o e) t -> o (e t)", o=1).broadcast_to((P, E * S))
                              ).then_inc(rep_in, 16)

            def put_max(b, par):
                sp_.wait_ge(mT_done, b + 1)
                sp_.dma_start(qst[R_MAX:R_MAX + 3, par], mT[:]).then_inc(max_in, 16)

            def load_x(b, par, dst, arrived):
                src = x_v[b] if isinstance(b, int) else x_v[bass.ds(b, 1)].rearrange("o p i c -> p (o i) c")
                sp_.dma_start(dst[:, par], src).then_inc(arrived, 16)

            def store_base(n, u):
                dst = scr_base[n] if isinstance(n, int) else scr_base[bass.ds(n, 1)].rearrange("o p i c -> p (o i) c")
                sp_.dma_start(dst, bs[:, u]).then_inc(base_stored, 16)

            def step(n, u, n_x):
                sp_.wait_ge(base_done, n)
                if not isinstance(n, int) or n > 0:
                    store_base(n - 1, 1 - u)
                load_x(n, u, xr, xr_in)
                if n_x == 3:
                    sp_.wait_ge(x_in, 16 * (n + 3))
                    load_x(n + 3, 1 - u, xt, x_in)
                if n_x:
                    spread_weights(n + 1, 1 - u)
                if n_x >= 2:
                    store_parts(n + 2, u)
                if n_x:
                    put_max(n + 1, 1 - u)
                if n_x >= 2:
                    stacks(n + 2, u, True)
                    store_weights(n + 2, u)

            store_parts(0, 0)
            stacks(0, 0, False)
            store_weights(0, 0)
            spread_weights(0, 0)
            sp_.wait_ge(ln_out, 1)
            sp_.wait_ge(x_in, 32)
            load_x(2, 0, xt, x_in)
            store_parts(1, 1)
            stacks(1, 1, False)
            store_weights(1, 1)
            put_max(0, 0)
            step(0, 0, 3)
            step(1, 1, 3)
            with sp_.Fori(1, NB // 2 - 2) as j:
                for u in range(2):
                    step(2 * j + u, u, 3)
            step(NB - 4, 0, 3)
            step(NB - 3, 1, 2)
            step(NB - 2, 0, 1)
            step(NB - 1, 1, 0)

            def store_weights2(g, par):
                sp_.wait_ge(rwT2_done, g + 1)
                sp_.dma_start(scr_rw2[par], rwT[:]).then_inc(rw2_stored, 16)

            def spread2(g, par):
                sp_.wait_ge(rw2_stored, 16 * (g + 1))
                sp_.dma_start(rep2[par].rearrange("p e t -> p (e t)"),
                              scr_rw2[par].rearrange("(o e) t -> o (e t)", o=1).broadcast_to((P, E * W2))
                              ).then_inc(rep2_in, 16)

            o_v = out.rearrange("b (i p) c -> p (b i) c", p=P)

            base_v = scr_base.rearrange("b p i c -> p b (i c)")

            def load_base(g, par):
                v = base_v[:, 2 * g:2 * g + 2] if isinstance(g, int) else base_v[:, bass.ds(g * 2, 2)]
                sp_.dma_start(bt[:, par].rearrange("p (b i) c -> p b (i c)", b=2), v).then_inc(base_in, 16)

            def store_out(g, u):
                dst = o_v[:, TM * g:TM * g + TM] if isinstance(g, int) else o_v[:, bass.ds(g * TM, TM)]
                sp_.dma_start(dst, ot[:, u]).then_inc(out_stored, 16)

            def step2(g, u, n_x):
                sp_.wait_ge(out_done, g)
                if not isinstance(g, int) or g > 0:
                    store_out(g - 1, 1 - u)
                if n_x:
                    sp_.wait_ge(rep2_in, 16 * (g + 1))
                    load_base(g + 1, 1 - u)
                    spread2(g + 1, 1 - u)
                if n_x >= 2:
                    store_weights2(g + 2, u)

            sp_.wait_ge(base_done, NB)
            store_base(NB - 1, 1)
            sp_.wait_ge(base_stored, 16 * NB)
            load_base(0, 0)
            store_weights2(0, 0)
            spread2(0, 0)
            store_weights2(1, 1)
            step2(0, 0, 3)
            step2(1, 1, 3)
            with sp_.Fori(1, MS // 2 - 2) as j:
                for u in range(2):
                    step2(2 * j + u, u, 3)
            step2(MS - 4, 0, 3)
            step2(MS - 3, 1, 2)
            step2(MS - 2, 0, 1)
            step2(MS - 1, 1, 0)
            sp_.wait_ge(out_done, MS)
            store_out(MS - 1, 1)
            sp_.wait_ge(out_stored, 16 * MS)

        @block.gpsimd
        def _(pool):
            pool.memset(qst[:], 0.0).then_inc(set_pool, 1)
            pool.memset(kst[:], 0.0).then_inc(set_pool, 1)

            def scale(b, par):
                pool.wait_ge(rep_in, 16 * (b + 1))
                pool.wait_ge(n1T_done, b + 1)
                pool.wait_ge(ve_out, b)
                pool.tensor_tensor(n1s[:], rep[:, par], n1T[:, par:par + 1, :].broadcast_to((P, E, S)),
                                   ALU.mult).then_inc(n1s_done, 1)

            def second_norm(b):
                pool.wait_ge(ln_chain, 2 * LN_LINKS * (b + 1))
                pool.wait_ge(xzT_out, b)
                pool.tensor_tensor(zt[:], xn[:], bmv[:, 1, 0:T, 0:1].broadcast_to((P, T, D)),
                                   ALU.subtract).then_inc(zp_done, 1)
                pool.wait_ge(zp_done, 2 * b + 1)
                pool.tensor_tensor(zt[:], zt[:],
                                   rstd[:, 1, 0:T].rearrange("p (i o) -> p i o", o=1).broadcast_to((P, T, D)),
                                   ALU.mult).then_inc(zp_done, 1)
                hv = hs[:, T * b:T * b + T] if isinstance(b, int) else hs[:, bass.ds(b * T, T)]
                pool.tensor_copy(hv, xn[:]).then_inc(keep_done, 1)

            def step(n, u, n_x):
                if n_x == 3:
                    second_norm(n + 3)
                if n_x:
                    scale(n + 1, 1 - u)

            second_norm(0)
            second_norm(1)
            second_norm(2)
            scale(0, 0)
            step(0, 0, 3)
            step(1, 1, 3)
            with pool.Fori(1, NB // 2 - 2) as j:
                for u in range(2):
                    step(2 * j + u, u, 3)
            step(NB - 4, 0, 3)
            step(NB - 3, 1, 2)
            step(NB - 2, 0, 1)
            step(NB - 1, 1, 0)

            def scale_gelu(g, e, par):
                pool.wait_ge(gelu_done, E * g + e + 1)
                pool.wait_ge(rep2_in, 16 * (g + 1))
                pool.wait_ge(moe_out, E * g + max(e - 1, 0))
                pool.tensor_tensor(hgs[:, 1], hg[:, 1], rep2[par][:, e], ALU.mult).then_inc(hgs2_done, 1)

            def norm2(g):
                pool.wait_ge(ln2_chain, LN_LINKS * (g + 1))
                pool.wait_ge(zT2_out, g)
                h = hs[:, TM * g:TM * g + TM] if isinstance(g, int) else hs[:, bass.ds(g * TM, TM)]
                pool.tensor_tensor(z2, h, bmv[:, 0, :, 0:1].broadcast_to((P, TM, D)), ALU.subtract
                                   ).then_inc(ln2_out, 1)
                pool.wait_ge(ln2_out, 2 * g + 1)
                pool.tensor_tensor(z2, z2, rstd[:, 0].rearrange("p (i o) -> p i o", o=1).broadcast_to((P, TM, D)),
                                   ALU.mult).then_inc(ln2_out, 1)

            def step2(g, u, n_x):
                for e in range(1, E, 2):
                    scale_gelu(g, e, u)
                    if e == 3 and n_x == 3:
                        norm2(g + 3)

            for g in range(3):
                norm2(g)
            step2(0, 0, 3)
            step2(1, 1, 3)
            with pool.Fori(1, MS // 2 - 2) as j:
                for u in range(2):
                    step2(2 * j + u, u, 3)
            step2(MS - 4, 0, 3)
            step2(MS - 3, 1, 2)
            step2(MS - 2, 0, 1)
            step2(MS - 1, 1, 0)

        @block.scalar
        def _(act):
            def col(v, n):
                return v.rearrange("(p o) -> p o", o=1)
            act.dma_start(pig[:], pi_logit.rearrange("(o h) -> o h", o=1).broadcast_to((DH, H))
                          ).then_inc(set_dma, 16)
            act.dma_start(bias_in[:, 0:1], col(log_xi, H)).then_inc(set_dma, 16)
            act.dma_start(bias_in[:, 1:2], col(e_logit, H)).then_inc(set_dma, 16)
            act.dma_start(sg[:, 0], gates1.rearrange("(o e) -> o e", o=1).broadcast_to((P, E))).then_inc(set_dma, 16)
            act.dma_start(sg[:, 1], gates2.rearrange("(o e) -> o e", o=1).broadcast_to((P, E))).then_inc(set_dma, 16)
            act.wait_ge(set_dma, 16 * N_SMALL)
            act.activation(pig[:], pig[:], ACT.Tanh, scale=0.5).then_inc(set_act, 1)
            act.activation(sg[:], sg[:], ACT.Tanh, scale=0.5).then_inc(set_act, 1)
            act.activation(bias_in[:, 1:2], bias_in[:, 1:2], ACT.Tanh, scale=0.5).then_inc(set_act, 1)
            act.activation(bias_in[:, 0:1], bias_in[:, 0:1], ACT.Exp, scale=-1.0).then_inc(set_act, 1)
            act.wait_ge(set_dve, SIN_READY)
            act.activation(red[:], red[:], ACT.Sin).then_inc(set_act, 1)

            def evac_norm(b, par):
                act.wait_ge(xzT_out, b + 1)
                if not isinstance(b, int) or b > 1:
                    act.wait_ge(n1s_done, b - 1)
                act.activation(xnT[:], ps[:, G0, 0:S], ACT.Copy).then_inc(xnT_done, 1)
                act.activation(n1T[:, par], ps[:, G0, S:2 * S], ACT.Identity, bias=lnp[:, 1:2],
                               scale=lnp[:, 0:1]).then_inc(n1T_done, 1)
                act.wait_ge(n1T_done, b + 1)
                act.activation(sqT[:, 0:S], n1T[:, par], ACT.Square).then_inc(sq_done, 1)

            def evac_logits(b):
                act.wait_ge(lgT_out, b + 1)
                act.activation(lgT[0:E, 0:S], ps[0:E, G0, 0:S], ACT.Copy).then_inc(lgT_done, 1)
                act.activation(lgT[32:32 + E, 0:S], ps[32:32 + E, G0, 0:S], ACT.Copy).then_inc(lgT_done, 1)

            def evac_v(b, par):
                act.wait_ge(v_out, b + 1)
                act.activation(vst[:, par, :, :, 0:DH],
                               ps[:, QKB, 0:T * D].rearrange("p (i h d) -> p i h d", i=T, d=DH),
                               ACT.Copy).then_inc(v_done, 1)

            def gate_tanh(b):
                act.wait_ge(tanh_in, b + 1)
                act.activation(gt[:, 9, 0:T], gt[:, 1, 0:T], ACT.Tanh, scale=0.5).then_inc(tanh_out, 1)

            def evac_weights(b):
                act.wait_ge(rwT_out, b + 1)
                act.wait_ge(rw_stored, 16 * b)
                act.activation(rwT[:, 0:S], ps[0:E, S1[1], 0:S], ACT.Copy).then_inc(rwT_done, 1)

            def evac_max(b):
                act.wait_ge(mT_out, b + 1)
                act.wait_ge(max_in, 16 * b)
                act.activation(mT[:], ps[0:3 * H, S1[0], 0:S // 2].bitcast(BF16), ACT.Copy).then_inc(mT_done, 1)

            def exps(n, k):
                G, i = divmod(k, 3)
                act.wait_ge(s2_out, UNITS * n + k + 1)
                if i == 0:
                    act.wait_ge(pv_out, NG * n + max(G - 1, 0))
                act.activation(pr[:, G % 2, i], ps[:, S2[k % 2]], ACT.Exp).then_inc(exp_done, 1)

            def evac_pv(n, G):
                act.wait_ge(pv_out, NG * n + G + 1)
                act.wait_ge(ot_out, NG * n + max(G - 1, 0))
                act.activation(ov[:, G % 2], ps[:, PVB, 0:S], ACT.Copy).then_inc(ov_done, 1)

            def evac_qk(n):
                act.wait_ge(qk_out, n + 1)
                act.activation(qT[:], ps[:, QKB, 0:S], ACT.Copy, scale=D ** -0.5).then_inc(qkT_done, 1)
                act.activation(kT[:], ps[:, QKB, S:2 * S], ACT.Copy).then_inc(qkT_done, 1)

            def soft_exp(n):
                act.wait_ge(smax_done, 2 * n + 2)
                act.activation(sp[:, 0:P], ps[:, G1, 0:P], ACT.Exp, bias=smx[:, 1, 0:1],
                               accum_out=smx[:, 2, 0:1]).then_inc(sexp_done, 1)
                act.activation(sp[:, P:3 * P], ps[:, G1, P:3 * P], ACT.Exp, bias=smx[:, 1, 1:2],
                               accum_out=smx[:, 2, 1:2]).then_inc(sexp_done, 1)

            def evac_soft(n):
                act.wait_ge(spT_out, n + 1)
                act.activation(spT[:], ps[:, G1, 0:3 * P], ACT.Copy).then_inc(spT_done, 1)

            def evac_ve(n):
                act.wait_ge(ve_out, n + 1)
                act.activation(vs[:], ps[:, QKB, 0:T * D].rearrange("p (i c) -> p i c", i=T),
                               ACT.Copy).then_inc(ve_done, 1)

            def evac_att(n):
                act.wait_ge(attT_out, n + 1)
                act.activation(attT[:], ps[:, G0, 0:S], ACT.Copy).then_inc(attT_done, 1)

            def evac_av(n):
                act.wait_ge(av_out, n + 1)
                act.activation(avT[:], ps[:, G1, 0:S], ACT.Copy).then_inc(av_done, 1)

            def step(n, u, n_x):
                if n_x >= 2:
                    evac_norm(n + 2, u)
                for k in range(3):
                    exps(n, k)
                if n_x >= 2:
                    evac_logits(n + 2)
                for k in range(3, 8):
                    exps(n, k)
                    if k in (4, 6):
                        evac_pv(n, k // 2 - 2)
                evac_qk(n)
                exps(n, 8)
                evac_pv(n, 2)
                if n_x >= 2:
                    gate_tanh(n + 2)
                exps(n, 9)
                soft_exp(n)
                exps(n, 10)
                exps(n, 11)
                evac_soft(n)
                evac_pv(n, 3)
                evac_ve(n)
                evac_av(n)
                if n_x >= 2:
                    evac_weights(n + 2)
                    evac_v(n + 2, u)
                if n_x:
                    evac_max(n + 1)
                evac_att(n)

            for b in range(2):
                evac_norm(b, b)
                evac_logits(b)
                evac_v(b, b)
                gate_tanh(b)
                evac_weights(b)
            evac_max(0)
            step(0, 0, 3)
            step(1, 1, 3)
            with act.Fori(1, NB // 2 - 2) as j:
                for u in range(2):
                    step(2 * j + u, u, 3)
            step(NB - 4, 0, 3)
            step(NB - 3, 1, 2)
            step(NB - 2, 0, 1)
            step(NB - 1, 1, 0)

            act.wait_ge(snorm_done, NB)
            act.activation(smx[:, 0], smx[:, 3], ACT.Gelu).then_inc(set_act, 1)

            def evac_norm2(g):
                act.wait_ge(zT2_out, g + 1)
                act.wait_ge(n2T_done, g)
                act.activation(n2Tn, ps[:, G0], ACT.Identity, bias=lnp[:, 3:4],
                               scale=lnp[:, 2:3]).then_inc(n2Tn_done, 1)
                act.wait_ge(n2Tn_done, g + 1)
                act.activation(sqT[:], n2Tn, ACT.Square).then_inc(sq2_done, 1)

            def place_norm2(g, par):
                if not isinstance(g, int) or g > 1:
                    act.wait_ge(up_out, E * (g - 1))
                act.activation(n2T[:, par], n2Tn, ACT.Copy).then_inc(n2T_done, 1)

            def evac_logits2(g):
                act.wait_ge(lgT2_out, g + 1)
                act.activation(lgT[0:E], ps[0:E, G1], ACT.Copy).then_inc(lgT2_done, 1)
                act.activation(lgT[32:32 + E], ps[32:32 + E, G1], ACT.Copy).then_inc(lgT2_done, 1)

            def gate_tanh2(g):
                act.wait_ge(tanh2_in, g + 1)
                act.activation(gt[:, 9], gt[:, 1], ACT.Tanh, scale=0.5).then_inc(tanh2_out, 1)

            def evac_weights2(g):
                act.wait_ge(rwT2_out, g + 1)
                act.wait_ge(rw2_stored, 16 * g)
                act.activation(rwT[:], ps[0:E, QKB], ACT.Copy).then_inc(rwT2_done, 1)

            def gelu(g, e):
                act.wait_ge(up_out, E * g + e + 1)
                if e % 2:
                    act.wait_ge(hgs2_done, E // 2 * g + e // 2)
                else:
                    act.wait_ge(hgs_done, E // 2 * g + e // 2)
                act.activation(hg[:, e % 2], ps[:, UP[e % 3]], ACT.Gelu).then_inc(gelu_done, 1)

            def step2(g, u, n_x):
                for e in range(E):
                    if n_x >= 2 and e == 5:
                        gate_tanh2(g + 2)
                    gelu(g, e)
                if n_x >= 2:
                    place_norm2(g + 2, u)
                if n_x == 3:
                    evac_norm2(g + 3)
                if n_x >= 2:
                    evac_weights2(g + 2)
                if n_x == 3:
                    evac_logits2(g + 3)

            for g in range(3):
                evac_norm2(g)
                evac_logits2(g)
                if g < 2:
                    gate_tanh2(g)
                    evac_weights2(g)
                    place_norm2(g, g)
            step2(0, 0, 3)
            step2(1, 1, 3)
            with act.Fori(1, MS // 2 - 2) as j:
                for u in range(2):
                    step2(2 * j + u, u, 3)
            step2(MS - 4, 0, 3)
            step2(MS - 3, 1, 2)
            step2(MS - 2, 0, 1)
            step2(MS - 1, 1, 0)

        @block.vector
        def _(dve):
            def layer_norm(b, par):
                c = Chain(dve, ln_chain, b, 2 * LN_LINKS)
                dve.wait_ge(x_in, 16 * (b + 1))
                dve.wait_ge(xzT_out, b)
                dve.wait_ge(keep_done, b)
                for rnd, src in enumerate((xt[:, par], xn[:])):
                    for i in range(T):
                        dve.bn_stats(bst[:, rnd, i], src[:, i])
                    dve.drain()
                    for i in range(T):
                        ins = dve.bn_aggr(bmv[:, rnd, i], bst[:, rnd, i])
                    c.add(ins)
                    yield
                    c.wait()
                    c.add(dve.tensor_scalar(vstd[:, 0, 0:T], bmv[:, rnd, 0:T, 1], EPS, None, ALU.add))
                    yield
                    c.wait()
                    yield from rsqrt(dve, c, rstd[:, rnd, 0:T], vstd[:, 0, 0:T], vstd[:, 1, 0:T])
                    if rnd == 0:
                        for i in range(T):
                            ins = dve.tensor_scalar(xn[:, i], src[:, i], bmv[:, 0, i, 0:1], rstd[:, 0, i:i + 1],
                                                    ALU.subtract, ALU.mult)
                        ins.then_inc(ln_out, 1)
                        yield
                        dve.wait_ge(ln_out, b + 1)
                c.close()

            ch = Chain(dve, set_dve, 0, N_SET_DVE)
            ch.add(dve.memset(ones_e[:], 1.0))
            ch.add(dve.memset(ones_p[:], 1.0))
            ch.add(dve.memset(ones_b[:], 1.0))
            ch.add(dve.memset(zeros_b[:], 0.0))
            ch.add(dve.memset(lgT[:], 0.0))
            ch.add(dve.memset(mpart[:], 0.0))
            ch.add(dve.memset(vst[:], 0.0))
            run(layer_norm(0, 0))
            dve.wait_ge(ld_const, 16 * N_CONST)
            dve.wait_ge(set_act, 4)
            ch.link(dve.tensor_scalar(pig[:], pig[:], 0.5, 0.5, ALU.mult, ALU.add))
            ch.link(dve.tensor_scalar(theta[:], theta[:], pig[:, 0:1], None, ALU.mult))
            ROUND = 1.5 * 2.0 ** 23
            C1 = 6.28125
            C2 = float(np.float32(np.round((2 * np.pi - C1) * 2 ** 22) / 2 ** 22))
            C3 = float(2 * np.pi - C1 - C2)
            LIM = 3.1415925
            ch.add(dve.tensor_scalar(trn[:, 0], theta[:], 0.5 / np.pi, 0.25, ALU.mult, ALU.add))
            ch.link(dve.tensor_scalar(trn[:, 1], theta[:], 0.5 / np.pi, None, ALU.mult))
            ch.link(dve.tensor_scalar(trn[:], trn[:], ROUND, None, ALU.add))
            ch.link(dve.tensor_scalar(trn[:], trn[:], -ROUND, None, ALU.add))
            for i in range(2):
                ins = dve.scalar_tensor_tensor(red[:, i], trn[:, i], -C1, theta[:], ALU.mult, ALU.add)
            ch.link(ins)
            ch.link(dve.scalar_tensor_tensor(red[:], trn[:], -C2, red[:], ALU.mult, ALU.add))
            ch.link(dve.scalar_tensor_tensor(red[:], trn[:], -C3, red[:], ALU.mult, ALU.add))
            ch.link(dve.tensor_scalar(red[:, 0], red[:, 0], float(np.pi / 2), None, ALU.add))
            ch.link(dve.tensor_scalar(red[:], red[:], LIM, -LIM, ALU.min, ALU.max))
            assert ch.k == SIN_READY, ch.k
            dve.wait_ge(set_act, 5)
            qs = DH ** -0.5
            ch.add(dve.tensor_scalar(cs[:, 0, 0], red[:, 0], qs, None, ALU.mult))
            ch.add(dve.tensor_scalar(cs[:, 0, 1], red[:, 1], sin_sign[:, 0:1], qs, ALU.mult, ALU.mult))
            ch.add(dve.tensor_copy(cs[:, 1, 0], red[:, 0]))
            ch.add(dve.tensor_scalar(cs[:, 1, 1], red[:, 1], sin_sign[:, 0:1], None, ALU.mult))
            ch.link(dve.tensor_scalar(bias_in[:, 1:2], bias_in[:, 1:2], 0.5, 0.5, ALU.mult, ALU.add))
            ch.link(dve.tensor_tensor(bias_in[:, 0:1], bias_in[:, 0:1], bias_in[:, 1:2], ALU.mult))
            ch.link(dve.tensor_scalar(cb[:, 0], cpos[:], bias_in[:, 0:1], None, ALU.mult))
            ch.link(dve.tensor_scalar(cb[:, 1], cb[:, 0], -1.0, None, ALU.mult))
            for part in range(3):
                ch.link(dve.tensor_copy(cbp[:, :, part], cb[:]))
                if part < 2:
                    ch.link(dve.tensor_tensor(cb[:], cb[:], cbp[:, :, part], ALU.subtract))
            for h in range(HG):
                ch.add(dve.tensor_copy(mask_qk[:, h], mask_in[:, 0]))
                ch.add(dve.tensor_copy(mask_kq[:, h], mask_in[:, 1]))
            ch.add(dve.tensor_copy(identb[:], ident[:]))
            ch.add(dve.memset(vst[:, :, :, :, DH:DH + 1], 1.0))
            ch.add(dve.tensor_scalar(sg[:], sg[:], 0.5, 0.5, ALU.mult, ALU.add))
            ch.link(dve.tensor_tensor(gt[:, 0:2, 0], sims[:], sims[:], ALU.mult))
            dve.wait_ge(set_pe, 1)
            ch.link(dve.tensor_scalar(gt[:, 2:4, 0], ps[:, G0, 0:2 * E].rearrange("p (a e) -> p a e", a=2),
                                      NORM2, None, ALU.max))
            run(rsqrt(dve, ch, gt[:, 4:6, 0], gt[:, 2:4, 0], gt[:, 6:8, 0]))
            ch.link(dve.tensor_tensor(simn[:], sims[:], gt[:, 4:6, 0], ALU.mult))
            ch.close()

            def rotate(b, beside=None):
                c = Chain(dve, rot_chain, b, ROT_LINKS, beside)
                dve.wait_ge(rot_q_out, b + 1)
                c.link(dve.tensor_tensor(rott[:, 0], ps[:, G1].rearrange("p (a t) -> p a t", a=2), cs[:, 0], ALU.mult))
                c.add(dve.tensor_tensor(rot[:, 0], rott[:, 0, 0], rott[:, 0, 1], ALU.add))
                dve.wait_ge(rot_k_out, b + 1)
                c.link(dve.tensor_tensor(rott[:, 1], ps[:, G1].rearrange("p (a t) -> p a t", a=2), cs[:, 1], ALU.mult))
                c.link(dve.tensor_tensor(rot[:, 1], rott[:, 1, 0], rott[:, 1, 1], ALU.add))
                dve.wait_ge(parts_stored, 16 * b)
                c.link(dve.tensor_copy(parts[:, 0], rot[:]))
                c.link(dve.tensor_tensor(rres[:], rot[:], parts[:, 0], ALU.subtract))
                c.link(dve.tensor_copy(parts[:, 1], rres[:]))
                dve.tensor_tensor(parts[:, 2], rres[:], parts[:, 1], ALU.subtract).then_inc(parts_out, 1)
                c.close()

            def gating(b, nt, which, q, beside=None):
                chain, lg_out, lg_read, tanh_in, tanh_out, rwT_out, rw_out = q
                c = Chain(dve, chain, b, GATE_LINKS, beside)
                L, Dm, A, B2, C2_, F = (gt[:, k, 0:nt] for k in range(6))
                th = gt[:, 9, 0:nt]
                m1, m2, mc, rn, ina, tot = (gs[:, k, 0:nt] for k in range(6))

                def bc(v):
                    return v.rearrange("p (t o) -> p t o", o=1).broadcast_to((P, nt, E))
                rk = rank[:].rearrange("p (o e) -> p o e", o=1).broadcast_to((P, nt, E))
                sgb = sg[:, which:which + 1].broadcast_to((P, nt, E))
                lg = ps[:, LGB[which], 0:P * nt].rearrange("p (i k) -> p i k", k=P)
                dve.wait_ge(lg_out, b + 1)
                c.link(dve.tensor_scalar(rn, lg[:, :, 32], NORM2, None, ALU.max))
                for _ in rsqrt(dve, c, gs[:, 6, 0:nt], rn, gs[:, 7, 0:nt]):
                    c.beside(c.k)
                dve.tensor_tensor(L, lg[:, :, 0:E], bc(gs[:, 6, 0:nt]), ALU.mult).then_inc(lg_read, 1)
                dve.wait_ge(lg_read, b + 1)
                c.link(dve.tensor_tensor(L, L, sgb, ALU.subtract))
                c.link(dve.tensor_reduce(m1, L, AX_X, ALU.max))
                dve.tensor_tensor(Dm, L, bc(m1), ALU.subtract).then_inc(tanh_in, 1)
                dve.wait_ge(tanh_in, b + 1)
                c.link(dve.scalar_tensor_tensor(A, Dm, 0.0, rk, ALU.is_ge, ALU.mult))
                c.link(dve.tensor_reduce(mc, A, AX_X, ALU.max))
                c.link(dve.tensor_tensor(A, A, bc(mc), ALU.is_equal))
                c.link(dve.scalar_tensor_tensor(B2, A, -BIG, L, ALU.mult, ALU.add))
                c.link(dve.tensor_reduce(m2, B2, AX_X, ALU.max))
                c.link(dve.tensor_tensor(C2_, B2, bc(m2), ALU.is_equal))
                c.link(dve.tensor_tensor(C2_, C2_, rk, ALU.mult))
                c.link(dve.tensor_reduce(mc, C2_, AX_X, ALU.max))
                c.link(dve.tensor_tensor(C2_, C2_, bc(mc), ALU.is_equal))
                c.add(dve.tensor_scalar(ina, m1, 0.0, None, ALU.is_le))
                c.link(dve.tensor_tensor(F, A, C2_, ALU.add))
                c.add(dve.tensor_tensor(F, F, bc(ina), ALU.mult))
                dve.wait_ge(tanh_out, b + 1)
                c.add(dve.tensor_scalar(A, th, 1.0, None, ALU.add))
                c.link(dve.tensor_scalar(B2, th, -1.0, 1.0, ALU.mult, ALU.add))
                c.link(dve.reciprocal(B2, B2))
                c.link(dve.tensor_tensor(A, A, B2, ALU.mult))
                c.link(dve.scalar_tensor_tensor(A, L, 0.0, A, ALU.is_gt, ALU.mult))
                dve.wait_ge(rwT_out, b)
                fin = gt[:, 6, 0:nt]
                dve.tensor_tensor(F, A, F, ALU.add).then_inc(rw_out, 1)
                dve.wait_ge(rw_out, 3 * b + 1)
                dve.tensor_reduce(tot, F, AX_X, ALU.add).then_inc(rw_out, 1)
                dve.wait_ge(rw_out, 3 * b + 2)
                c.link(dve.reciprocal(tot, tot))
                dve.tensor_tensor(fin, F, bc(tot), ALU.mult).then_inc(rw_out, 1)
                c.close()

            LGB = (G0, G0)
            gate1 = (gate_chain, lg_out, lg_read, tanh_in, tanh_out, rwT_out, rw_out)
            gate2 = (gate2_chain, lg2_out, lg2_read, tanh2_in, tanh2_out, rwT2_out, rw2_out)

            def row_max(b, k):
                G, i = divmod(k, 3)
                dve.wait_ge(s1_out, UNITS * b + k + 1)
                if k == 0:
                    dve.wait_ge(max_chain, (MAX_LINKS + 1) * b)
                n = HG if i == 0 else 2
                h = HG * G + (0 if i < 2 else 2)
                dve.tensor_reduce(mx[:, min(i, 1), h:h + n], ps[:, S1[k % 2]].rearrange("p (h t) -> p h t", h=n),
                                  AX_X, ALU.max).then_inc(s1_read, 1)

            def max_parts(b):
                c = Chain(dve, max_chain, b, MAX_LINKS + 1)
                mp = [mpart[:, :, k * H:(k + 1) * H] for k in range(3)]
                dve.wait_ge(s1_read, UNITS * (b + 1))
                dve.wait_ge(mT_out, b)
                c.link(dve.tensor_scalar(mp[0], mx[:], -1.0, None, ALU.mult))
                c.link(dve.scalar_tensor_tensor(mres[:], mx[:], -1.0, mp[0], ALU.mult, ALU.subtract))
                c.link(dve.tensor_copy(mp[1], mres[:]))
                c.add(dve.tensor_tensor(mp[2], mres[:], mp[1], ALU.subtract))
                c.close()

            def normalise(n, G):
                dve.wait_ge(ot_out, NG * n + G + 1)
                o = ps[:, PVB, S:2 * S].rearrange("p (i h r) -> p i h r", i=T, r=32)
                c = Chain(dve, ot_read, NG * n + G, 2)
                c.link(dve.reciprocal(rden[:], o[:, :, :, DH]))
                if G == 0:
                    dve.wait_ge(attT_out, n)
                for i in range(T):
                    ins = dve.tensor_tensor(
                        att[:, i, DH * HG * G:DH * HG * (G + 1)].rearrange("p (h d) -> p h d", d=DH),
                        o[:, i, :, 0:DH],
                        rden[:, i].rearrange("p (h o) -> p h o", o=1).broadcast_to((P, HG, DH)), ALU.mult)
                c.add(ins)
                c.close()

            def soft_max(n):
                dve.wait_ge(ss_out, n + 1)
                dve.tensor_reduce(smx[:, 0, 0:1], ps[:, G1, 0:P], AX_X, ALU.max)
                dve.tensor_reduce(smx[:, 0, 1:2], ps[:, G1, P:3 * P], AX_X, ALU.max).then_inc(smax_done, 1)
                dve.wait_ge(smax_done, 2 * n + 1)
                dve.tensor_scalar(smx[:, 1], smx[:, 0], -1.0, None, ALU.mult).then_inc(smax_done, 1)

            def soft_norm(n):
                dve.wait_ge(sexp_done, 2 * n + 2)
                dve.reciprocal(smx[:, 3], smx[:, 2]).then_inc(snorm_chain, 1)
                dve.wait_ge(snorm_chain, n + 1)
                dve.tensor_scalar(sp[:, 0:P], sp[:, 0:P], smx[:, 3, 0:1], None, ALU.mult)
                dve.tensor_scalar(sp[:, P:3 * P], sp[:, P:3 * P], smx[:, 3, 1:2], None, ALU.mult
                                  ).then_inc(snorm_done, 1)

            def scale_att(n, u, e, ne):
                if e == 0:
                    dve.wait_ge(oe_out, n)
                    dve.wait_ge(rep_in, 16 * (n + 1))
                    dve.wait_ge(av_done, n + 1)
                dve.tensor_tensor(ats[:, e:e + ne], rep[:, u, e:e + ne],
                                  avT[:].rearrange("p (o t) -> p o t", o=1).broadcast_to((P, ne, S)), ALU.mult
                                  ).then_inc(ats_done, 1)

            def add_x(n, u):
                dve.wait_ge(wo_out, n + 1)
                dve.wait_ge(xr_in, 16 * (n + 1))
                dve.tensor_tensor(xa[:, u], xr[:, u], ps[:, G0, 0:T * D].rearrange("p (i c) -> p i c", i=T),
                                  ALU.add).then_inc(xa_done, 1)

            def add_hs(n, u):
                dve.wait_ge(oe_out, n + 1)
                dve.wait_ge(keep_done, n + 1)
                hv = hs[:, T * n:T * n + T] if isinstance(n, int) else hs[:, bass.ds(n * T, T)]
                dve.tensor_tensor(hv, hv, ps[:, G1, 0:T * D].rearrange("p (i c) -> p i c", i=T),
                                  ALU.add).then_inc(hs_done, 1)
                dve.wait_ge(hs_done, n + 1)
                dve.wait_ge(xa_done, n + 1)
                dve.wait_ge(base_stored, 16 * n)
                dve.tensor_tensor(bs[:, u], hv, xa[:, u], ALU.add).then_inc(base_done, 1)

            def step(n, u, n_x):
                def next_max(k):
                    if n_x:
                        row_max(n + 1, k)

                def beside_rotation(k):
                    if k in (1, 3, 5):
                        next_max((1, 3, 5).index(k))

                norm = layer_norm(n + 3, 1 - u) if n_x == 3 else iter(())

                def beside_gating(k):
                    next(norm, None)
                    if k in GATE_MAX_AT:
                        next_max(4 + GATE_MAX_AT.index(k))
                    if k in (12, 22):
                        normalise(n, 1 + (12, 22).index(k))
                    if k == 16:
                        soft_max(n)
                    if k == 20:
                        soft_norm(n)
                if n_x >= 2:
                    rotate(n + 2, beside_rotation)
                    normalise(n, 0)
                    next_max(3)
                    gating(n + 2, T, 0, gate1, beside_gating)
                    run(norm)
                else:
                    for k in range(1, ROT_LINKS + 1):
                        beside_rotation(k)
                    normalise(n, 0)
                    next_max(3)
                    for k in range(1, GATE_LINKS + 1):
                        beside_gating(k)
                next_max(11)
                normalise(n, 3)
                if n_x:
                    max_parts(n + 1)
                for e, ne in ATS_CHUNKS:
                    scale_att(n, u, e, ne)
                add_x(n, u)
                add_hs(n, u)

            for b in range(2):
                norm = layer_norm(b + 1, 1 - b)
                rotate(b)
                gating(b, T, 0, gate1, lambda k, norm=norm: next(norm, None))
                run(norm)
            for k in range(UNITS):
                row_max(0, k)
            max_parts(0)
            step(0, 0, 3)
            step(1, 1, 3)
            with dve.Fori(1, NB // 2 - 2) as j:
                for u in range(2):
                    step(2 * j + u, u, 3)
            step(NB - 4, 0, 3)
            step(NB - 3, 1, 2)
            step(NB - 2, 0, 1)
            step(NB - 1, 1, 0)

            def layer_norm2(g):
                c = Chain(dve, ln2_chain, g, LN_LINKS)
                dve.wait_ge(ln2_out, 2 * g)
                for i in range(TM):
                    h = hs[:, TM * g + i] if isinstance(g, int) else hs[:, bass.ds(g * TM + i, 1)].rearrange(
                        "p o c -> p (o c)")
                    dve.bn_stats(bst[:, 0, i], h)
                dve.drain()
                for i in range(TM):
                    ins = dve.bn_aggr(bmv[:, 0, i], bst[:, 0, i])
                c.add(ins)
                yield
                c.wait()
                c.add(dve.tensor_scalar(vstd[:, 0], bmv[:, 0, :, 1], EPS, None, ALU.add))
                yield
                c.wait()
                yield from rsqrt(dve, c, rstd[:, 0], vstd[:, 0], vstd[:, 1])
                c.close()

            def scale_gelu(g, e, par):
                dve.wait_ge(gelu_done, E * g + e + 1)
                dve.wait_ge(rep2_in, 16 * (g + 1))
                dve.wait_ge(moe_out, E * g + max(e - 1, 0))
                dve.tensor_tensor(hgs[:, 0], hg[:, 0], rep2[par][:, e], ALU.mult).then_inc(hgs_done, 1)

            def finish(g, u):
                dve.wait_ge(moe_out, E * (g + 1))
                dve.wait_ge(out_stored, 16 * g)
                dve.wait_ge(base_in, 16 * (g + 1))
                dve.tensor_tensor(ot[:, u], bt[:, u], ps[:, MOE[u]].rearrange("p (i c) -> p i c", i=TM),
                                  ALU.add).then_inc(out_done, 1)

            def step2(g, u, n_x):
                scale_gelu(g, 0, u)
                if not isinstance(g, int) or g > 0:
                    finish(g - 1, 1 - u)

                norm = layer_norm2(g + 3) if n_x == 3 else iter(())

                def beside_gating(k):
                    next(norm, None)
                    if k in (4, 15, 27):
                        scale_gelu(g, 2 + 2 * (4, 15, 27).index(k), u)

                if n_x >= 2:
                    gating(g + 2, TM, 1, gate2, beside_gating)
                else:
                    for e in (2, 4, 6):
                        scale_gelu(g, e, u)
                run(norm)

            dve.wait_ge(base_done, NB)
            run(layer_norm2(0))
            for g in range(2):
                norm = layer_norm2(g + 1)
                gating(g, TM, 1, gate2, lambda k, norm=norm: next(norm, None))
                run(norm)
            step2(0, 0, 3)
            step2(1, 1, 3)
            with dve.Fori(1, MS // 2 - 2) as j:
                for u in range(2):
                    step2(2 * j + u, u, 3)
            step2(MS - 4, 0, 3)
            step2(MS - 3, 1, 2)
            step2(MS - 2, 0, 1)
            step2(MS - 1, 1, 0)
            finish(MS - 1, 1)

        @block.tensor
        def _(pe):
            mm = pe.matmul
            pe.wait_ge(set_dve, N_SET_DVE - 12)
            mm(ps[:, G0, 0:2 * E], ones_p[:], gt[:, 0:2, 0], start=True, stop=True).then_inc(set_pe, 1)
            pe.wait_ge(set_dve, N_SET_DVE)
            pe.wait_ge(ld_w, 16 * N_W)

            def norm_T(b, free):
                free()
                pe.wait_ge(ln_out, b + 1)
                pe.wait_ge(zp_done, 2 * (b + 1))
                for k, src in enumerate((xn[:], zt[:])):
                    for i in range(T):
                        ins = pe.transpose(ps[:, G0, (T * k + i) * P:(T * k + i + 1) * P], src[:, i], ident[:])
                ins.then_inc(xzT_out, 1)

            def proj(b, side, prev):
                pe.wait_ge(xnT_done, b + 1)
                prev()
                for k in range(2):
                    ins = mm(ps[:, G1, k * S:(k + 1) * S], wa[:, 2 * side + k], xnT[:], start=True, stop=True)
                ins.then_inc((rot_q_out, rot_k_out)[side], 1)

            def logits_T(b, par):
                pe.wait_ge(sq_done, b + 1)
                mm(ps[0:E, G0, 0:S], simn[:, 0], n1T[:, par], start=True, stop=True)
                mm(ps[32:32 + E, G0, 0:S], ones_e[:], sqT[:, 0:S], start=True, stop=True).then_inc(lgT_out, 1)

            def logits(b):
                pe.wait_ge(lgT_done, 2 * (b + 1))
                for i in range(T):
                    ins = pe.transpose(ps[:, G0, i * P:(i + 1) * P], lgT[:, i * P:(i + 1) * P], ident[:])
                ins.then_inc(lg_out, 1)

            def proj_v(b, old):
                pe.wait_ge(xnT_done, b + 1)
                if old:
                    pe.wait_ge(ve_done, b - 1)
                else:
                    pe.wait_ge(v_done, b)
                for i in range(T):
                    ins = mm(ps[:, QKB, i * D:(i + 1) * D], xnT[:, i * P:(i + 1) * P], wa[:, 4], start=True, stop=True)
                ins.then_inc(v_out, 1)

            def weights_T(b, old):
                pe.wait_ge(rw_out, 3 * (b + 1))
                if old:
                    pe.wait_ge(s1_read, UNITS * b)
                else:
                    pe.wait_ge(rwT_done, b)
                for i in range(T):
                    ins = pe.transpose(ps[0:E, S1[1], i * P:(i + 1) * P], gt[:, 6, i], ident[:])
                ins.then_inc(rwT_out, 1)

            def unit1(b, par, k):
                G, i = divmod(k, 3)
                if k == 1:
                    pe.wait_ge(rwT_done, b + 1 if not isinstance(b, int) or b else 2)
                if k == 0:
                    pe.wait_ge(stack_in, 16 * 7 * (b + 1 if not isinstance(b, int) or b else 2))
                if k == 0:
                    pe.wait_ge(mT_done, b)
                pe.wait_ge(s1_read, UNITS * b + max(k - 1, 0))
                bank = ps[:, S1[k % 2]]
                if i == 0:
                    mm(bank, identb[:], mask_qk[:].rearrange("p h t -> p (h t)"), start=True, stop=False,
                       skip_group_check=True)
                    for h in range(HG):
                        hh = HG * G + h
                        ins = mm(bank[:, h * P:(h + 1) * P], qst[0:KR, par, hh, 0:P], kst[0:KR, par, hh, 0:P],
                                 start=False, stop=True, skip_group_check=True)
                else:
                    mm(bank.rearrange("p (h t) -> p h t", h=2)[:, :, P:S], identb[:], mask_qk[:, 0:2],
                       start=True, stop=False, skip_group_check=True)
                    for h in range(2):
                        hh = HG * G + 2 * (i - 1) + h
                        ins = mm(bank[:, h * S:(h + 1) * S], qst[0:KR, par, hh, P:S], kst[0:KR, par, hh, :],
                                 start=False, stop=True, skip_group_check=True)
                ins.then_inc(s1_out, 1)

            def max_T(b):
                pe.wait_ge(max_chain, (MAX_LINKS + 1) * (b + 1))
                pv = ps[:, S1[0], 0:S // 2].bitcast(BF16)
                for i in range(T):
                    ins = pe.transpose(pv[:, i * P:(i + 1) * P], mpart[:, i], identb[:])
                ins.then_inc(mT_out, 1)

            def unit2(n, u, k):
                G, i = divmod(k, 3)
                if k == 0:
                    pe.wait_ge(max_in, 16 * (n + 1))
                pe.wait_ge(exp_done, UNITS * n + max(k - 1, 0))
                bank = ps[:, S2[k % 2]]
                if i < 2:
                    mm(bank.rearrange("p (h t) -> p h t", h=2)[:, :, 0:P], identb[:], mask_kq[:, 0:2],
                       start=True, stop=False, skip_group_check=True)
                    for h in range(2):
                        hh = HG * G + 2 * i + h
                        ins = mm(bank[:, h * S:(h + 1) * S], kst[0:KR, u, hh, 0:P], qst[0:KR, u, hh, :],
                                 start=False, stop=True, skip_group_check=True)
                else:
                    mm(bank, identb[:], mask_kq[:].rearrange("p h t -> p (h t)"), start=True, stop=False,
                       skip_group_check=True)
                    for h in range(HG):
                        hh = HG * G + h
                        ins = mm(bank[:, h * P:(h + 1) * P], kst[0:KR, u, hh, P:S], qst[0:KR, u, hh, P:S],
                                 start=False, stop=True, skip_group_check=True)
                ins.then_inc(s2_out, 1)

            def pv(n, u, G):
                pe.wait_ge(exp_done, UNITS * n + 3 * (G + 1))
                pe.wait_ge(ot_read, 2 * (NG * n + G))
                if G == 0:
                    pe.wait_ge(v_done, n + 1)
                for h in range(HG):
                    mm(ps[32 * h:32 * h + 32, PVB, 0:S], vst[:, u, 0, HG * G + h],
                       pr[:, G % 2, h // 2, (h % 2) * S:(h % 2 + 1) * S], start=True, stop=False,
                       skip_group_check=True)
                for h in range(HG):
                    ins = mm(ps[32 * h:32 * h + 32, PVB, P:S], vst[:, u, 1, HG * G + h],
                             pr[:, G % 2, 2, h * P:(h + 1) * P], start=False, stop=True, skip_group_check=True)
                ins.then_inc(pv_out, 1)

            def out_T(n, G):
                pe.wait_ge(ov_done, NG * n + G + 1)
                for i in range(T):
                    ins = pe.transpose(ps[:, PVB, (T + i) * P:(T + i + 1) * P], ov[:, G % 2, i * P:(i + 1) * P],
                                       ident[:])
                ins.then_inc(ot_out, 1)

            def qk(n, e):
                if e == 0:
                    pe.wait_ge(n1s_done, n + 1)
                    pe.wait_ge(ve_done, n)
                    pe.wait_ge(v_done, min(n + 2, NB) if isinstance(n, int) else n + 2)
                mm(ps[:, QKB, 0:S], wq[:, e], n1s[:, e], start=(e == 0), stop=(e == E - 1), skip_group_check=True)
                ins = mm(ps[:, QKB, S:2 * S], wk[:, e], n1s[:, e], start=False, stop=(e == E - 1),
                         skip_group_check=True)
                if e == E - 1:
                    ins.then_inc(qk_out, 1)

            def ve(n, e):
                if e == 0:
                    pe.wait_ge(qkT_done, 2 * (n + 1))
                for i in range(T):
                    ins = mm(ps[:, QKB, i * D:(i + 1) * D], n1s[:, e, i * P:(i + 1) * P], wv[:, e],
                             start=(e == 0 and i == 0), stop=(e == E - 1), skip_group_check=True)
                if e == E - 1:
                    ins.then_inc(ve_out, 1)

            def soft_scores(n, free):
                pe.wait_ge(qkT_done, 2 * (n + 1))
                free()
                b = ps[:, G1]
                mm(b.rearrange("p (a t) -> p a t", a=2)[:, :, 0:P], identb[:], mask_qk[:, 0:2], start=True,
                   stop=False, skip_group_check=True)
                mm(b[:, 0:P], qT[:, 0:P], kT[:, 0:P], start=False, stop=True, skip_group_check=True)
                mm(b[:, P:3 * P], qT[:, P:S], kT[:], start=False, stop=True, skip_group_check=True
                   ).then_inc(ss_out, 1)

            def soft_T(n):
                pe.wait_ge(snorm_done, n + 1)
                for k in range(3):
                    ins = pe.transpose(ps[:, G1, k * P:(k + 1) * P], sp[:, k * P:(k + 1) * P], ident[:])
                ins.then_inc(spT_out, 1)

            def soft_av(n):
                pe.wait_ge(spT_done, n + 1)
                pe.wait_ge(ve_done, n + 1)
                mm(ps[:, G1, 0:S], vs[:, 0], spT[:, 0:S], start=True, stop=False, skip_group_check=True)
                mm(ps[:, G1, P:S], vs[:, 1], spT[:, S:3 * P], start=False, stop=True, skip_group_check=True
                   ).then_inc(av_out, 1)

            ATS_FIRST = [e for e, _ in ATS_CHUNKS]

            def oe(n, e):
                if e in ATS_FIRST:
                    pe.wait_ge(ats_done, len(ATS_CHUNKS) * n + ATS_FIRST.index(e) + 1)
                for i in range(T):
                    ins = mm(ps[:, G1, i * D:(i + 1) * D], ats[:, e, i * P:(i + 1) * P], wop[:, e],
                             start=(e == 0 and i == 0), stop=(e == E - 1), skip_group_check=True)
                if e == E - 1:
                    ins.then_inc(oe_out, 1)

            def att_T(n, free):
                free()
                pe.wait_ge(ot_read, 2 * NG * (n + 1))
                for i in range(T):
                    ins = pe.transpose(ps[:, G0, i * P:(i + 1) * P], att[:, i], ident[:])
                ins.then_inc(attT_out, 1)

            def att_out(n):
                pe.wait_ge(attT_done, n + 1)
                for i in range(T):
                    ins = mm(ps[:, G0, i * D:(i + 1) * D], attT[:, i * P:(i + 1) * P], wo[:], start=True, stop=True)
                ins.then_inc(wo_out, 1)

            def step(n, u, n_x):
                f = n + 2

                def next_max(k):
                    if n_x:
                        unit1(n + 1, 1 - u, k)

                if n_x >= 2:
                    norm_T(f, lambda: pe.wait_ge(xa_done, n))
                unit2(n, u, 0)
                qk(n, 0)
                unit2(n, u, 1)
                if n_x >= 2:
                    proj(f, 0, lambda: pe.wait_ge(hs_done, n))
                qk(n, 1)
                next_max(0)
                unit2(n, u, 2)
                if n_x >= 2:
                    logits_T(f, u)
                qk(n, 2)
                if n_x >= 2:
                    proj(f, 1, lambda: pe.wait_ge(rot_chain, ROT_LINKS * f + 1))
                next_max(1)
                unit2(n, u, 3)
                if n_x >= 2:
                    logits(f)
                qk(n, 3)
                pv(n, u, 0)
                next_max(2)
                unit2(n, u, 4)
                qk(n, 4)
                next_max(3)
                out_T(n, 0)
                unit2(n, u, 5)
                qk(n, 5)
                next_max(4)
                unit2(n, u, 6)
                pv(n, u, 1)
                next_max(5)
                qk(n, 6)
                next_max(6)
                unit2(n, u, 7)
                out_T(n, 1)
                qk(n, 7)
                next_max(7)
                unit2(n, u, 8)
                soft_scores(n, (lambda: pe.wait_ge(rot_chain, ROT_LINKS * f + 3)) if n_x >= 2 else
                            (lambda: pe.wait_ge(hs_done, n)))
                ve(n, 0)
                next_max(8)
                pv(n, u, 2)
                unit2(n, u, 9)
                ve(n, 1)
                next_max(9)
                unit2(n, u, 10)
                out_T(n, 2)
                ve(n, 2)
                next_max(10)
                unit2(n, u, 11)
                ve(n, 3)
                soft_T(n)
                next_max(11)
                ve(n, 4)
                pv(n, u, 3)
                for e in range(5, E):
                    ve(n, e)
                out_T(n, 3)
                soft_av(n)
                if n_x >= 2:
                    weights_T(f, True)
                    proj_v(f, True)
                if n_x:
                    max_T(n + 1)
                att_T(n, (lambda: pe.wait_ge(lg_read, f + 1)) if n_x >= 2 else (lambda: pe.wait_ge(xa_done, n)))
                oe(n, 0)
                oe(n, 1)
                att_out(n)
                for e in range(2, E):
                    oe(n, e)

            for b in range(2):
                norm_T(b, lambda: pe.wait_ge(lg_read, b))
                proj(b, 0, lambda: pe.wait_ge(rot_chain, ROT_LINKS * b))
                logits_T(b, b)
                proj(b, 1, lambda: pe.wait_ge(rot_chain, ROT_LINKS * b + 1))
                logits(b)
                proj_v(b, False)
                weights_T(b, False)
            pe.wait_ge(set_dma, 16 * (N_SMALL + N_ROWS))
            for k in range(UNITS):
                unit1(0, 0, k)
            max_T(0)
            step(0, 0, 3)
            step(1, 1, 3)
            with pe.Fori(1, NB // 2 - 2) as j:
                for u in range(2):
                    step(2 * j + u, u, 3)
            step(NB - 4, 0, 3)
            step(NB - 3, 1, 2)
            step(NB - 2, 0, 1)
            step(NB - 1, 1, 0)

            def norm_T2(g):
                pe.wait_ge(ln2_out, 2 * (g + 1))
                pe.wait_ge(lg2_read, g)
                for i in range(TM):
                    ins = pe.transpose(ps[:, G0, i * P:(i + 1) * P], z2[:, i], ident[:])
                ins.then_inc(zT2_out, 1)

            def logits_T2(g):
                pe.wait_ge(sq2_done, g + 1)
                mm(ps[0:E, G1], simn[:, 1], n2Tn, start=True, stop=True)
                mm(ps[32:32 + E, G1], ones_e[:], sqT[:], start=True, stop=True).then_inc(lgT2_out, 1)

            def logits2(g):
                pe.wait_ge(lgT2_done, 2 * (g + 1))
                for i in range(TM):
                    ins = pe.transpose(ps[:, G0, i * P:(i + 1) * P], lgT[:, i * P:(i + 1) * P], ident[:])
                ins.then_inc(lg2_out, 1)

            def weights_T2(g):
                pe.wait_ge(rw2_out, 3 * (g + 1))
                pe.wait_ge(rwT2_done, g)
                for i in range(TM):
                    ins = pe.transpose(ps[0:E, QKB, i * P:(i + 1) * P], gt[:, 6, i], ident[:])
                ins.then_inc(rwT2_out, 1)

            def up(g, u, e):
                pe.wait_ge(n2T_done, g + 1)
                pe.wait_ge(gelu_done, E * g + max(e - 2, 0))
                mm(ps[:, UP[e % 3]], w1s[:, e], n2T[:, u], start=True, stop=True).then_inc(up_out, 1)

            def down(g, u, e):
                pe.wait_ge(hgs2_done if e % 2 else hgs_done, E // 2 * g + e // 2 + 1)
                if e == 0:
                    pe.wait_ge(out_done, max(g - 1, 0) if isinstance(g, int) else g - 1)
                for i in range(TM):
                    ins = mm(ps[:, MOE[u], i * D:(i + 1) * D], hgs[:, e % 2, i * P:(i + 1) * P], w2s[:, e],
                             start=(e == 0 and i == 0), stop=(e == E - 1), skip_group_check=True)
                ins.then_inc(moe_out, 1)

            def step2(g, u, n_x):
                up(g, u, 0)
                up(g, u, 1)
                if n_x >= 2:
                    logits2(g + 2)
                for e in range(E):
                    if n_x >= 2 and e == 7:
                        weights_T2(g + 2)
                    down(g, u, e)
                    if e + 2 < E:
                        up(g, u, e + 2)
                    if n_x == 3 and e == 5:
                        norm_T2(g + 3)
                    if n_x == 3 and e == 7:
                        logits_T2(g + 3)

            for g in range(3):
                norm_T2(g)
                logits_T2(g)
                if g < 2:
                    logits2(g)
                    weights_T2(g)
            step2(0, 0, 3)
            step2(1, 1, 3)
            with pe.Fori(1, MS // 2 - 2) as j:
                for u in range(2):
                    step2(2 * j + u, u, 3)
            step2(MS - 4, 0, 3)
            step2(MS - 3, 1, 2)
            step2(MS - 2, 0, 1)
            step2(MS - 1, 1, 0)


def kernel(L0_attn_x, L0_attn_Wqkv, L0_attn_Wo, L0_attn_log_xi, L0_attn_pi_gate_logit, L0_attn_e_gate_logit,
           L0_ffn_ln1_w, L0_ffn_ln1_b, L0_ffn_ln2_w, L0_ffn_ln2_b, L0_ffn_smha_sim, L0_ffn_smha_gates,
           L0_ffn_q_proj, L0_ffn_k_proj, L0_ffn_v_proj, L0_ffn_o_proj, L0_ffn_moe_sim, L0_ffn_moe_gates,
           L0_ffn_w1, L0_ffn_w2):
    import concourse.bacc as bacc
    from concourse.bass_utils import run_bass_kernel_spmd

    wqkv_t = np.ascontiguousarray(L0_attn_Wqkv).T.reshape(D, 3, D)
    swap = np.arange(D) ^ 1
    by_pos = np.arange(D).reshape(H, DH).T.reshape(D)
    w_attn = np.stack([wqkv_t[:, k][:, cols] for k in range(2) for cols in (by_pos, swap[by_pos])]
                      + [wqkv_t[:, 2]], 1)

    inv_freq = np.float32(np.pi) ** (np.float32(1.0) - np.arange(0, DH, 2, dtype=np.float32) / np.float32(DH))
    pos = np.arange(S, dtype=np.float32)
    pos_freq = pos[None, :] * inv_freq.astype(np.float32)[np.arange(D) // H // 2][:, None]
    r = np.arange(P)
    arrays = {
        "x": L0_attn_x, "w_attn": w_attn, "w_o": np.ascontiguousarray(L0_attn_Wo).T,
        "log_xi": L0_attn_log_xi, "pi_logit": L0_attn_pi_gate_logit, "e_logit": L0_attn_e_gate_logit,
        "ln1_w": np.reshape(L0_ffn_ln1_w, (D, 1)), "ln1_b": np.reshape(L0_ffn_ln1_b, (D, 1)),
        "ln2_w": np.reshape(L0_ffn_ln2_w, (D, 1)), "ln2_b": np.reshape(L0_ffn_ln2_b, (D, 1)),
        "sim1": L0_ffn_smha_sim, "gates1": L0_ffn_smha_gates,
        "q_proj": L0_ffn_q_proj, "k_proj": L0_ffn_k_proj, "v_proj": L0_ffn_v_proj, "o_proj": L0_ffn_o_proj,
        "sim2": L0_ffn_moe_sim, "gates2": L0_ffn_moe_gates, "w1": L0_ffn_w1, "w2": L0_ffn_w2,
        "c_ident": np.eye(P, dtype=np.float32),
        "c_mask_qk": np.where(r[None, :] > r[:, None], -BIG, 0.0).astype(np.float32),
        "c_mask_kq": np.where(r[:, None] > r[None, :], -BIG, 0.0).astype(np.float32),
        "c_pos_freq": pos_freq.astype(np.float32),
        "c_sin_sign": np.where(r // H % 2 == 0, -1.0, 1.0).astype(np.float32)[:, None],
        "c_pos": np.broadcast_to(pos, (H, S)).astype(np.float32),
        "c_rank": np.broadcast_to(np.arange(E, 0, -1), (P, E)).astype(np.float32),
    }
    arrays = {f"in_{k}": np.ascontiguousarray(v) for k, v in arrays.items()}
    nc = bacc.Bacc("TRN2", target_bir_lowering=False, num_devices=1)
    args = [nc.dram_tensor(k, v.shape, mybir.dt.from_np(v.dtype), kind="ExternalInput").ap() for k, v in arrays.items()]
    out = nc.dram_tensor("out", (NB, S, D), F32, kind="ExternalOutput").ap()
    build(nc, *args, out)
    r = run_bass_kernel_spmd(nc, [arrays], core_ids=[0])
    return r.results[0]["out"]
```
